# Optimizing a Trainium2 kernel written in Bass

```python
import numpy as np
import jax
import jax.numpy as jnp

def _softmax(x, axis=-1):
    return jax.nn.softmax(x, axis=axis)

def _gelu(x):
    return jax.nn.gelu(x, approximate=True)

def _silu(x):
    return jax.nn.silu(x)

def _sigmoid(x):
    return jax.nn.sigmoid(x)

def _layernorm(x, axis=-1, eps=1e-05):
    m = jnp.mean(x, axis=axis, keepdims=True)
    v = jnp.var(x, axis=axis, keepdims=True)
    return (x - m) / jnp.sqrt(v + eps)

def _scatter_add(tgt, idx, src, axis=0):
    return tgt.at[idx].add(src)

def _segment_sum(src, seg, n):
    return jax.ops.segment_sum(src, seg, n)
kernel_name = 'mk_early_fusion_d1_tok_img1024_r4_aae693'

def setup_inputs(seed: int=0):
    np.random.seed(seed)
    _w = jnp.asarray

    def _rec_inputs():
        import jax
        import jax.numpy as jnp
        _rk = jax.random.key(seed)
        x = -0.00016672 + 0.999947 * jax.random.normal(jax.random.fold_in(_rk, 1), (64, 3, 96, 96), jnp.float32)
        txt = 0.00180885 + 1.15405 * jax.random.normal(jax.random.fold_in(_rk, 2), (64, 77, 256), jnp.float32)
        return (x, txt)
    x, txt = _rec_inputs()

    def _L0_tok_setup():
        import jax, jax.numpy as jnp
        import numpy as np
        PATCH = 16

        def _patchify(x, p):
            B, C, H, W = x.shape
            nh, nw = (H // p, W // p)
            x = x.reshape(B, C, nh, p, nw, p)
            x = x.transpose(0, 2, 4, 1, 3, 5)
            return x.reshape(B, nh * nw, C * p * p)
        key = jax.random.key(seed)
        k1, k2, k3, k4, k5 = jax.random.split(key, 5)
        B, C, H = (64, 3, 96)
        d_model = 256
        p = PATCH
        num_patches = (H // p) ** 2
        in_dim = p * p * C
        x = jax.random.normal(k1, (B, C, H, H), dtype=jnp.float32)
        bound = 1.0 / np.sqrt(in_dim)
        W = jax.random.uniform(k2, (d_model, in_dim), dtype=jnp.float32, minval=-bound, maxval=bound)
        b = jax.random.uniform(k3, (d_model,), dtype=jnp.float32, minval=-bound, maxval=bound)
        cls_token = jax.random.normal(k4, (1, 1, d_model), dtype=jnp.float32)
        pos_enc = jax.random.normal(k5, (1, num_patches + 1, d_model), dtype=jnp.float32)
        return {'x': x, 'W': W, 'b': b, 'cls_token': cls_token, 'pos_enc': pos_enc}
    _L0_tok_all = _L0_tok_setup()
    _L0_tok_in = {k: v for k, v in _L0_tok_all.items() if k in ('W', 'b', 'cls_token', 'pos_enc')}
    del _L0_tok_all

    def _L0_attn_setup():
        import jax, jax.numpy as jnp
        from jax import lax
        import numpy as np
        D_MODEL = 256
        D_STATE = 16
        D_CONV = 4
        EXPAND = 2
        D_INNER = D_MODEL * EXPAND
        DT_RANK = (D_MODEL + 15) // 16
        B, T = (2, 512)

        def _silu(v):
            return v * jax.nn.sigmoid(v)
        key = jax.random.key(seed)
        ks = jax.random.split(key, 8)

        def rn(k, shape, scale):
            return jax.random.normal(k, shape, dtype=jnp.float32) * scale
        x = rn(ks[0], (B, T, D_MODEL), 1.0)
        W_in = rn(ks[1], (D_MODEL, 2 * D_INNER), D_MODEL ** (-0.5))
        conv_w = rn(ks[2], (D_INNER, D_CONV), D_CONV ** (-0.5))
        conv_b = jnp.zeros((D_INNER,), jnp.float32)
        W_x = rn(ks[3], (D_INNER, DT_RANK + 2 * D_STATE), D_INNER ** (-0.5))
        W_dt = rn(ks[4], (DT_RANK, D_INNER), DT_RANK ** (-0.5))
        b_dt = jnp.log(jnp.expm1(jnp.full((D_INNER,), 0.01, jnp.float32)))
        A_log = jnp.log(jnp.broadcast_to(jnp.arange(1, D_STATE + 1, dtype=jnp.float32), (D_INNER, D_STATE)))
        Dp = jnp.ones((D_INNER,), jnp.float32)
        W_out = rn(ks[5], (D_INNER, D_MODEL), D_INNER ** (-0.5))
        return dict(x=x, W_in=W_in, conv_w=conv_w, conv_b=conv_b, W_x=W_x, W_dt=W_dt, b_dt=b_dt, A_log=A_log, D=Dp, W_out=W_out)
    _L0_attn_all = _L0_attn_setup()
    _L0_attn_in = {k: v for k, v in _L0_attn_all.items() if k in ('W_in', 'conv_w', 'conv_b', 'W_x', 'W_dt', 'b_dt', 'A_log', 'D', 'W_out')}
    del _L0_attn_all

    def _L0_ffn_setup():
        import jax, jax.numpy as jnp
        import numpy as np
        EPS = 1e-05

        def _ln(x, g, b):
            mu = jnp.mean(x, axis=-1, keepdims=True)
            var = jnp.mean(jnp.square(x - mu), axis=-1, keepdims=True)
            return (x - mu) * jax.lax.rsqrt(var + EPS) * g + b

        def _forward(x, index_b, index_t, sw1, sb1, sw2, sb2, sw3, sb3, s_ln_g, s_ln_b, sg_w, sg_b, eg_w, eg_b, exp_bias, ew1, eb1, ew2, eb2, ew3, eb3, sel_ln_g, sel_ln_b):
            x1 = jnp.einsum('btd,hd->bth', x, sw1) + sb1
            x2 = jnp.einsum('btd,hd->bth', x, sw2) + sb2
            sh = _ln(jax.nn.silu(x1) * x2, s_ln_g, s_ln_b)
            shared_out = jnp.einsum('bth,dh->btd', sh, sw3) + sb3
            x_moe = x[index_b, index_t]
            shared_scores = jax.nn.sigmoid(x_moe @ sg_w.T + sg_b)
            expert_scores = jax.nn.sigmoid(x_moe @ eg_w.T + eg_b)
            top1_idx = jnp.argmax(expert_scores + exp_bias, axis=-1)
            top1_score = jnp.take_along_axis(expert_scores, top1_idx[:, None], axis=-1)
            weights = jax.nn.softmax(jnp.concatenate([shared_scores, top1_score], axis=-1), axis=-1)
            shared_w, expert_w = (weights[:, 0], weights[:, 1])
            shared_moe_out = shared_out[index_b, index_t] * shared_w[:, None]
            h1 = jnp.einsum('md,ehd->meh', x_moe, ew1) + eb1
            h2 = jnp.einsum('md,ehd->meh', x_moe, ew2) + eb2
            z = _ln(jax.nn.silu(h1) * h2, sel_ln_g, sel_ln_b)
            out_all = jnp.einsum('meh,edh->med', z, ew3) + eb3
            expert_out = jnp.take_along_axis(out_all, top1_idx[:, None, None], axis=1)[:, 0]
            expert_moe_out = expert_out * expert_w[:, None]
            final_out = shared_out.at[index_b, index_t].set(shared_moe_out + expert_moe_out)
            return final_out
        B, T, D, E, H, M = (2, 512, 256, 8, 128, 512)
        key = jax.random.key(seed)
        ks = jax.random.split(key, 24)
        s = 0.02
        inp = {}
        inp['x'] = jax.random.normal(ks[0], (B, T, D), jnp.float32)
        flat = jnp.arange(M, dtype=jnp.int32) * 2
        inp['index_b'] = flat // T
        inp['index_t'] = flat % T
        inp['sw1'] = jax.random.normal(ks[1], (H, D), jnp.float32) * s
        inp['sb1'] = jnp.zeros((H,), jnp.float32)
        inp['sw2'] = jax.random.normal(ks[2], (H, D), jnp.float32) * s
        inp['sb2'] = jnp.zeros((H,), jnp.float32)
        inp['sw3'] = jax.random.normal(ks[3], (D, H), jnp.float32) * s
        inp['sb3'] = jnp.zeros((D,), jnp.float32)
        inp['s_ln_g'] = jnp.ones((H,), jnp.float32)
        inp['s_ln_b'] = jnp.zeros((H,), jnp.float32)
        inp['sg_w'] = jax.random.normal(ks[4], (1, D), jnp.float32) * s
        inp['sg_b'] = jnp.zeros((1,), jnp.float32)
        inp['eg_w'] = jax.random.normal(ks[5], (E, D), jnp.float32) * s
        inp['eg_b'] = jnp.zeros((E,), jnp.float32)
        inp['exp_bias'] = jnp.zeros((E,), jnp.float32)
        inp['ew1'] = jax.random.normal(ks[6], (E, H, D), jnp.float32) * s
        inp['eb1'] = jnp.zeros((E, H), jnp.float32)
        inp['ew2'] = jax.random.normal(ks[7], (E, H, D), jnp.float32) * s
        inp['eb2'] = jnp.zeros((E, H), jnp.float32)
        inp['ew3'] = jax.random.normal(ks[8], (E, D, H), jnp.float32) * s
        inp['eb3'] = jnp.zeros((E, D), jnp.float32)
        inp['sel_ln_g'] = jnp.ones((H,), jnp.float32)
        inp['sel_ln_b'] = jnp.zeros((H,), jnp.float32)
        return inp
    _L0_ffn_all = _L0_ffn_setup()
    _L0_ffn_in = {k: v for k, v in _L0_ffn_all.items() if k in ('index_b', 'index_t', 'sw1', 'sb1', 'sw2', 'sb2', 'sw3', 'sb3', 's_ln_g', 's_ln_b', 'sg_w', 'sg_b', 'eg_w', 'eg_b', 'exp_bias', 'ew1', 'eb1', 'ew2', 'eb2', 'ew3', 'eb3', 'sel_ln_g', 'sel_ln_b')}
    del _L0_ffn_all
    return {'x': x, 'txt': txt, 'L0_tok_W': _L0_tok_in['W'], 'L0_tok_b': _L0_tok_in['b'], 'L0_tok_cls_token': _L0_tok_in['cls_token'], 'L0_tok_pos_enc': _L0_tok_in['pos_enc'], 'L0_attn_W_in': _L0_attn_in['W_in'], 'L0_attn_conv_w': _L0_attn_in['conv_w'], 'L0_attn_conv_b': _L0_attn_in['conv_b'], 'L0_attn_W_x': _L0_attn_in['W_x'], 'L0_attn_W_dt': _L0_attn_in['W_dt'], 'L0_attn_b_dt': _L0_attn_in['b_dt'], 'L0_attn_A_log': _L0_attn_in['A_log'], 'L0_attn_D': _L0_attn_in['D'], 'L0_attn_W_out': _L0_attn_in['W_out'], 'L0_ffn_index_b': _L0_ffn_in['index_b'], 'L0_ffn_index_t': _L0_ffn_in['index_t'], 'L0_ffn_sw1': _L0_ffn_in['sw1'], 'L0_ffn_sb1': _L0_ffn_in['sb1'], 'L0_ffn_sw2': _L0_ffn_in['sw2'], 'L0_ffn_sb2': _L0_ffn_in['sb2'], 'L0_ffn_sw3': _L0_ffn_in['sw3'], 'L0_ffn_sb3': _L0_ffn_in['sb3'], 'L0_ffn_s_ln_g': _L0_ffn_in['s_ln_g'], 'L0_ffn_s_ln_b': _L0_ffn_in['s_ln_b'], 'L0_ffn_sg_w': _L0_ffn_in['sg_w'], 'L0_ffn_sg_b': _L0_ffn_in['sg_b'], 'L0_ffn_eg_w': _L0_ffn_in['eg_w'], 'L0_ffn_eg_b': _L0_ffn_in['eg_b'], 'L0_ffn_exp_bias': _L0_ffn_in['exp_bias'], 'L0_ffn_ew1': _L0_ffn_in['ew1'], 'L0_ffn_eb1': _L0_ffn_in['eb1'], 'L0_ffn_ew2': _L0_ffn_in['ew2'], 'L0_ffn_eb2': _L0_ffn_in['eb2'], 'L0_ffn_ew3': _L0_ffn_in['ew3'], 'L0_ffn_eb3': _L0_ffn_in['eb3'], 'L0_ffn_sel_ln_g': _L0_ffn_in['sel_ln_g'], 'L0_ffn_sel_ln_b': _L0_ffn_in['sel_ln_b']}

def reference(x, txt, L0_tok_W, L0_tok_b, L0_tok_cls_token, L0_tok_pos_enc, L0_attn_W_in, L0_attn_conv_w, L0_attn_conv_b, L0_attn_W_x, L0_attn_W_dt, L0_attn_b_dt, L0_attn_A_log, L0_attn_D, L0_attn_W_out, L0_ffn_index_b, L0_ffn_index_t, L0_ffn_sw1, L0_ffn_sb1, L0_ffn_sw2, L0_ffn_sb2, L0_ffn_sw3, L0_ffn_sb3, L0_ffn_s_ln_g, L0_ffn_s_ln_b, L0_ffn_sg_w, L0_ffn_sg_b, L0_ffn_eg_w, L0_ffn_eg_b, L0_ffn_exp_bias, L0_ffn_ew1, L0_ffn_eb1, L0_ffn_ew2, L0_ffn_eb2, L0_ffn_ew3, L0_ffn_eb3, L0_ffn_sel_ln_g, L0_ffn_sel_ln_b):
    import jax
    import jax.numpy as jnp

    def _L0_tok_ref(x, W, b, cls_token, pos_enc):
        import jax, jax.numpy as jnp
        import numpy as np
        PATCH = 16

        def _patchify(x, p):
            B, C, H, W = x.shape
            nh, nw = (H // p, W // p)
            x = x.reshape(B, C, nh, p, nw, p)
            x = x.transpose(0, 2, 4, 1, 3, 5)
            return x.reshape(B, nh * nw, C * p * p)
        B = x.shape[0]
        patches = _patchify(x, PATCH)
        proj = jnp.einsum('bnf,df->bnd', patches, W) + b
        cls = jnp.broadcast_to(cls_token, (B, 1, cls_token.shape[-1]))
        out = jnp.concatenate([cls, proj], axis=1) + pos_enc
        return out

    def _L0_attn_ref(x, W_in, conv_w, conv_b, W_x, W_dt, b_dt, A_log, D, W_out):
        import jax, jax.numpy as jnp
        from jax import lax
        import numpy as np
        D_MODEL = 256
        D_STATE = 16
        D_CONV = 4
        EXPAND = 2
        D_INNER = D_MODEL * EXPAND
        DT_RANK = (D_MODEL + 15) // 16
        B, T = (2, 512)

        def _silu(v):
            return v * jax.nn.sigmoid(v)
        Bb, Tt, _ = x.shape
        xz = x @ W_in
        xi, z = jnp.split(xz, 2, axis=-1)
        xi_nch = jnp.transpose(xi, (0, 2, 1))
        xc = lax.conv_general_dilated(xi_nch, conv_w[:, None, :], (1,), [(D_CONV - 1, 0)], feature_group_count=D_INNER, dimension_numbers=('NCH', 'OIH', 'NCH'))
        xc = _silu(jnp.transpose(xc, (0, 2, 1)) + conv_b)
        x_dbl = xc @ W_x
        dt, Bm, Cm = jnp.split(x_dbl, [DT_RANK, DT_RANK + D_STATE], axis=-1)
        delta = jax.nn.softplus(dt @ W_dt + b_dt)
        A = -jnp.exp(A_log)
        dA = jnp.exp(delta[..., None] * A)
        dBu = delta[..., None] * Bm[:, :, None, :] * xc[..., None]

        def step(h, inp):
            dA_t, dBu_t, C_t = inp
            h = dA_t * h + dBu_t
            y = jnp.einsum('bdn,bn->bd', h, C_t)
            return (h, y)
        h0 = jnp.zeros((Bb, D_INNER, D_STATE), x.dtype)
        _, ys = lax.scan(step, h0, (jnp.transpose(dA, (1, 0, 2, 3)), jnp.transpose(dBu, (1, 0, 2, 3)), jnp.transpose(Cm, (1, 0, 2))))
        y = jnp.transpose(ys, (1, 0, 2)) + xc * D
        return y * _silu(z) @ W_out

    def _L0_ffn_ref(x, index_b, index_t, sw1, sb1, sw2, sb2, sw3, sb3, s_ln_g, s_ln_b, sg_w, sg_b, eg_w, eg_b, exp_bias, ew1, eb1, ew2, eb2, ew3, eb3, sel_ln_g, sel_ln_b):
        import jax, jax.numpy as jnp
        import numpy as np
        EPS = 1e-05

        def _ln(x, g, b):
            mu = jnp.mean(x, axis=-1, keepdims=True)
            var = jnp.mean(jnp.square(x - mu), axis=-1, keepdims=True)
            return (x - mu) * jax.lax.rsqrt(var + EPS) * g + b

        def _forward(x, index_b, index_t, sw1, sb1, sw2, sb2, sw3, sb3, s_ln_g, s_ln_b, sg_w, sg_b, eg_w, eg_b, exp_bias, ew1, eb1, ew2, eb2, ew3, eb3, sel_ln_g, sel_ln_b):
            x1 = jnp.einsum('btd,hd->bth', x, sw1) + sb1
            x2 = jnp.einsum('btd,hd->bth', x, sw2) + sb2
            sh = _ln(jax.nn.silu(x1) * x2, s_ln_g, s_ln_b)
            shared_out = jnp.einsum('bth,dh->btd', sh, sw3) + sb3
            x_moe = x[index_b, index_t]
            shared_scores = jax.nn.sigmoid(x_moe @ sg_w.T + sg_b)
            expert_scores = jax.nn.sigmoid(x_moe @ eg_w.T + eg_b)
            top1_idx = jnp.argmax(expert_scores + exp_bias, axis=-1)
            top1_score = jnp.take_along_axis(expert_scores, top1_idx[:, None], axis=-1)
            weights = jax.nn.softmax(jnp.concatenate([shared_scores, top1_score], axis=-1), axis=-1)
            shared_w, expert_w = (weights[:, 0], weights[:, 1])
            shared_moe_out = shared_out[index_b, index_t] * shared_w[:, None]
            h1 = jnp.einsum('md,ehd->meh', x_moe, ew1) + eb1
            h2 = jnp.einsum('md,ehd->meh', x_moe, ew2) + eb2
            z = _ln(jax.nn.silu(h1) * h2, sel_ln_g, sel_ln_b)
            out_all = jnp.einsum('meh,edh->med', z, ew3) + eb3
            expert_out = jnp.take_along_axis(out_all, top1_idx[:, None, None], axis=1)[:, 0]
            expert_moe_out = expert_out * expert_w[:, None]
            final_out = shared_out.at[index_b, index_t].set(shared_moe_out + expert_moe_out)
            return final_out
        return _forward(x, index_b, index_t, sw1, sb1, sw2, sb2, sw3, sb3, s_ln_g, s_ln_b, sg_w, sg_b, eg_w, eg_b, exp_bias, ew1, eb1, ew2, eb2, ew3, eb3, sel_ln_g, sel_ln_b)
    h = _L0_tok_ref(x, L0_tok_W, L0_tok_b, L0_tok_cls_token, L0_tok_pos_enc)
    h = jnp.concatenate([h, txt], axis=1)
    h = h + _L0_attn_ref(_layernorm(h, axis=-1), L0_attn_W_in, L0_attn_conv_w, L0_attn_conv_b, L0_attn_W_x, L0_attn_W_dt, L0_attn_b_dt, L0_attn_A_log, L0_attn_D, L0_attn_W_out)
    h = h + _L0_ffn_ref(_layernorm(h, axis=-1), L0_ffn_index_b, L0_ffn_index_t, L0_ffn_sw1, L0_ffn_sb1, L0_ffn_sw2, L0_ffn_sb2, L0_ffn_sw3, L0_ffn_sb3, L0_ffn_s_ln_g, L0_ffn_s_ln_b, L0_ffn_sg_w, L0_ffn_sg_b, L0_ffn_eg_w, L0_ffn_eg_b, L0_ffn_exp_bias, L0_ffn_ew1, L0_ffn_eb1, L0_ffn_ew2, L0_ffn_eb2, L0_ffn_ew3, L0_ffn_eb3, L0_ffn_sel_ln_g, L0_ffn_sel_ln_b)
    return h

_drawn_inputs = setup_inputs


def setup_inputs(seed=0):
    import zlib

    import numpy as np

    out = dict(_drawn_inputs(seed))
    spreads = {'L0_attn_conv_b': (0.0, 0.1),
     'L0_attn_b_dt': (-4.600166320800781, 0.6),
     'L0_attn_D': (1.0, 0.2),
     'L0_ffn_sb1': (0.0, 0.1),
     'L0_ffn_sb2': (0.0, 0.1),
     'L0_ffn_sb3': (0.0, 0.1),
     'L0_ffn_s_ln_g': (1.0, 0.2),
     'L0_ffn_s_ln_b': (0.0, 0.417),
     'L0_ffn_eg_b': (0.0, 2.0),
     'L0_ffn_exp_bias': (0.0, 0.496),
     'L0_ffn_eb1': (0.0, 0.8),
     'L0_ffn_eb2': (0.0, 0.8),
     'L0_ffn_eb3': (0.0, 0.8),
     'L0_ffn_sel_ln_g': (1.0, 0.6),
     'L0_ffn_sel_ln_b': (0.0, 0.8)}
    factors = {'L0_tok_b': 4.982,
     'L0_attn_W_dt': 4.582,
     'L0_attn_A_log': 3.975,
     'L0_ffn_sg_w': 75.784,
     'L0_ffn_eg_w': 6.563,
     'L0_ffn_ew1': 4.951,
     'L0_ffn_ew2': 4.753,
     'L0_ffn_ew3': 4.559}
    for name, (base, spread) in spreads.items():
        noise = np.random.default_rng([zlib.crc32(name.encode()), seed]).standard_normal(out[name].shape)
        drawn = base * np.exp(spread * noise) if base else spread * noise
        out[name] = jnp.asarray(drawn.astype(out[name].dtype))
    for name, factor in factors.items():
        out[name] = (out[name] * factor).astype(out[name].dtype)
    return out
```

```python
from contextlib import ExitStack

import concourse.bass as bass
from concourse import mybir

ALU = mybir.AluOpType
ACT = mybir.ActivationFunctionType
AX = mybir.AxisListType
F32 = mybir.dt.float32
I32 = mybir.dt.int32

P = 128
EPS = 1e-5


def fusion_kernel(nc, x_patches, txt_t, tok_w, tok_b, cls_t, pos_t, w_in, conv_w, conv_b, w_x, w_dt, b_dt,
                  a_log, d_skip, w_out, index_b, index_t, sw1, sb1, sw2, sb2, sw3, sb3, s_ln_g, s_ln_b,
                  gate_w, sg_b, eg_b, exp_bias, ew1, eb1, ew2, eb2, ew3, eb3, sel_ln_g, sel_ln_b, out):
    GROUPS, _, FK, IMG2 = x_patches.shape
    SEQ = 2
    IMG = IMG2 // SEQ
    TXT = txt_t.shape[-1]
    T = 1 + IMG + TXT
    TOK = SEQ * T
    DM = out.shape[2]
    DC = DM // P
    DI = d_skip.shape[0] * d_skip.shape[1]
    CH = DI // P
    NS = a_log.shape[2]
    HN = NS // 2
    UNITS = 2 * CH
    TAPS = conv_w.shape[2]
    PAD = TAPS - 1
    R = w_dt.shape[0]
    H = sw3.shape[0]
    BATCH = GROUPS * SEQ
    ROWS = BATCH * T
    XRING, ARING = 4, 2
    M = index_b.shape[0] * index_b.shape[1]
    MT = M // P
    E = gate_w.shape[2] - 1

    bc_scratch = nc.dram_tensor("bc_scratch", (2, 2 * NS, TOK), F32, kind="Internal").ap()
    h2_scratch = nc.dram_tensor("h2_scratch", (ROWS, DM), F32, kind="Internal").ap()
    h2_groups = h2_scratch.rearrange("(g s t) d -> g t s d", s=SEQ, t=T)
    out_groups = out.rearrange("(g s) t d -> g t s d", s=SEQ)
    out_rows = out.rearrange("b t d -> (b t) d")

    with ExitStack() as whole:
        def sem(name):
            return whole.enter_context(nc.semaphore(name))

        def sb_in(stack, name, shape, dt=F32):
            return stack.enter_context(nc.sbuf_tensor(name, shape, dt))

        psum = whole.enter_context(nc.psum_tensor("psum", [P, 8, 512], F32))

        with ExitStack() as ctx:
            def sb(name, shape, dt=F32):
                return sb_in(ctx, name, shape, dt)

            tokw = sb("tokw", [P, FK, DM])
            tokb = sb("tokb", [P, DC])
            cls = sb("cls", [P, DC])
            pos = sb("pos", [P, DC, 1 + IMG])
            win = sb("win", [P, DC, 2 * DI])
            cw = sb("cw", [P, CH, TAPS])
            cb = sb("cb", [P, CH])
            wx = sb("wx", [P, CH, 2 * NS + R])
            wdt = sb("wdt", [64, DI])
            a_neg = sb("a_neg", [P, CH, NS])
            dsk = sb("dsk", [P, CH])
            wout = sb("wout", [P, CH, DM])
            w12 = sb("w12", [P, DC, 2 * H])
            b12 = sb("b12", [P, 2 * H])
            w3 = sb("w3", [P, DM])
            b3 = sb("b3", [P, DM])
            lng = sb("lng", [P, 1])
            lnb = sb("lnb", [P, 1])
            ident = sb("ident", [P, P])
            mean_w = sb("mean_w", [P, P])
            neg_half = sb("neg_half", [P, TOK])

            xp = sb("xp", [P, 2, FK, IMG2])
            h0 = sb("h0", [P, 2, DC, TOK])
            xh = sb("xh", [P, DC, TOK])
            sq = sb("sq", [P, DC, TOK])
            vare = sb("vare", [P, TOK])
            rstd = sb("rstd", [P, TOK])
            xi = sb("xi", [P, CH, SEQ, PAD + T])
            xc = sb("xc", [P, CH, TOK])
            tap = sb("tap", [P, CH, TOK])
            xc_tanh = sb("xc_tanh", [P, CH, TOK])
            z_tanh = sb("z_tanh", [P, CH, TOK])
            soft = z_tanh
            xs = sb("xs", [P, 2, CH, TOK])
            sz = sb("sz", [P, 2, CH, TOK])
            dbl = sb("dbl", [64, TOK])
            bbc = sb("bbc", [P, 2, NS, TOK])
            cbc = sb("cbc", [P, 2, NS, TOK])
            delta = sb("delta", [P, 2, CH, TOK])
            u = sb("u", [P, CH, TOK])
            da = sb("da", [P, ARING, HN, SEQ, T])
            xr = sb("xr", [P, XRING, HN, TOK])
            ytmp = sb("ytmp", [P, TOK])
            y = sb("y", [P, CH, TOK])
            h2 = sb("h2", [P, SEQ, DM])
            st2 = sb("st2", [P, SEQ, 6])
            mv2 = sb("mv2", [P, SEQ, 2])
            rs2 = sb("rs2", [P, SEQ])
            ve2 = sb("ve2", [P, SEQ])
            x2 = sb("x2", [P, SEQ, DM])
            x2t = sb("x2t", [P, DC, SEQ, T])
            x12 = sb("x12", [P, SEQ, 2, H])
            th1 = sb("th1", [P, SEQ, H])
            vv = sb("vv", [P, SEQ, H])
            st3 = sb("st3", [P, SEQ, 6])
            mv3 = sb("mv3", [P, SEQ, 2])
            ve3 = sb("ve3", [P, SEQ])
            rs3 = sb("rs3", [P, SEQ])
            vt = sb("vt", [P, SEQ, T])
            ob = sb("ob", [P, SEQ, DM])

            def y_bank(c):
                return psum[:, c % 2, 0:TOK]
            F0, F1 = 2, 3

            def pair(bank):
                return psum[:, bank, 0:2 * TOK].rearrange("p (c t) -> p c t", c=2)
            tok_ps = psum[:, 4, 0:DC * IMG2].rearrange("p (c t) -> p c t", c=DC)
            var_ps = psum[:, 4, 0:TOK]
            mean_ps = psum[:, 5, 0:TOK]
            dbl_ps = psum[0:2 * NS + R, 5, 0:TOK]
            h2_ps = psum[0:T, 6, 0:SEQ * DM].rearrange("p (s d) -> p s d", s=SEQ)
            f12_ps = psum[0:T, 6, 0:SEQ * 2 * H].rearrange("p (s d) -> p s d", s=SEQ)
            x2t_ps = psum[:, 7, 0:DC * TOK].rearrange("p (c s t) -> p c s t", c=DC, s=SEQ)
            vt_ps = psum[:, 7, 0:TOK].rearrange("p (s t) -> p s t", s=SEQ)
            f3_ps = psum[0:T, 7, 0:SEQ * DM].rearrange("p (s d) -> p s d", s=SEQ)

            const_in = sem("const_in")
            const_pool = sem("const_pool")
            const_dve = sem("const_dve")
            const_act = sem("const_act")
            xp_in = sem("xp_in")
            txt_in = sem("txt_in")
            tok_mm = sem("tok_mm")
            img_done = sem("img_done")
            mean_mm = sem("mean_mm")
            cent_done = sem("cent_done")
            sq_done = sem("sq_done")
            var_mm = sem("var_mm")
            vare_done = sem("vare_done")
            rstd_done = sem("rstd_done")
            xh_done = sem("xh_done")
            xi_mm = sem("xi_mm")
            xi_ev = sem("xi_ev")
            tap0_done = sem("tap0_done")
            tap_act = sem("tap_act")
            taps_done = sem("taps_done")
            xct_done = sem("xct_done")
            xs_done = sem("xs_done")
            z_mm = sem("z_mm")
            zt_done = sem("zt_done")
            sz_done = sem("sz_done")
            dbl_mm = sem("dbl_mm")
            dbl_ev = sem("dbl_ev")
            bc_out = sem("bc_out")
            b_in = sem("b_in")
            c_in = sem("c_in")
            dt_mm = sem("dt_mm")
            abs_done = sem("abs_done")
            spe_done = sem("spe_done")
            spl_done = sem("spl_done")
            delta_done = sem("delta_done")
            u_done = sem("u_done")
            exp_done = sem("exp_done")
            dbu_done = sem("dbu_done")
            scan_done = sem("scan_done")
            hc_done = sem("hc_done")
            red_mm = sem("red_mm")
            skip_done = sem("skip_done")
            y_done = sem("y_done")
            h2_mm = sem("h2_mm")
            h2_ev = sem("h2_ev")
            h2_out = sem("h2_out")
            h2b_done = sem("h2b_done")
            st2_done = sem("st2_done")
            mv2_done = sem("mv2_done")
            ve2_done = sem("ve2_done")
            rs2_done = sem("rs2_done")
            x2_done = sem("x2_done")
            x2t_mm = sem("x2t_mm")
            x2t_ev = sem("x2t_ev")
            f12_mm = sem("f12_mm")
            x12_done = sem("x12_done")
            th1_done = sem("th1_done")
            gate_done = sem("gate_done")
            v_done = sem("v_done")
            st3_done = sem("st3_done")
            mv3_done = sem("mv3_done")
            ve3_done = sem("ve3_done")
            rs3_done = sem("rs3_done")
            vn_done = sem("vn_done")
            vt_mm = sem("vt_mm")
            vt_ev = sem("vt_ev")
            f3_mm = sem("f3_mm")
            o_done = sem("o_done")
            out_out = sem("out_out")

            const_loads = [
                (tokw[:], tok_w), (tokb[:], tok_b), (cls[:], cls_t), (pos[:], pos_t), (win[:], w_in),
                (cw[:], conv_w), (cb[:], conv_b), (wx[:], w_x), (wdt[32:32 + R, :], w_dt),
                (wdt[32 + R:33 + R, :], b_dt), (a_neg[:], a_log), (dsk[:], d_skip), (wout[:], w_out),
                (w12[:, :, 0:H], sw1), (w12[:, :, H:2 * H], sw2), (w3[:], sw3),
                (b12[:, 0:H], sb1.partition_broadcast(P)), (b12[:, H:2 * H], sb2.partition_broadcast(P)),
                (b3[:], sb3.partition_broadcast(P)), (lng[:], s_ln_g), (lnb[:], s_ln_b),
            ]
            CONST_IN = 16 * len(const_loads)
            CONST_POOL = 7
            CONST_DVE = 4 + 2 * DC

            def over_groups(e, body):
                body(0, 0, True, False)
                with e.Fori(0, (GROUPS - 2) // 2) as turn:
                    body(2 * turn + 1, 1, True, True)
                    body(2 * turn + 2, 0, True, True)
                body(GROUPS - 1, (GROUPS - 1) % 2, False, True)

            with nc.Block() as block:

                @block.sync
                def _(sp):
                    def load_patches(g, p):
                        sp.dma_start(xp[:, p], x_patches[g]).then_inc(xp_in, 16)

                    def load_text(g, p):
                        for s in range(SEQ):
                            sp.dma_start(h0[:, p, :, s * T + 1 + IMG:(s + 1) * T], txt_t[g, :, :, s]).then_inc(txt_in, 16)

                    def bc_steps(g, p):
                        sp.wait_ge(dbl_ev, g + 1)
                        sp.dma_start(bc_scratch[p], dbl[0:2 * NS, :]).then_inc(bc_out, 16)
                        sp.wait_ge(bc_out, 16 * (g + 1))
                        for buf, lo, s in ((bbc, 0, b_in), (cbc, NS, c_in)):
                            sp.dma_start(buf[:, p].rearrange("p n t -> p (n t)"),
                                         bc_scratch[p, lo:lo + NS].rearrange("n t -> (n t)").partition_broadcast(P)
                                         ).then_inc(s, 16)

                    def body(i, p, front, back):
                        q = 1 - p
                        if front:
                            if back:
                                sp.wait_ge(tok_mm, i)
                            load_patches(i + 1, q)
                        if back:
                            sp.wait_ge(h2_mm, i)
                        if front:
                            load_text(i + 1, q)
                        if back:
                            sp.wait_ge(dbu_done, UNITS * i)
                            sp.wait_ge(hc_done, UNITS * i)
                            sp.wait_ge(h2_ev, i)
                            sp.dma_start(h2_groups[i - 1], h2[0:T]).then_inc(h2_out, 16)
                        if front:
                            bc_steps(i + 1, q)
                        if back:
                            sp.wait_ge(o_done, i)
                            sp.dma_start(out_groups[i - 1], ob[0:T]).then_inc(out_out, 16)

                    for dst, src in const_loads:
                        sp.dma_start(dst, src).then_inc(const_in, 16)
                    sp.wait_ge(const_dve, CONST_DVE)
                    load_patches(0, 0)
                    load_text(0, 0)
                    bc_steps(0, 0)
                    over_groups(sp, body)
                    sp.wait_ge(h2_ev, GROUPS)
                    sp.dma_start(h2_groups[GROUPS - 1], h2[0:T]).then_inc(h2_out, 16)
                    sp.wait_ge(o_done, GROUPS)
                    sp.dma_start(out_groups[GROUPS - 1], ob[0:T]).then_inc(out_out, 16)
                    sp.wait_ge(h2_out, 16 * GROUPS)
                    sp.wait_ge(out_out, 16 * GROUPS)

                @block.tensor
                def _(pe):
                    def project(bank, half, lhs, first):
                        for c in range(2):
                            for k in range(DC):
                                mm = pe.matmul(pair(bank)[:, c], lhs[:, k, (first + 2 * half + c) * P:(first + 2 * half + c + 1) * P],
                                               xh[:, k], start=(k == 0), stop=(k == DC - 1))
                        return mm

                    def tokens(g, p, first):
                        pe.wait_ge(xp_in, 16 * (g + 1))
                        if not first:
                            pe.wait_ge(vare_done, g)
                        for c in range(DC):
                            for k in range(FK):
                                mm = pe.matmul(tok_ps[:, c], tokw[:, k, c * P:(c + 1) * P], xp[:, p, k],
                                               start=(k == 0), stop=(k == FK - 1))
                        mm.then_inc(tok_mm, 1)

                    def mean(g, p, first):
                        pe.wait_ge(img_done, g + 1)
                        pe.wait_ge(txt_in, 16 * SEQ * (g + 1))
                        if not first:
                            pe.wait_ge(dbl_ev, g)
                        for k in range(DC):
                            mm = pe.matmul(mean_ps, mean_w[:], h0[:, p, k], start=(k == 0), stop=(k == DC - 1))
                        mm.then_inc(mean_mm, 1)

                    def var(g):
                        pe.wait_ge(sq_done, g + 1)
                        for k in range(DC):
                            mm = pe.matmul(var_ps, mean_w[:], sq[:, k], start=(k == 0), stop=(k == DC - 1))
                        mm.then_inc(var_mm, 1)

                    def proj_x(g, first):
                        pe.wait_ge(xh_done, g + 1)
                        for half, bank in ((0, F0), (1, F1)):
                            if not first:
                                pe.wait_ge(delta_done, 2 * g - 1 + half)
                            project(bank, half, win, 0).then_inc(xi_mm, 1)

                    def proj_z(g):
                        for half, bank in ((0, F0), (1, F1)):
                            pe.wait_ge(xi_ev, 2 * g + 1 + half)
                            project(bank, half, win, CH).then_inc(z_mm, 1)

                    def proj_bcdt(g, p):
                        pe.wait_ge(xs_done, g + 1)
                        for c in range(CH):
                            mm = pe.matmul(dbl_ps, wx[:, c], xs[:, p, c], start=(c == 0), stop=(c == CH - 1))
                        mm.then_inc(dbl_mm, 1)

                    def proj_delta(g):
                        pe.wait_ge(dbl_ev, g + 1)
                        for half, bank in ((0, F0), (1, F1)):
                            pe.wait_ge(sz_done, 2 * g + 1 + half)
                            for c in range(2):
                                mm = pe.matmul(pair(bank)[:, c], wdt[32:33 + R, (2 * half + c) * P:(2 * half + c + 1) * P],
                                               dbl[32:33 + R, :], start=True, stop=True)
                            mm.then_inc(dt_mm, 1)

                    def reduce_states(i, k, first):
                        c, v = k // 2, UNITS * i + k
                        pe.wait_ge(hc_done, v + 1)
                        if k % 2 == 0 and not (first and c < 2):
                            pe.wait_ge(skip_done, CH * i + c - 1)
                        for n in range(HN):
                            mm = pe.matmul(y_bank(c), ident[:], xr[:, k % XRING, n],
                                           start=(k % 2 == 0 and n == 0), stop=(k % 2 == 1 and n == HN - 1))
                        mm.then_inc(red_mm, 1)

                    def out_proj(g, p, first):
                        pe.wait_ge(y_done, CH * (g + 1))
                        if not first:
                            pe.wait_ge(x12_done, g)
                        for s in range(SEQ):
                            for k in range(DC):
                                pe.matmul(h2_ps[:, s, k * P:(k + 1) * P], h0[:, p, k, s * T:(s + 1) * T], ident[:],
                                          start=(k == 0), stop=False)
                            for c in range(CH):
                                mm = pe.matmul(h2_ps[:, s], y[:, c, s * T:(s + 1) * T], wout[:, c],
                                               start=False, stop=(c == CH - 1))
                        mm.then_inc(h2_mm, 1)

                    def x2_turn(g, first):
                        pe.wait_ge(x2_done, g + 1)
                        if not first:
                            pe.wait_ge(o_done, g)
                        for k in range(DC):
                            for s in range(SEQ):
                                mm = pe.transpose(x2t_ps[:, k, s], x2[0:T, s, k * P:(k + 1) * P], ident[0:T, 0:T])
                        mm.then_inc(x2t_mm, 1)

                    def ffn_in(g):
                        pe.wait_ge(x2t_ev, g + 1)
                        pe.wait_ge(h2_ev, g + 1)
                        for s in range(SEQ):
                            for k in range(DC):
                                mm = pe.matmul(f12_ps[:, s], x2t[:, k, s], w12[:, k], start=(k == 0), stop=(k == DC - 1))
                        mm.then_inc(f12_mm, 1)

                    def v_turn(g):
                        pe.wait_ge(vn_done, g + 1)
                        for s in range(SEQ):
                            mm = pe.transpose(vt_ps[:, s], vv[0:T, s], ident[0:T, 0:T])
                        mm.then_inc(vt_mm, 1)

                    def ffn_out(g):
                        pe.wait_ge(vt_ev, g + 1)
                        for s in range(SEQ):
                            mm = pe.matmul(f3_ps[:, s], vt[:, s], w3[:], start=True, stop=True)
                        mm.then_inc(f3_mm, 1)

                    def body(i, p, front, back):
                        q, f, b = 1 - p, i + 1, i - 1
                        b_first = isinstance(i, int) and i == 1
                        reduce_states(i, 0, not back)
                        if back:
                            out_proj(b, q, b_first)
                        if front:
                            tokens(f, q, False)
                        reduce_states(i, 1, not back)
                        if front:
                            mean(f, q, False)
                        reduce_states(i, 2, not back)
                        if back:
                            x2_turn(b, b_first)
                        if front:
                            var(f)
                        reduce_states(i, 3, not back)
                        if front:
                            proj_x(f, False)
                        if back:
                            ffn_in(b)
                        reduce_states(i, 4, not back)
                        if front:
                            proj_z(f)
                        reduce_states(i, 5, not back)
                        if front:
                            proj_bcdt(f, q)
                        reduce_states(i, 6, not back)
                        if back:
                            v_turn(b)
                        if front:
                            proj_delta(f)
                        if back:
                            ffn_out(b)
                        reduce_states(i, 7, not back)

                    pe.wait_ge(const_in, CONST_IN)
                    pe.wait_ge(const_pool, CONST_POOL)
                    pe.wait_ge(const_dve, CONST_DVE)
                    tokens(0, 0, True)
                    mean(0, 0, True)
                    var(0)
                    proj_x(0, True)
                    proj_z(0)
                    proj_bcdt(0, 0)
                    proj_delta(0)
                    over_groups(pe, body)
                    g = GROUPS - 1
                    out_proj(g, g % 2, False)
                    x2_turn(g, False)
                    ffn_in(g)
                    v_turn(g)
                    ffn_out(g)

                @block.scalar
                def _(act):
                    def exps(i, p, k, first):
                        c, v, slot = k // 2, UNITS * i + k, k % ARING
                        act.wait_ge(delta_done, 2 * i + 2)
                        if not (first and k < ARING):
                            act.wait_ge(scan_done, v - ARING + 1)
                        for n in range(HN):
                            st = (k % 2) * HN + n
                            ins = nc.scalar.activation(
                                da[:, slot, n, :, 1:T], delta[:, p, c].rearrange("p (s t) -> p s t", s=SEQ)[:, :, 1:T],
                                ACT.Exp, scale=a_neg[:, c, st:st + 1])
                        ins.then_inc(exp_done, 1)

                    def square(g):
                        act.wait_ge(cent_done, g + 1)
                        nc.scalar.activation(sq[:], xh[:], ACT.Square).then_inc(sq_done, 1)

                    def x_out(g, first):
                        for half, bank in ((0, F0), (1, F1)):
                            act.wait_ge(xi_mm, 2 * g + 1 + half)
                            if not first:
                                act.wait_ge(xs_done, g)
                            nc.scalar.activation(xi[:, 2 * half:2 * half + 2, :, PAD:],
                                                 pair(bank).rearrange("p c (s t) -> p c s t", s=SEQ),
                                                 ACT.Copy).then_inc(xi_ev, 1)
                        act.wait_ge(xi_ev, 2 * g + 2)
                        for c in range(CH):
                            ins = nc.scalar.activation(xc[:, c].rearrange("p (s t) -> p s t", s=SEQ), xi[:, c, :, PAD:],
                                                       ACT.Identity, bias=cb[:, c:c + 1], scale=cw[:, c, PAD:TAPS])
                        ins.then_inc(tap0_done, 1)
                        for t in range(PAD):
                            if t >= 2:
                                act.wait_ge(taps_done, PAD * g + t - 1)
                            to = (tap, xc_tanh)[t % 2]
                            for c in range(CH):
                                ins = nc.scalar.activation(to[:, c].rearrange("p (s t) -> p s t", s=SEQ), xi[:, c, :, t:t + T],
                                                           ACT.Copy, scale=cw[:, c, t:t + 1])
                            ins.then_inc(tap_act, 1)

                    def z_gate(g):
                        for half, bank in ((0, F0), (1, F1)):
                            act.wait_ge(z_mm, 2 * g + 1 + half)
                            nc.scalar.activation(z_tanh[:, 2 * half:2 * half + 2], pair(bank), ACT.Tanh).then_inc(zt_done, 1)

                    def x_gate(g):
                        act.wait_ge(taps_done, PAD * (g + 1))
                        nc.scalar.activation(xc_tanh[:], xc[:], ACT.Tanh).then_inc(xct_done, 1)

                    def dbl_copy(g, first):
                        act.wait_ge(dbl_mm, g + 1)
                        if not first:
                            act.wait_ge(bc_out, 16 * g)
                        nc.scalar.activation(dbl[0:2 * NS + R, :], dbl_ps, ACT.Copy).then_inc(dbl_ev, 1)

                    def softplus(g):
                        for half, bank in ((0, F0), (1, F1)):
                            act.wait_ge(dt_mm, 2 * g + 1 + half)
                            nc.scalar.activation(soft[:, 2 * half:2 * half + 2], pair(bank), ACT.Abs).then_inc(abs_done, 1)
                        act.wait_ge(abs_done, 2 * g + 2)
                        nc.scalar.activation(soft[:], soft[:], ACT.Exp, scale=-1.0).then_inc(spe_done, 1)
                        act.wait_ge(spe_done, g + 1)
                        nc.scalar.activation(soft[:], soft[:], ACT.Ln, bias=1.0).then_inc(spl_done, 1)

                    def h2_copy(g, first):
                        act.wait_ge(h2_mm, g + 1)
                        if not first:
                            act.wait_ge(h2_out, 16 * g)
                            act.wait_ge(h2b_done, g)
                        nc.scalar.activation(h2[0:T], h2_ps, ACT.Copy).then_inc(h2_ev, 1)

                    def x2t_copy(g):
                        act.wait_ge(x2t_mm, g + 1)
                        nc.scalar.activation(x2t[:], x2t_ps, ACT.Copy).then_inc(x2t_ev, 1)

                    def ffn_tanh(g):
                        act.wait_ge(x12_done, g + 1)
                        nc.scalar.activation(th1[0:T], x12[0:T, :, 0], ACT.Tanh, scale=0.5).then_inc(th1_done, 1)

                    def vt_copy(g):
                        act.wait_ge(vt_mm, g + 1)
                        nc.scalar.activation(vt[:], vt_ps, ACT.Identity, bias=lnb[:, 0:1], scale=lng[:, 0:1]).then_inc(vt_ev, 1)

                    def body(i, p, front, back):
                        f, b = i + 1, i - 1
                        b_first = isinstance(i, int) and i == 1
                        exps(i, p, 0, not back)
                        exps(i, p, 1, not back)
                        if back:
                            h2_copy(b, b_first)
                        exps(i, p, 2, not back)
                        if front:
                            square(f)
                        exps(i, p, 3, not back)
                        if back:
                            x2t_copy(b)
                        exps(i, p, 4, not back)
                        if front:
                            x_out(f, False)
                        exps(i, p, 5, not back)
                        if front:
                            z_gate(f)
                        if back:
                            ffn_tanh(b)
                        if front:
                            x_gate(f)
                        exps(i, p, 6, not back)
                        if front:
                            dbl_copy(f, False)
                        if back:
                            vt_copy(b)
                        exps(i, p, 7, not back)
                        if front:
                            softplus(f)

                    act.wait_ge(const_in, CONST_IN)
                    nc.scalar.activation(a_neg[:], a_neg[:], ACT.Exp).then_inc(const_act, 1)
                    act.wait_ge(const_pool, CONST_POOL)
                    act.wait_ge(const_dve, CONST_DVE)
                    square(0)
                    x_out(0, True)
                    z_gate(0)
                    x_gate(0)
                    dbl_copy(0, True)
                    softplus(0)
                    over_groups(act, body)
                    g = GROUPS - 1
                    h2_copy(g, False)
                    x2t_copy(g)
                    ffn_tanh(g)
                    vt_copy(g)

                @block.vector
                def _(dve):
                    def scan(i, p, k):
                        v = UNITS * i + k
                        dve.wait_ge(exp_done, v + 1)
                        dve.wait_ge(dbu_done, v + 1)
                        x = xr[:, k % XRING].rearrange("p n t -> p (n t)")
                        nc.vector.tensor_tensor_scan(x, da[:, k % ARING].rearrange("p n s t -> p (n s t)"), x, 0.0,
                                                     ALU.mult, ALU.add).then_inc(scan_done, 1)

                    def times_c(i, p, k):
                        v = UNITS * i + k
                        if k == 0:
                            dve.wait_ge(c_in, 16 * (i + 1))
                        dve.wait_ge(scan_done, v + 1)
                        nc.vector.tensor_tensor(xr[:, k % XRING], xr[:, k % XRING], cbc[:, p, (k % 2) * HN:(k % 2 + 1) * HN],
                                                ALU.mult).then_inc(hc_done, 1)

                    def y_out(g, p, c, first):
                        dve.wait_ge(red_mm, UNITS * g + 2 * c + 2)
                        nc.vector.scalar_tensor_tensor(out=ytmp[:], in0=xs[:, p, c], scalar=dsk[:, c:c + 1], in1=y_bank(c),
                                                       op0=ALU.mult, op1=ALU.add).then_inc(skip_done, 1)
                        dve.wait_ge(skip_done, CH * g + c + 1)
                        if not first:
                            dve.wait_ge(h2_mm, g)
                        nc.vector.tensor_tensor(y[:, c], ytmp[:], sz[:, p, c], ALU.mult).then_inc(y_done, 1)

                    def image_tokens(g, p):
                        dve.wait_ge(tok_mm, g + 1)
                        nc.vector.tensor_tensor(
                            h0[:, p].rearrange("p c (s t) -> p c s t", s=SEQ)[:, :, :, 1:1 + IMG],
                            tok_ps.rearrange("p c (s t) -> p c s t", s=SEQ),
                            pos[:, :, 1:].unsqueeze(2).to_broadcast([P, DC, SEQ, IMG]), ALU.add).then_inc(img_done, 1)

                    def center(g, p):
                        dve.wait_ge(mean_mm, g + 1)
                        nc.vector.tensor_tensor(xh[:], h0[:, p], mean_ps.unsqueeze(1).to_broadcast([P, DC, TOK]),
                                                ALU.subtract).then_inc(cent_done, 1)

                    def var_eps(g):
                        dve.wait_ge(var_mm, g + 1)
                        nc.vector.tensor_scalar(vare[:], var_ps, EPS, None, ALU.add).then_inc(vare_done, 1)

                    def normalize(g):
                        dve.wait_ge(rstd_done, g + 1)
                        dve.wait_ge(cent_done, g + 1)
                        nc.vector.tensor_tensor(xh[:], xh[:], rstd[:].unsqueeze(1).to_broadcast([P, DC, TOK]),
                                                ALU.mult).then_inc(xh_done, 1)

                    def z_silu(g, p):
                        for half, bank in ((0, F0), (1, F1)):
                            dve.wait_ge(zt_done, 2 * g + 1 + half)
                            nc.vector.scalar_tensor_tensor(out=sz[:, p, 2 * half:2 * half + 2], in0=z_tanh[:, 2 * half:2 * half + 2],
                                                           scalar=1.0, in1=pair(bank), op0=ALU.add,
                                                           op1=ALU.mult).then_inc(sz_done, 1)

                    def x_silu(g, p):
                        dve.wait_ge(xct_done, g + 1)
                        nc.vector.scalar_tensor_tensor(out=xs[:, p], in0=xc_tanh[:], scalar=1.0, in1=xc[:],
                                                       op0=ALU.add, op1=ALU.mult).then_inc(xs_done, 1)

                    def ffn_gate(g):
                        dve.wait_ge(th1_done, g + 1)
                        nc.vector.scalar_tensor_tensor(out=vv[0:T], in0=th1[0:T], scalar=1.0, in1=x12[0:T, :, 0],
                                                       op0=ALU.add, op1=ALU.mult).then_inc(gate_done, 1)
                        dve.wait_ge(gate_done, g + 1)
                        nc.vector.scalar_tensor_tensor(out=vv[0:T], in0=vv[0:T], scalar=0.5, in1=x12[0:T, :, 1],
                                                       op0=ALU.mult, op1=ALU.mult).then_inc(v_done, 1)

                    def delta_out(g, p):
                        dve.wait_ge(spl_done, g + 1)
                        for half, bank in ((0, F0), (1, F1)):
                            nc.vector.scalar_tensor_tensor(out=delta[:, p, 2 * half:2 * half + 2], in0=pair(bank), scalar=0.0,
                                                           in1=soft[:, 2 * half:2 * half + 2], op0=ALU.max,
                                                           op1=ALU.add).then_inc(delta_done, 1)

                    def ln2_stats(g):
                        dve.wait_ge(h2_ev, g + 1)
                        for s in range(SEQ):
                            ins = nc.vector.bn_stats(st2[0:T, s], h2[0:T, s])
                        ins.then_inc(st2_done, 1)
                        dve.wait_ge(st2_done, g + 1)

                    def ln2_moments(g):
                        for s in range(SEQ):
                            ins = nc.vector.bn_aggr(mv2[0:T, s], st2[0:T, s])
                        ins.then_inc(mv2_done, 1)
                        dve.wait_ge(mv2_done, g + 1)
                        nc.vector.tensor_scalar(ve2[0:T], mv2[0:T, :, 1], EPS, None, ALU.add).then_inc(ve2_done, 1)

                    def ln2_apply(g):
                        dve.wait_ge(rs2_done, g + 1)
                        for s in range(SEQ):
                            ins = nc.vector.tensor_scalar(x2[0:T, s], h2[0:T, s], mv2[0:T, s, 0:1], rs2[0:T, s:s + 1],
                                                          ALU.subtract, ALU.mult)
                        ins.then_inc(x2_done, 1)

                    def ffn_bias(g):
                        dve.wait_ge(f12_mm, g + 1)
                        nc.vector.tensor_tensor(x12[0:T].rearrange("p s a h -> p s (a h)"), f12_ps,
                                                b12[0:T].unsqueeze(1).to_broadcast([T, SEQ, 2 * H]),
                                                ALU.add).then_inc(x12_done, 1)

                    def ln3_stats(g):
                        dve.wait_ge(v_done, g + 1)
                        for s in range(SEQ):
                            ins = nc.vector.bn_stats(st3[0:T, s], vv[0:T, s])
                        ins.then_inc(st3_done, 1)
                        dve.wait_ge(st3_done, g + 1)

                    def ln3_moments(g):
                        for s in range(SEQ):
                            ins = nc.vector.bn_aggr(mv3[0:T, s], st3[0:T, s])
                        ins.then_inc(mv3_done, 1)
                        dve.wait_ge(mv3_done, g + 1)
                        nc.vector.tensor_scalar(ve3[0:T], mv3[0:T, :, 1], EPS, None, ALU.add).then_inc(ve3_done, 1)

                    def ln3_apply(g):
                        dve.wait_ge(rs3_done, g + 1)
                        for s in range(SEQ):
                            ins = nc.vector.tensor_scalar(vv[0:T, s], vv[0:T, s], mv3[0:T, s, 0:1], rs3[0:T, s:s + 1],
                                                          ALU.subtract, ALU.mult)
                        ins.then_inc(vn_done, 1)

                    def ffn_residual(g):
                        dve.wait_ge(f3_mm, g + 1)
                        dve.wait_ge(h2b_done, g + 1)
                        nc.vector.tensor_tensor(ob[0:T], f3_ps, ob[0:T], ALU.add).then_inc(o_done, 1)

                    def body(i, p, front, back):
                        q, f, b = 1 - p, i + 1, i - 1
                        b_first = isinstance(i, int) and i == 1
                        scan(i, p, 0)
                        if back:
                            y_out(b, q, CH - 1, b_first)
                        times_c(i, p, 0)
                        scan(i, p, 1)
                        if front:
                            image_tokens(f, q)
                        times_c(i, p, 1)
                        scan(i, p, 2)
                        if back:
                            ln2_stats(b)
                        y_out(i, p, 0, not back)
                        if back:
                            ln2_moments(b)
                        if front:
                            center(f, q)
                        if back:
                            ln2_apply(b)
                        times_c(i, p, 2)
                        scan(i, p, 3)
                        if front:
                            var_eps(f)
                        times_c(i, p, 3)
                        if front:
                            normalize(f)
                        scan(i, p, 4)
                        y_out(i, p, 1, not back)
                        if back:
                            ffn_bias(b)
                        times_c(i, p, 4)
                        scan(i, p, 5)
                        times_c(i, p, 5)
                        scan(i, p, 6)
                        if front:
                            z_silu(f, q)
                            x_silu(f, q)
                        if back:
                            ffn_gate(b)
                            ln3_stats(b)
                        y_out(i, p, 2, not back)
                        if back:
                            ln3_moments(b)
                        times_c(i, p, 6)
                        if back:
                            ln3_apply(b)
                        scan(i, p, 7)
                        times_c(i, p, 7)
                        if front:
                            delta_out(f, q)
                        if back:
                            ffn_residual(b)

                    nc.vector.memset(da[:], 0.0).then_inc(const_dve, 1)
                    nc.vector.memset(dbl[32:64, :], 1.0).then_inc(const_dve, 1)
                    dve.wait_ge(const_in, CONST_IN)
                    nc.vector.tensor_scalar(win[:, :, DI:], win[:, :, DI:], 0.5, None, ALU.mult).then_inc(const_dve, 1)
                    nc.vector.tensor_scalar(cw[:], cw[:], 0.5, None, ALU.mult).then_inc(const_dve, 1)
                    for k in range(DC):
                        nc.vector.tensor_scalar(pos[:, k, 1:], pos[:, k, 1:], tokb[:, k:k + 1], None,
                                                ALU.add).then_inc(const_dve, 1)
                    for k in range(DC):
                        nc.vector.tensor_tensor(
                            h0[:, :, k].rearrange("p a (s t) -> p a s t", s=SEQ)[:, :, :, 0],
                            cls[:, k:k + 1].unsqueeze(2).to_broadcast([P, 2, SEQ]),
                            pos[:, k, 0:1].unsqueeze(2).to_broadcast([P, 2, SEQ]), ALU.add).then_inc(const_dve, 1)
                    dve.wait_ge(const_dve, CONST_DVE)
                    dve.wait_ge(const_pool, CONST_POOL)
                    image_tokens(0, 0)
                    center(0, 0)
                    var_eps(0)
                    normalize(0)
                    z_silu(0, 0)
                    x_silu(0, 0)
                    delta_out(0, 0)
                    over_groups(dve, body)
                    g = GROUPS - 1
                    y_out(g, g % 2, CH - 1, False)
                    ln2_stats(g)
                    ln2_moments(g)
                    ln2_apply(g)
                    ffn_bias(g)
                    ffn_gate(g)
                    ln3_stats(g)
                    ln3_moments(g)
                    ln3_apply(g)
                    ffn_residual(g)

                @block.gpsimd
                def _(pool):
                    def dbu(i, p, k, first):
                        c, v = k // 2, UNITS * i + k
                        if k == 0:
                            pool.wait_ge(b_in, 16 * (i + 1))
                            pool.wait_ge(u_done, i + 1)
                        if not (first and k < XRING):
                            pool.wait_ge(red_mm, v - XRING + 1)
                        nc.gpsimd.tensor_tensor(xr[:, k % XRING], bbc[:, p, (k % 2) * HN:(k % 2 + 1) * HN],
                                                u[:, c].unsqueeze(1).to_broadcast([P, HN, TOK]), ALU.mult).then_inc(dbu_done, 1)

                    def rstd_pow(g):
                        pool.wait_ge(vare_done, g + 1)
                        nc.gpsimd.tensor_tensor(rstd[:], vare[:], neg_half[:], ALU.pow).then_inc(rstd_done, 1)

                    def convolve(g):
                        pool.wait_ge(tap0_done, g + 1)
                        for t in range(PAD):
                            pool.wait_ge(tap_act, PAD * g + t + 1)
                            if t:
                                pool.wait_ge(taps_done, PAD * g + t)
                            nc.gpsimd.tensor_tensor(xc[:], xc[:], (tap, xc_tanh)[t % 2][:], ALU.add).then_inc(taps_done, 1)

                    def u_out(g, p):
                        pool.wait_ge(delta_done, 2 * g + 2)
                        pool.wait_ge(xs_done, g + 1)
                        nc.gpsimd.tensor_tensor(u[:], delta[:, p], xs[:, p], ALU.mult).then_inc(u_done, 1)

                    def ln2_pow(g):
                        pool.wait_ge(ve2_done, g + 1)
                        nc.gpsimd.tensor_tensor(rs2[0:T], ve2[0:T], neg_half[0:T, 0:SEQ], ALU.pow).then_inc(rs2_done, 1)

                    def residual_bias(g, first):
                        pool.wait_ge(h2_ev, g + 1)
                        if not first:
                            pool.wait_ge(out_out, 16 * g)
                        nc.gpsimd.tensor_tensor(ob[0:T], h2[0:T], b3[0:T].unsqueeze(1).to_broadcast([T, SEQ, DM]),
                                                ALU.add).then_inc(h2b_done, 1)

                    def ln3_pow(g):
                        pool.wait_ge(ve3_done, g + 1)
                        nc.gpsimd.tensor_tensor(rs3[0:T], ve3[0:T], neg_half[0:T, 0:SEQ], ALU.pow).then_inc(rs3_done, 1)

                    def body(i, p, front, back):
                        q, f, b = 1 - p, i + 1, i - 1
                        b_first = isinstance(i, int) and i == 1
                        first = not back
                        dbu(i, p, 0, first)
                        dbu(i, p, 1, first)
                        dbu(i, p, 2, first)
                        dbu(i, p, 3, first)
                        if back:
                            ln2_pow(b)
                            residual_bias(b, b_first)
                        dbu(i, p, 4, first)
                        if front:
                            rstd_pow(f)
                        dbu(i, p, 5, first)
                        dbu(i, p, 6, first)
                        if front:
                            convolve(f)
                        if back:
                            ln3_pow(b)
                        dbu(i, p, 7, first)
                        if front:
                            u_out(f, q)

                    nc.gpsimd.memset(ident[:], 0.0).then_inc(const_pool, 1)
                    nc.gpsimd.memset(mean_w[:], 1.0 / DM).then_inc(const_pool, 1)
                    nc.gpsimd.memset(neg_half[:], -0.5).then_inc(const_pool, 1)
                    nc.gpsimd.memset(xi[:], 0.0).then_inc(const_pool, 1)
                    pool.wait_ge(const_pool, 4)
                    nc.gpsimd.affine_select(out=ident[:], in_=ident[:], compare_op=ALU.not_equal, fill=1.0, base=0,
                                            pattern=[[-1, P]], channel_multiplier=1).then_inc(const_pool, 1)
                    pool.wait_ge(const_act, 1)
                    pool.wait_ge(const_in, CONST_IN)
                    nc.gpsimd.tensor_scalar(a_neg[:], a_neg[:], -1.0, None, ALU.mult).then_inc(const_pool, 1)
                    nc.gpsimd.tensor_scalar(cb[:], cb[:], 0.5, None, ALU.mult).then_inc(const_pool, 1)
                    pool.wait_ge(const_dve, CONST_DVE)
                    rstd_pow(0)
                    convolve(0)
                    u_out(0, 0)
                    over_groups(pool, body)
                    g = GROUPS - 1
                    ln2_pow(g)
                    residual_bias(g, False)
                    ln3_pow(g)

        with ExitStack() as ctx:
            def sb(name, shape, dt=F32):
                return sb_in(ctx, name, shape, dt)

            e1 = sb("e1", [P, DC, E * H])
            e2 = sb("e2", [P, DC, E * H])
            e3 = sb("e3", [P, E, DM])
            eb1b = sb("eb1b", [P, E * H])
            eb2b = sb("eb2b", [P, E * H])
            eb3r = sb("eb3r", [E, DM])
            gw = sb("gw", [P, DC, 1 + E])
            gb = sb("gb", [P, 1 + E])
            xb = sb("xb", [P, E])
            selg = sb("selg", [P, H])
            selb = sb("selb", [P, H])
            prio = sb("prio", [P, E])
            prio_i = sb("prio_i", [P, E], I32)
            ident2 = sb("ident2", [P, P])
            half_neg = sb("half_neg", [P, MT, E])
            raw = sb("raw", [P, 2, MT], I32)
            pos_f = sb("pos_f", [P, 2, MT])
            tmp_f = sb("tmp_f", [P, 2, MT])
            ok_f = sb("ok_f", [P, 2, MT])
            row_f = sb("row_f", [P, MT])
            to_f = sb("to_f", [P, MT])
            row_i = sb("row_i", [P, MT], I32)
            to_i = sb("to_i", [P, MT], I32)
            hg = sb("hg", [P, MT, DM])
            og = sb("og", [P, MT, DM])
            mst = sb("mst", [P, MT, 6])
            mmv = sb("mmv", [P, MT, 2])
            mve = sb("mve", [P, MT])
            mrs = sb("mrs", [P, MT])
            xm = sb("xm", [P, MT, DM])
            xmt = sb("xmt", [P, DC, MT, P])
            sc = sb("sc", [P, MT, 1 + E])
            biased = sb("biased", [P, MT, E])
            best = sb("best", [P, MT])
            hot = sb("hot", [P, MT, E])
            hot_t = sb("hot_t", [E, MT, P])
            two = sb("two", [P, MT, 2])
            wts = sb("wts", [P, MT, 2])
            a1 = sb("a1", [P, 2, E, H])
            a2 = sb("a2", [P, 2, E, H])
            at = sb("at", [P, 2, E, H])
            est = sb("est", [P, 2, E, 6])
            emv = sb("emv", [P, 2, E, 2])
            eve = sb("eve", [P, 2, E])
            ers = sb("ers", [P, 2, E])
            zt = sb("zt", [P, 2, E, P])
            res = sb("res", [P, MT, DM])

            ew_in = sem("ew_in")
            idx_in = sem("idx_in")
            pool_c = sem("pool_c")
            idx_step = sem("idx_step")
            gathered = sem("gathered")
            lnm = sem("lnm")
            lnm_pow = sem("lnm_pow")
            xmt_mm = sem("xmt_mm")
            xmt_ev = sem("xmt_ev")
            gate_mm = sem("gate_mm")
            gate_act = sem("gate_act")
            gate_step = sem("gate_step")
            hot_mm = sem("hot_mm")
            hot_ev = sem("hot_ev")
            h12_mm = sem("h12_mm")
            a_done = sem("a_done")
            at_done = sem("at_done")
            shared_done = sem("shared_done")
            gated_1 = sem("gated_1")
            ev_done = sem("ev_done")
            est_step = sem("est_step")
            ers_done = sem("ers_done")
            zn_step = sem("zn_step")
            zt_mm = sem("zt_mm")
            zt_ev = sem("zt_ev")
            e3_mm = sem("e3_mm")
            part_done = sem("part_done")
            res_done = sem("res_done")
            scattered = sem("scattered")

            EW = [(e1[:], ew1), (e2[:], ew2), (e3[:], ew3), (eb1b[:], eb1.partition_broadcast(P)),
                  (eb2b[:], eb2.partition_broadcast(P)), (eb3r[:], eb3), (gw[:], gate_w),
                  (gb[:, 0:1], sg_b.partition_broadcast(P)), (gb[:, 1:], eg_b.partition_broadcast(P)),
                  (xb[:], exp_bias.partition_broadcast(P)), (selg[:], sel_ln_g.partition_broadcast(P)),
                  (selb[:], sel_ln_b.partition_broadcast(P))]
            EW_IN = 16 * len(EW)

            IDX_STEPS, GATE_STEPS = 15, 17

            with nc.Block() as block:

                def zt_copy(act, m):
                    act.wait_ge(zt_mm, m + 1)
                    if m >= 2:
                        act.wait_ge(e3_mm, m - 1)
                    nc.scalar.activation(zt[:, m % 2].rearrange("p (a e) t -> p a (e t)", a=2), psum[:, 4:6, :],
                                         ACT.Copy).then_inc(zt_ev, 1)

                @block.sync
                def _(sp):
                    sp.dma_start(raw[:, 0], index_b).then_inc(idx_in, 16)
                    sp.dma_start(raw[:, 1], index_t).then_inc(idx_in, 16)
                    for dst, src in EW:
                        sp.dma_start(dst, src).then_inc(ew_in, 16)

                @block.tensor
                def _(pe):
                    pe.wait_ge(pool_c, 3)
                    for m in range(MT):
                        pe.wait_ge(lnm, MT + 2 + m)
                        for k in range(DC):
                            mm = pe.transpose(psum[:, k, m * P:(m + 1) * P], xm[:, m, k * P:(k + 1) * P], ident2[:])
                        mm.then_inc(xmt_mm, 1)
                    pe.wait_ge(xmt_ev, DC)
                    pe.wait_ge(ew_in, EW_IN)
                    for m in range(MT):
                        for k in range(DC):
                            mm = pe.matmul(psum[:, 7, m * (1 + E):(m + 1) * (1 + E)], xmt[:, k, m], gw[:, k],
                                           start=(k == 0), stop=(k == DC - 1))
                    mm.then_inc(gate_mm, 1)

                    def hidden(m):
                        if m >= 1:
                            pe.wait_ge(a_done, 2 * m)
                        for j, w in ((0, e1), (1, e2)):
                            for half in range(2):
                                for k in range(DC):
                                    mm = pe.matmul(psum[:, 2 * j + half, :], xmt[:, k, m], w[:, k, half * 512:(half + 1) * 512],
                                                   start=(k == 0), stop=(k == DC - 1))
                            mm.then_inc(h12_mm, 1)

                    def out_of(m):
                        pe.wait_ge(zn_step, 5 * (m + 1))
                        if m >= 1:
                            pe.wait_ge(zt_ev, m)
                        for x in range(E):
                            mm = pe.transpose(psum[:, 4 + x // 4, (x % 4) * P:(x % 4 + 1) * P], a1[:, m % 2, x], ident2[:])
                        mm.then_inc(zt_mm, 1)
                        pe.wait_ge(zt_ev, m + 1)
                        if m >= 1:
                            pe.wait_ge(res_done, m)
                        pe.matmul(psum[:, 6, 0:DM], hot_t[:, m], eb3r[:], start=True, stop=False)
                        for x in range(E):
                            mm = pe.matmul(psum[:, 6, 0:DM], zt[:, m % 2, x], e3[:, x], start=False, stop=(x == E - 1))
                        mm.then_inc(e3_mm, 1)

                    hidden(0)
                    pe.wait_ge(gate_step, GATE_STEPS)
                    for m in range(MT):
                        mm = pe.transpose(psum[0:E, 7, m * P:(m + 1) * P], hot[:, m], ident2[:])
                    mm.then_inc(hot_mm, 1)
                    pe.wait_ge(hot_ev, 1)
                    for m in range(MT):
                        if m + 1 < MT:
                            hidden(m + 1)
                        out_of(m)

                @block.scalar
                def _(act):
                    act.wait_ge(xmt_mm, MT)
                    for k in range(DC):
                        nc.scalar.activation(xmt[:, k].rearrange("p m t -> p (m t)"), psum[:, k, :], ACT.Copy).then_inc(xmt_ev, 1)
                    act.wait_ge(gate_step, 1)
                    nc.scalar.activation(sc[:], sc[:], ACT.Exp, scale=-1.0).then_inc(gate_act, 1)
                    act.wait_ge(gate_step, GATE_STEPS - 3)
                    nc.scalar.activation(wts[:], two[:], ACT.Exp).then_inc(gate_act, 1)
                    act.wait_ge(hot_mm, 1)
                    nc.scalar.activation(hot_t[:].rearrange("p m t -> p (m t)"), psum[0:E, 7, :], ACT.Copy).then_inc(hot_ev, 1)
                    for m in range(MT):
                        act.wait_ge(a_done, 2 * m + 1)
                        nc.scalar.activation(at[:, m % 2], a1[:, m % 2], ACT.Tanh, scale=0.5).then_inc(at_done, 1)
                        if m >= 1:
                            zt_copy(act, m - 1)
                    zt_copy(act, MT - 1)

                @block.vector
                def _(dve):
                    count = [0]

                    def index(ins):
                        count[0] += 1
                        ins.then_inc(idx_step, 1)
                        dve.wait_ge(idx_step, count[0])

                    dve.wait_ge(idx_in, 32)
                    index(nc.vector.tensor_copy(pos_f[:], raw[:]))
                    for j, size in ((0, BATCH), (1, T)):
                        index(nc.vector.tensor_scalar(tmp_f[:, j], pos_f[:, j], 0.0, float(size), ALU.is_lt, ALU.mult))
                        index(nc.vector.tensor_tensor(pos_f[:, j], pos_f[:, j], tmp_f[:, j], ALU.add))
                        index(nc.vector.tensor_scalar(tmp_f[:, j], pos_f[:, j], 0.0, float(size - 1), ALU.max, ALU.min))
                        index(nc.vector.tensor_tensor(ok_f[:, j], tmp_f[:, j], pos_f[:, j], ALU.is_equal))
                    index(nc.vector.scalar_tensor_tensor(out=row_f[:], in0=tmp_f[:, 0], scalar=float(T), in1=tmp_f[:, 1],
                                                         op0=ALU.mult, op1=ALU.add))
                    index(nc.vector.tensor_tensor(ok_f[:, 0], ok_f[:, 0], ok_f[:, 1], ALU.mult))
                    index(nc.vector.tensor_scalar(ok_f[:, 0], ok_f[:, 0], -float(2 * ROWS), float(2 * ROWS), ALU.mult, ALU.add))
                    index(nc.vector.tensor_tensor(to_f[:], row_f[:], ok_f[:, 0], ALU.add))
                    index(nc.vector.tensor_copy(row_i[:], row_f[:]))
                    index(nc.vector.tensor_copy(to_i[:], to_f[:]))
                    assert count[0] == IDX_STEPS

                    dve.wait_ge(gathered, 16 * 2 * MT)
                    for m in range(MT):
                        ins = nc.vector.bn_stats(mst[:, m], hg[:, m])
                    ins.then_inc(lnm, 1)
                    dve.wait_ge(lnm, 1)
                    for m in range(MT):
                        ins = nc.vector.bn_aggr(mmv[:, m], mst[:, m])
                    ins.then_inc(lnm, 1)
                    dve.wait_ge(lnm, 2)
                    nc.vector.tensor_scalar(mve[:], mmv[:, :, 1], EPS, None, ALU.add).then_inc(lnm, MT - 1)
                    dve.wait_ge(lnm_pow, 1)
                    for m in range(MT):
                        nc.vector.tensor_scalar(xm[:, m], hg[:, m], mmv[:, m, 0:1], mrs[:, m:m + 1],
                                                ALU.subtract, ALU.mult).then_inc(lnm, 1)

                    gates = [0]

                    def gate(ins):
                        gates[0] += 1
                        ins.then_inc(gate_step, 1)
                        dve.wait_ge(gate_step, gates[0])

                    dve.wait_ge(gate_mm, 1)
                    dve.wait_ge(ew_in, EW_IN)
                    gate(nc.vector.tensor_tensor(sc[:], psum[:, 7, 0:MT * (1 + E)].rearrange("p (m e) -> p m e", m=MT),
                                                 gb[:].unsqueeze(1).to_broadcast([P, MT, 1 + E]), ALU.add))
                    dve.wait_ge(gate_act, 1)
                    gate(nc.vector.tensor_scalar(sc[:], sc[:], 1.0, None, ALU.add))
                    gate(nc.vector.reciprocal(sc[:], sc[:]))
                    gate(nc.vector.tensor_tensor(biased[:], sc[:, :, 1:], xb[:].unsqueeze(1).to_broadcast([P, MT, E]), ALU.add))
                    gate(nc.vector.tensor_reduce(best[:], biased[:], AX.X, ALU.max))
                    gate(nc.vector.tensor_tensor(hot[:], biased[:], best[:].unsqueeze(2).to_broadcast([P, MT, E]), ALU.is_equal))
                    dve.wait_ge(pool_c, 3)
                    gate(nc.vector.tensor_tensor(hot[:], hot[:], prio[:].unsqueeze(1).to_broadcast([P, MT, E]), ALU.mult))
                    gate(nc.vector.tensor_reduce(best[:], hot[:], AX.X, ALU.max))
                    gate(nc.vector.tensor_tensor(hot[:], hot[:], best[:].unsqueeze(2).to_broadcast([P, MT, E]), ALU.is_equal))
                    gate(nc.vector.tensor_tensor(biased[:], hot[:], sc[:, :, 1:], ALU.mult))
                    gate(nc.vector.tensor_reduce(two[:, :, 1:2], biased[:], AX.X, ALU.add))
                    gate(nc.vector.tensor_copy(two[:, :, 0:1], sc[:, :, 0:1]))
                    gate(nc.vector.tensor_reduce(best[:], two[:], AX.X, ALU.max))
                    gate(nc.vector.tensor_tensor(two[:], two[:], best[:].unsqueeze(2).to_broadcast([P, MT, 2]), ALU.subtract))
                    dve.wait_ge(gate_act, 2)
                    gate(nc.vector.tensor_reduce(best[:], wts[:], AX.X, ALU.add))
                    gate(nc.vector.reciprocal(best[:], best[:]))
                    gate(nc.vector.tensor_tensor(wts[:], wts[:], best[:].unsqueeze(2).to_broadcast([P, MT, 2]), ALU.mult))
                    assert gates[0] == GATE_STEPS

                    def bias_in(m):
                        for j, (a, b) in enumerate(((a1, eb1b), (a2, eb2b))):
                            dve.wait_ge(h12_mm, 2 * m + j + 1)
                            if m >= 2:
                                dve.wait_ge(zt_mm, m - 1)
                            nc.vector.tensor_tensor(a[:, m % 2].rearrange("p (c e) h -> p c (e h)", c=2),
                                                    psum[:, 2 * j:2 * j + 2, :],
                                                    b[:].rearrange("p (c n) -> p c n", c=2), ALU.add).then_inc(a_done, 1)

                    def gated(m):
                        dve.wait_ge(at_done, m + 1)
                        dve.wait_ge(a_done, 2 * m + 2)
                        nc.vector.scalar_tensor_tensor(out=a1[:, m % 2], in0=at[:, m % 2], scalar=1.0, in1=a1[:, m % 2],
                                                       op0=ALU.add, op1=ALU.mult).then_inc(gated_1, 1)
                        dve.wait_ge(gated_1, m + 1)
                        nc.vector.scalar_tensor_tensor(out=a1[:, m % 2], in0=a1[:, m % 2], scalar=0.5, in1=a2[:, m % 2],
                                                       op0=ALU.mult, op1=ALU.mult).then_inc(ev_done, 1)

                    def stats(m):
                        dve.wait_ge(ev_done, m + 1)
                        for x in range(E):
                            ins = nc.vector.bn_stats(est[:, m % 2, x], a1[:, m % 2, x])
                        ins.then_inc(est_step, 1)
                        dve.wait_ge(est_step, 3 * m + 1)
                        for x in range(E):
                            ins = nc.vector.bn_aggr(emv[:, m % 2, x], est[:, m % 2, x])
                        ins.then_inc(est_step, 1)
                        dve.wait_ge(est_step, 3 * m + 2)
                        nc.vector.tensor_scalar(eve[:, m % 2], emv[:, m % 2, :, 1], EPS, None, ALU.add).then_inc(est_step, 1)

                    def affine(m):
                        z = a1[:, m % 2]
                        over_h = [P, E, H]
                        dve.wait_ge(ers_done, m + 1)
                        steps = ((emv[:, m % 2, :, 0:1].to_broadcast(over_h), ALU.subtract),
                                 (ers[:, m % 2].unsqueeze(2).to_broadcast(over_h), ALU.mult),
                                 (selg[:].unsqueeze(1).to_broadcast(over_h), ALU.mult),
                                 (selb[:].unsqueeze(1).to_broadcast(over_h), ALU.add),
                                 (hot[:, m].unsqueeze(2).to_broadcast(over_h), ALU.mult))
                        for n, (other, op) in enumerate(steps):
                            nc.vector.tensor_tensor(z, z, other, op).then_inc(zn_step, 1)
                            if n < 4:
                                dve.wait_ge(zn_step, 5 * m + n + 1)

                    def combine(m):
                        nc.vector.scalar_tensor_tensor(out=og[:, m], in0=og[:, m], scalar=wts[:, m, 0:1], in1=hg[:, m],
                                                       op0=ALU.mult, op1=ALU.add).then_inc(part_done, 1)
                        dve.wait_ge(part_done, m + 1)
                        dve.wait_ge(e3_mm, m + 1)
                        nc.vector.scalar_tensor_tensor(out=res[:, m], in0=psum[:, 6, 0:DM], scalar=wts[:, m, 1:2], in1=og[:, m],
                                                       op0=ALU.mult, op1=ALU.add).then_inc(res_done, 1)

                    dve.wait_ge(shared_done, 1)
                    bias_in(0)
                    for m in range(MT):
                        if m + 1 < MT:
                            bias_in(m + 1)
                        gated(m)
                        stats(m)
                        affine(m)
                        if m >= 1:
                            combine(m - 1)
                    combine(MT - 1)

                @block.gpsimd
                def _(pool):
                    nc.gpsimd.memset(ident2[:], 0.0).then_inc(pool_c, 1)
                    pool.wait_ge(pool_c, 1)
                    nc.gpsimd.affine_select(out=ident2[:], in_=ident2[:], compare_op=ALU.not_equal, fill=1.0, base=0,
                                            pattern=[[-1, P]], channel_multiplier=1)
                    nc.gpsimd.memset(half_neg[:], -0.5)
                    nc.gpsimd.iota(prio_i[:], [[-1, E]], base=E, channel_multiplier=0).then_inc(pool_c, 1)
                    pool.wait_ge(pool_c, 2)
                    nc.gpsimd.tensor_copy(prio[:], prio_i[:]).then_inc(pool_c, 1)

                    pool.wait_ge(idx_step, IDX_STEPS)
                    for m in range(MT):
                        for dst, table in ((hg, h2_scratch), (og, out_rows)):
                            nc.gpsimd.indirect_dma_start(out=dst[:, m], out_offset=None, in_=table,
                                                         in_offset=bass.IndirectOffsetOnAxis(ap=row_i[:, m:m + 1], axis=0)
                                                         ).then_inc(gathered, 16)
                    pool.wait_ge(lnm, 1 + MT)
                    nc.gpsimd.tensor_tensor(mrs[:], mve[:], half_neg[:, :, 0], ALU.pow).then_inc(lnm_pow, 1)
                    nc.gpsimd.tensor_tensor(og[:], og[:], hg[:], ALU.subtract).then_inc(shared_done, 1)

                    def rstd_of(m):
                        pool.wait_ge(est_step, 3 * m + 3)
                        nc.gpsimd.tensor_tensor(ers[:, m % 2], eve[:, m % 2], half_neg[:, 0], ALU.pow).then_inc(ers_done, 1)

                    def scatter(m):
                        pool.wait_ge(res_done, m + 1)
                        nc.gpsimd.indirect_dma_start(out=out_rows, out_offset=bass.IndirectOffsetOnAxis(ap=to_i[:, m:m + 1], axis=0),
                                                     in_=res[:, m], in_offset=None, bounds_check=ROWS - 1,
                                                     oob_is_err=False).then_inc(scattered, 16)

                    for m in range(MT):
                        rstd_of(m)
                        if m >= 1:
                            scatter(m - 1)
                    scatter(MT - 1)
                    pool.wait_ge(scattered, 16 * MT)


def kernel(**inputs):
    import numpy as np
    import concourse.bacc as bacc
    from concourse.bass_utils import run_bass_kernel_spmd

    a = {k.replace("L0_", ""): np.asarray(v) for k, v in inputs.items()}

    def chunks(w):
        w = w.reshape(w.shape[0], -1)
        return w.reshape(-1, P, w.shape[1]).transpose(1, 0, 2)

    B, C, HW, _ = a["x"].shape
    PATCH, SEQ = 16, 2
    S = HW // PATCH
    G = B // SEQ
    DM = a["tok_W"].shape[0]
    R = a["attn_W_dt"].shape[0]
    E, H, _ = a["ffn_ew1"].shape
    M = a["ffn_index_b"].shape[0]
    x = a["x"].reshape(G, SEQ, C, S, PATCH, S, PATCH).transpose(2, 4, 6, 0, 1, 3, 5)
    x = x.reshape(-1, P, G, SEQ * S * S).transpose(2, 1, 0, 3)
    txt = a["txt"].reshape(G, SEQ, -1, DM // P, P).transpose(0, 4, 3, 1, 2)
    w_x = a["attn_W_x"]
    feed = {
        "x_patches": x, "txt_t": txt, "tok_w": chunks(a["tok_W"].T), "tok_b": a["tok_b"].reshape(-1, P).T,
        "cls_t": a["tok_cls_token"].reshape(-1, P).T, "pos_t": chunks(a["tok_pos_enc"][0].T),
        "w_in": chunks(a["attn_W_in"]), "conv_w": chunks(a["attn_conv_w"]), "conv_b": a["attn_conv_b"].reshape(-1, P).T,
        "w_x": chunks(np.concatenate([w_x[:, R:], w_x[:, :R]], axis=1)), "w_dt": a["attn_W_dt"],
        "b_dt": a["attn_b_dt"][None], "a_log": chunks(a["attn_A_log"]), "d_skip": a["attn_D"].reshape(-1, P).T,
        "w_out": chunks(a["attn_W_out"]), "index_b": a["ffn_index_b"].reshape(M // P, P).T,
        "index_t": a["ffn_index_t"].reshape(M // P, P).T, "sw1": chunks(a["ffn_sw1"].T), "sb1": a["ffn_sb1"],
        "sw2": chunks(a["ffn_sw2"].T), "sb2": a["ffn_sb2"], "sw3": a["ffn_sw3"].T, "sb3": a["ffn_sb3"],
        "s_ln_g": a["ffn_s_ln_g"][:, None], "s_ln_b": a["ffn_s_ln_b"][:, None], "gate_w": chunks(np.concatenate([a["ffn_sg_w"], a["ffn_eg_w"]]).T),
        "sg_b": a["ffn_sg_b"], "eg_b": a["ffn_eg_b"], "exp_bias": a["ffn_exp_bias"],
        "ew1": chunks(a["ffn_ew1"].reshape(E * H, DM).T), "eb1": a["ffn_eb1"].reshape(-1),
        "ew2": chunks(a["ffn_ew2"].reshape(E * H, DM).T), "eb2": a["ffn_eb2"].reshape(-1),
        "ew3": a["ffn_ew3"].transpose(2, 0, 1), "eb3": a["ffn_eb3"],
        "sel_ln_g": a["ffn_sel_ln_g"], "sel_ln_b": a["ffn_sel_ln_b"],
    }
    feed = {k: np.ascontiguousarray(v) for k, v in feed.items()}
    nc = bacc.Bacc("TRN2", target_bir_lowering=False, num_devices=1)
    args = {k: nc.dram_tensor(k, v.shape, mybir.dt.from_np(v.dtype), kind="ExternalInput").ap() for k, v in feed.items()}
    T = 1 + S * S + a["txt"].shape[1]
    out = nc.dram_tensor("out", (B, T, DM), F32, kind="ExternalOutput").ap()
    fusion_kernel(nc, out=out, **args)
    r = run_bass_kernel_spmd(nc, [feed], core_ids=[0])
    return r.results[0]["out"]
```

```python
from contextlib import ExitStack

import concourse.bass as bass
from concourse import mybir

ALU = mybir.AluOpType
ACT = mybir.ActivationFunctionType
AX = mybir.AxisListType
F32 = mybir.dt.float32
I32 = mybir.dt.int32

P = 128
EPS = 1e-5


def fusion_kernel(nc, x_patches, txt_t, tok_w, tok_b, cls_t, pos_t, w_in, conv_w, conv_b, w_x, w_dt, b_dt,
                  a_log, d_skip, w_out, index_b, index_t, sw1, sb1, sw2, sb2, sw3, sb3, s_ln_g, s_ln_b,
                  gate_w, sg_b, eg_b, exp_bias, ew1, eb1, ew2, eb2, ew3, eb3, sel_ln_g, sel_ln_b, out):
    GROUPS, _, FK, IMG2 = x_patches.shape
    SEQ = 2
    IMG = IMG2 // SEQ
    TXT = txt_t.shape[-1]
    T = 1 + IMG + TXT
    TOK = SEQ * T
    DM = out.shape[2]
    DC = DM // P
    DI = d_skip.shape[0] * d_skip.shape[1]
    CH = DI // P
    NS = a_log.shape[2]
    HN = NS // 2
    UNITS = 2 * CH
    TAPS = conv_w.shape[2]
    PAD = TAPS - 1
    R = w_dt.shape[0]
    H = sw3.shape[0]
    BATCH = GROUPS * SEQ
    ROWS = BATCH * T
    XRING, ARING, HRING = 4, 2, 4
    M = index_b.shape[0] * index_b.shape[1]
    MT = M // P
    E = gate_w.shape[2] - 1

    bc_scratch = nc.dram_tensor("bc_scratch", (2, 2 * NS, TOK), F32, kind="Internal").ap()
    h2_scratch = nc.dram_tensor("h2_scratch", (ROWS, DM), F32, kind="Internal").ap()
    h2_groups = h2_scratch.rearrange("(g s t) d -> g t s d", s=SEQ, t=T)
    out_groups = out.rearrange("(g s) t d -> g t s d", s=SEQ)
    out_rows = out.rearrange("b t d -> (b t) d")

    with ExitStack() as whole:
        def sem(name):
            return whole.enter_context(nc.semaphore(name))

        def sb_in(stack, name, shape, dt=F32):
            return stack.enter_context(nc.sbuf_tensor(name, shape, dt))

        psum = whole.enter_context(nc.psum_tensor("psum", [P, 8, 512], F32))

        with ExitStack() as ctx:
            def sb(name, shape, dt=F32):
                return sb_in(ctx, name, shape, dt)

            tokw = sb("tokw", [P, FK, DM])
            tokb = sb("tokb", [P, DC])
            cls = sb("cls", [P, DC])
            pos = sb("pos", [P, DC, 1 + IMG])
            win = sb("win", [P, DC, 2 * DI])
            cw = sb("cw", [P, CH, TAPS])
            cb = sb("cb", [P, CH])
            wx = sb("wx", [P, CH, 2 * NS + R])
            wdt = sb("wdt", [64, DI])
            a_neg = sb("a_neg", [P, CH, NS])
            dsk = sb("dsk", [P, CH])
            wout = sb("wout", [P, CH, DM])
            w12 = sb("w12", [P, DC, 2 * H])
            b12 = sb("b12", [P, 2 * H])
            w3 = sb("w3", [P, DM])
            b3 = sb("b3", [P, DM])
            lng = sb("lng", [P, 1])
            lnb = sb("lnb", [P, 1])
            ident = sb("ident", [P, P])
            mean_w = sb("mean_w", [P, P])
            neg_half = sb("neg_half", [P, SEQ])

            xp = sb("xp", [P, FK, IMG2])
            h0 = sb("h0", [P, HRING, DC, TOK])
            xh = sb("xh", [P, DC, TOK])
            sq = sb("sq", [P, DC, TOK])
            lnv = sb("lnv", [P, TOK])
            eps = sb("eps", [P, 1])
            rstd = sb("rstd", [P, TOK])
            xi = sb("xi", [P, CH, SEQ, PAD + T])
            xc = sb("xc", [P, CH, TOK])
            tap = sb("tap", [P, CH, TOK])
            xc_tanh = sb("xc_tanh", [P, CH, TOK])
            z_tanh = sb("z_tanh", [P, CH, TOK])
            soft = z_tanh
            xs = sb("xs", [P, 2, CH, TOK])
            sz = sb("sz", [P, 2, CH, TOK])
            dbl = sb("dbl", [64, TOK])
            bbc = sb("bbc", [P, 2, NS, TOK])
            cbc = sb("cbc", [P, 2, NS, TOK])
            delta = sb("delta", [P, 2, CH, TOK])
            u = sb("u", [P, CH, TOK])
            da = sb("da", [P, ARING, HN, SEQ, T])
            xr = sb("xr", [P, XRING, HN, TOK])
            ytmp = sb("ytmp", [P, TOK])
            y = sb("y", [P, CH, TOK])
            h2 = sb("h2", [P, SEQ, DM])
            st2 = sb("st2", [P, SEQ, 6])
            mv2 = sb("mv2", [P, SEQ, 2])
            rs2 = sb("rs2", [P, SEQ])
            ve2 = sb("ve2", [P, SEQ])
            x2 = sb("x2", [P, SEQ, DM])
            x2t = sb("x2t", [P, DC, SEQ, T])
            x12 = sb("x12", [P, SEQ, 2, H])
            th1 = sb("th1", [P, SEQ, H])
            vv = x12[:, :, 0]
            st3 = sb("st3", [P, SEQ, 6])
            mv3 = sb("mv3", [P, SEQ, 2])
            ve3 = sb("ve3", [P, SEQ])
            rs3 = sb("rs3", [P, SEQ])
            vt = sb("vt", [P, SEQ, T])
            ob = sb("ob", [P, 2, SEQ, DM])

            def y_bank(c):
                return psum[:, c % 2, 0:TOK]
            F0, F1 = 2, 3

            def pair(bank):
                return psum[:, bank, 0:2 * TOK].rearrange("p (c t) -> p c t", c=2)
            tok_ps = psum[:, 4, 0:DC * IMG2].rearrange("p (c t) -> p c t", c=DC)
            var_ps = psum[:, 4, 0:TOK]
            mean_ps = psum[:, 5, 0:TOK]
            dbl_ps = psum[0:2 * NS + R, 5, 0:TOK]
            h2_ps = psum[0:T, 6, 0:SEQ * DM].rearrange("p (s d) -> p s d", s=SEQ)
            f12_ps = psum[0:T, 6, 0:SEQ * 2 * H].rearrange("p (s d) -> p s d", s=SEQ)
            x2t_ps = psum[:, 7, 0:DC * TOK].rearrange("p (c s t) -> p c s t", c=DC, s=SEQ)
            vt_ps = psum[:, 5, 0:TOK].rearrange("p (s t) -> p s t", s=SEQ)
            f3_ps = psum[0:T, 6, 0:SEQ * DM].rearrange("p (s d) -> p s d", s=SEQ)

            const_in = sem("const_in")
            const_pool = sem("const_pool")
            const_dve = sem("const_dve")
            const_act = sem("const_act")
            xp_in = sem("xp_in")
            txt_in = sem("txt_in")
            tok_mm = sem("tok_mm")
            img_done = sem("img_done")
            mean_mm = sem("mean_mm")
            cent_done = sem("cent_done")
            sq_done = sem("sq_done")
            var_mm = sem("var_mm")
            lnv_done = sem("lnv_done")
            rstd_done = sem("rstd_done")
            xh_done = sem("xh_done")
            xi_mm = sem("xi_mm")
            xi_ev = sem("xi_ev")
            tap0_done = sem("tap0_done")
            tap_act = sem("tap_act")
            taps_done = sem("taps_done")
            xct_done = sem("xct_done")
            xs_done = sem("xs_done")
            z_mm = sem("z_mm")
            zt_done = sem("zt_done")
            sz_done = sem("sz_done")
            dbl_mm = sem("dbl_mm")
            dbl_ev = sem("dbl_ev")
            bc_out = sem("bc_out")
            b_in = sem("b_in")
            c_in = sem("c_in")
            dt_mm = sem("dt_mm")
            abs_done = sem("abs_done")
            spe_done = sem("spe_done")
            spl_done = sem("spl_done")
            delta_done = sem("delta_done")
            u_done = sem("u_done")
            exp_done = sem("exp_done")
            dbu_done = sem("dbu_done")
            scan_done = sem("scan_done")
            hc_done = sem("hc_done")
            red_mm = sem("red_mm")
            skip_done = sem("skip_done")
            y_done = sem("y_done")
            h2_mm = sem("h2_mm")
            h2_ev = sem("h2_ev")
            h2_out = sem("h2_out")
            h2b_done = sem("h2b_done")
            st2_done = sem("st2_done")
            mv2_done = sem("mv2_done")
            ve2_done = sem("ve2_done")
            rs2_done = sem("rs2_done")
            x2_done = sem("x2_done")
            x2t_mm = sem("x2t_mm")
            x2t_ev = sem("x2t_ev")
            f12_mm = sem("f12_mm")
            x12_done = sem("x12_done")
            th1_done = sem("th1_done")
            gate_done = sem("gate_done")
            v_done = sem("v_done")
            st3_done = sem("st3_done")
            mv3_done = sem("mv3_done")
            ve3_done = sem("ve3_done")
            rs3_done = sem("rs3_done")
            vn_done = sem("vn_done")
            vt_mm = sem("vt_mm")
            vt_ev = sem("vt_ev")
            f3_mm = sem("f3_mm")
            o_done = sem("o_done")
            out_out = sem("out_out")

            const_loads = [
                (tokw[:], tok_w), (tokb[:], tok_b), (cls[:], cls_t), (pos[:], pos_t), (win[:], w_in),
                (cw[:], conv_w), (cb[:], conv_b), (wx[:], w_x), (wdt[32:32 + R, :], w_dt),
                (wdt[32 + R:33 + R, :], b_dt), (a_neg[:], a_log), (dsk[:], d_skip), (wout[:], w_out),
                (w12[:, :, 0:H], sw1), (w12[:, :, H:2 * H], sw2), (w3[:], sw3),
                (b12[:, 0:H], sb1.partition_broadcast(P)), (b12[:, H:2 * H], sb2.partition_broadcast(P)),
                (b3[:], sb3.partition_broadcast(P)), (lng[:], s_ln_g), (lnb[:], s_ln_b),
            ]
            CONST_IN = 16 * len(const_loads)
            CONST_POOL = 8
            CONST_DVE = 4 + 2 * DC

            def need(e, semaphore, value):
                if not isinstance(value, int) or value > 0:
                    e.wait_ge(semaphore, value)

            def runs(g):
                return not isinstance(g, int) or 0 <= g < GROUPS

            def upto(count):
                return min(count, GROUPS) if isinstance(count, int) else count

            def over_steps(e, body):
                turns = (GROUPS - 6) // HRING
                for i in range(-3, 3):
                    body(i, i % HRING)
                with e.Fori(0, turns) as turn:
                    for j in range(HRING):
                        body(HRING * turn + 3 + j, (3 + j) % HRING)
                for i in range(3 + HRING * turns, GROUPS + 3):
                    body(i, i % HRING)

            with nc.Block() as block:

                @block.sync
                def _(sp):
                    def load_patches(g):
                        sp.dma_start(xp[:], x_patches[g]).then_inc(xp_in, 16)

                    def load_text(g, r):
                        for s in range(SEQ):
                            sp.dma_start(h0[:, r, :, s * T + 1 + IMG:(s + 1) * T], txt_t[g, :, :, s]).then_inc(txt_in, 16)

                    def body(i, r):
                        if runs(i - 3):
                            sp.wait_ge(o_done, i - 2)
                            sp.dma_start(out_groups[i - 3], ob[0:T, (r - 3) % 2]).then_inc(out_out, 16)
                        if runs(i):
                            need(sp, dbu_done, UNITS * i)
                            need(sp, hc_done, UNITS * i)
                        if runs(i + 3):
                            if isinstance(i, int):
                                need(sp, mean_mm, i + 3)
                            need(sp, h2_mm, i)
                            load_text(i + 3, (r + 3) % HRING)
                        if runs(i + 1):
                            p = (r + 1) % 2
                            sp.wait_ge(dbl_ev, i + 2)
                            sp.dma_start(bc_scratch[p], dbl[0:2 * NS, :]).then_inc(bc_out, 16)
                            sp.wait_ge(bc_out, 16 * (i + 2))
                            for buf, lo, s in ((bbc, 0, b_in), (cbc, NS, c_in)):
                                sp.dma_start(buf[:, p].rearrange("p n t -> p (n t)"),
                                             bc_scratch[p, lo:lo + NS].rearrange("n t -> (n t)").partition_broadcast(P)
                                             ).then_inc(s, 16)
                        if runs(i - 1):
                            sp.wait_ge(h2_ev, i)
                            sp.wait_ge(h2b_done, i)
                            sp.dma_start(h2_groups[i - 1], h2[0:T]).then_inc(h2_out, 16)
                        if runs(i + 4):
                            sp.wait_ge(tok_mm, i + 4)
                            load_patches(i + 4)

                    for dst, src in const_loads:
                        sp.dma_start(dst, src).then_inc(const_in, 16)
                    load_patches(0)
                    over_steps(sp, body)
                    sp.wait_ge(h2_out, 16 * GROUPS)
                    sp.wait_ge(out_out, 16 * GROUPS)

                @block.tensor
                def _(pe):
                    def project(bank, half, lhs, first):
                        for c in range(2):
                            for k in range(DC):
                                mm = pe.matmul(pair(bank)[:, c], lhs[:, k, (first + 2 * half + c) * P:(first + 2 * half + c + 1) * P],
                                               xh[:, k], start=(k == 0), stop=(k == DC - 1))
                        return mm

                    def tokens(g):
                        pe.wait_ge(xp_in, 16 * (g + 1))
                        need(pe, lnv_done, g)
                        for c in range(DC):
                            for k in range(FK):
                                mm = pe.matmul(tok_ps[:, c], tokw[:, k, c * P:(c + 1) * P], xp[:, k],
                                               start=(k == 0), stop=(k == FK - 1))
                        mm.then_inc(tok_mm, 1)

                    def mean(g, r):
                        pe.wait_ge(img_done, g + 1)
                        pe.wait_ge(txt_in, 16 * SEQ * (g + 1))
                        need(pe, dbl_ev, g - 1)
                        need(pe, vt_ev, g - 4)
                        for k in range(DC):
                            mm = pe.matmul(mean_ps, mean_w[:], h0[:, r, k], start=(k == 0), stop=(k == DC - 1))
                        mm.then_inc(mean_mm, 1)

                    def var(g):
                        pe.wait_ge(sq_done, g + 1)
                        for k in range(DC):
                            mm = pe.matmul(var_ps, mean_w[:], sq[:, k], start=(k == 0), stop=(k == DC - 1))
                        mm.then_inc(var_mm, 1)

                    def proj_x(g):
                        pe.wait_ge(xh_done, g + 1)
                        for half, bank in ((0, F0), (1, F1)):
                            if not (isinstance(g, int) and g == 0):
                                pe.wait_ge(delta_done, 2 * g - 1 + half)
                            project(bank, half, win, 0).then_inc(xi_mm, 1)

                    def proj_z(g):
                        for half, bank in ((0, F0), (1, F1)):
                            pe.wait_ge(xi_ev, 2 * g + 1 + half)
                            project(bank, half, win, CH).then_inc(z_mm, 1)

                    def proj_bcdt(g, p):
                        pe.wait_ge(xs_done, g + 1)
                        pe.wait_ge(cent_done, upto(g + 2))
                        for c in range(CH):
                            mm = pe.matmul(dbl_ps, wx[:, c], xs[:, p, c], start=(c == 0), stop=(c == CH - 1))
                        mm.then_inc(dbl_mm, 1)

                    def proj_delta(g):
                        pe.wait_ge(dbl_ev, g + 1)
                        for half, bank in ((0, F0), (1, F1)):
                            pe.wait_ge(sz_done, 2 * g + 1 + half)
                            for c in range(2):
                                mm = pe.matmul(pair(bank)[:, c], wdt[32:33 + R, (2 * half + c) * P:(2 * half + c + 1) * P],
                                               dbl[32:33 + R, :], start=True, stop=True)
                            mm.then_inc(dt_mm, 1)

                    def reduce_states(i, k):
                        c, v = k // 2, UNITS * i + k
                        pe.wait_ge(hc_done, v + 1)
                        if k % 2 == 0:
                            need(pe, skip_done, CH * i + c - 1)
                        for n in range(HN):
                            mm = pe.matmul(y_bank(c), ident[:], xr[:, k % XRING, n],
                                           start=(k % 2 == 0 and n == 0), stop=(k % 2 == 1 and n == HN - 1))
                        mm.then_inc(red_mm, 1)

                    def out_proj(g, r):
                        pe.wait_ge(y_done, CH * (g + 1))
                        need(pe, x12_done, g)
                        for s in range(SEQ):
                            for k in range(DC):
                                pe.matmul(h2_ps[:, s, k * P:(k + 1) * P], h0[:, r, k, s * T:(s + 1) * T], ident[:],
                                          start=(k == 0), stop=False)
                            for c in range(CH):
                                mm = pe.matmul(h2_ps[:, s], y[:, c, s * T:(s + 1) * T], wout[:, c],
                                               start=False, stop=(c == CH - 1))
                        mm.then_inc(h2_mm, 1)

                    def x2_turn(g):
                        pe.wait_ge(x2_done, g + 1)
                        need(pe, x2t_ev, g)
                        for k in range(DC):
                            for s in range(SEQ):
                                mm = pe.transpose(x2t_ps[:, k, s], x2[0:T, s, k * P:(k + 1) * P], ident[0:T, 0:T])
                        mm.then_inc(x2t_mm, 1)

                    def ffn_in(g):
                        pe.wait_ge(x2t_ev, g + 1)
                        need(pe, o_done, g)
                        for s in range(SEQ):
                            for k in range(DC):
                                mm = pe.matmul(f12_ps[:, s], x2t[:, k, s], w12[:, k], start=(k == 0), stop=(k == DC - 1))
                        mm.then_inc(f12_mm, 1)

                    def v_turn(g):
                        pe.wait_ge(vn_done, g + 1)
                        pe.wait_ge(dbl_ev, upto(g + 4))
                        for s in range(SEQ):
                            mm = pe.transpose(vt_ps[:, s], vv[0:T, s], ident[0:T, 0:T])
                        mm.then_inc(vt_mm, 1)

                    def ffn_out(g):
                        pe.wait_ge(vt_ev, g + 1)
                        pe.wait_ge(h2_ev, upto(g + 2))
                        for s in range(SEQ):
                            mm = pe.matmul(f3_ps[:, s], vt[:, s], w3[:], start=True, stop=True)
                        mm.then_inc(f3_mm, 1)

                    def body(i, r):
                        if runs(i + 1):
                            proj_z(i + 1)
                        if runs(i - 2):
                            ffn_in(i - 2)
                        if runs(i):
                            reduce_states(i, 0)
                        if runs(i + 2):
                            mean(i + 2, (r + 2) % HRING)
                        if runs(i):
                            reduce_states(i, 1)
                        if runs(i - 1):
                            out_proj(i - 1, (r - 1) % HRING)
                        if runs(i):
                            reduce_states(i, 2)
                        if runs(i + 1):
                            proj_bcdt(i + 1, (r + 1) % 2)
                        if runs(i):
                            reduce_states(i, 3)
                        if runs(i + 2):
                            var(i + 2)
                        if runs(i + 1):
                            proj_delta(i + 1)
                        if runs(i):
                            reduce_states(i, 4)
                            reduce_states(i, 5)
                        if runs(i - 1):
                            x2_turn(i - 1)
                        if runs(i - 2):
                            v_turn(i - 2)
                        if runs(i + 2):
                            proj_x(i + 2)
                        if runs(i):
                            reduce_states(i, 6)
                        if runs(i - 2):
                            ffn_out(i - 2)
                        if runs(i + 3):
                            tokens(i + 3)
                        if runs(i):
                            reduce_states(i, 7)

                    pe.wait_ge(const_in, CONST_IN)
                    pe.wait_ge(const_pool, CONST_POOL)
                    pe.wait_ge(const_dve, CONST_DVE)
                    over_steps(pe, body)

                @block.scalar
                def _(act):
                    def exps(i, p, k):
                        c, v, slot = k // 2, UNITS * i + k, k % ARING
                        act.wait_ge(delta_done, 2 * i + 2)
                        need(act, scan_done, v - ARING + 1)
                        for n in range(HN):
                            st = (k % 2) * HN + n
                            ins = nc.scalar.activation(
                                da[:, slot, n, :, 1:T], delta[:, p, c].rearrange("p (s t) -> p s t", s=SEQ)[:, :, 1:T],
                                ACT.Exp, scale=a_neg[:, c, st:st + 1])
                        ins.then_inc(exp_done, 1)

                    def square(g):
                        act.wait_ge(cent_done, g + 1)
                        nc.scalar.activation(sq[:], xh[:], ACT.Square).then_inc(sq_done, 1)

                    def rstd_out(g):
                        act.wait_ge(var_mm, g + 1)
                        nc.scalar.activation(lnv[:], var_ps, ACT.Ln, bias=eps[:, 0:1]).then_inc(lnv_done, 1)
                        act.wait_ge(lnv_done, g + 1)
                        nc.scalar.activation(rstd[:], lnv[:], ACT.Exp, scale=-0.5).then_inc(rstd_done, 1)

                    def x_out(g):
                        for half, bank in ((0, F0), (1, F1)):
                            act.wait_ge(xi_mm, 2 * g + 1 + half)
                            nc.scalar.activation(xi[:, 2 * half:2 * half + 2, :, PAD:],
                                                 pair(bank).rearrange("p c (s t) -> p c s t", s=SEQ),
                                                 ACT.Copy).then_inc(xi_ev, 1)
                        act.wait_ge(xi_ev, 2 * g + 2)
                        need(act, xs_done, g)
                        for c in range(CH):
                            ins = nc.scalar.activation(xc[:, c].rearrange("p (s t) -> p s t", s=SEQ), xi[:, c, :, PAD:],
                                                       ACT.Identity, bias=cb[:, c:c + 1], scale=cw[:, c, PAD:TAPS])
                        ins.then_inc(tap0_done, 1)

                    def taps(g):
                        for t in range(PAD):
                            if t >= 2:
                                act.wait_ge(taps_done, PAD * g + t - 1)
                            to = (tap, xc_tanh)[t % 2]
                            for c in range(CH):
                                ins = nc.scalar.activation(to[:, c].rearrange("p (s t) -> p s t", s=SEQ), xi[:, c, :, t:t + T],
                                                           ACT.Copy, scale=cw[:, c, t:t + 1])
                            ins.then_inc(tap_act, 1)

                    def z_gate(g):
                        for half, bank in ((0, F0), (1, F1)):
                            act.wait_ge(z_mm, 2 * g + 1 + half)
                            nc.scalar.activation(z_tanh[:, 2 * half:2 * half + 2], pair(bank), ACT.Tanh).then_inc(zt_done, 1)

                    def x_gate(g):
                        act.wait_ge(taps_done, PAD * (g + 1))
                        nc.scalar.activation(xc_tanh[:], xc[:], ACT.Tanh).then_inc(xct_done, 1)

                    def dbl_copy(g):
                        act.wait_ge(dbl_mm, g + 1)
                        need(act, bc_out, 16 * g)
                        nc.scalar.activation(dbl[0:2 * NS + R, :], dbl_ps, ACT.Copy).then_inc(dbl_ev, 1)

                    def softplus(g):
                        for half, bank in ((0, F0), (1, F1)):
                            act.wait_ge(dt_mm, 2 * g + 1 + half)
                            nc.scalar.activation(soft[:, 2 * half:2 * half + 2], pair(bank), ACT.Abs).then_inc(abs_done, 1)
                        act.wait_ge(abs_done, 2 * g + 2)
                        nc.scalar.activation(soft[:], soft[:], ACT.Exp, scale=-1.0).then_inc(spe_done, 1)
                        act.wait_ge(spe_done, g + 1)
                        nc.scalar.activation(soft[:], soft[:], ACT.Ln, bias=1.0).then_inc(spl_done, 1)

                    def h2_copy(g):
                        act.wait_ge(h2_mm, g + 1)
                        need(act, h2_out, 16 * g)
                        need(act, h2b_done, g)
                        nc.scalar.activation(h2[0:T], h2_ps, ACT.Copy).then_inc(h2_ev, 1)

                    def x2t_copy(g):
                        act.wait_ge(x2t_mm, g + 1)
                        nc.scalar.activation(x2t[:], x2t_ps, ACT.Copy).then_inc(x2t_ev, 1)

                    def ffn_tanh(g):
                        act.wait_ge(x12_done, g + 1)
                        nc.scalar.activation(th1[0:T], x12[0:T, :, 0], ACT.Tanh, scale=0.5).then_inc(th1_done, 1)

                    def vt_copy(g):
                        act.wait_ge(vt_mm, g + 1)
                        nc.scalar.activation(vt[:], vt_ps, ACT.Identity, bias=lnb[:, 0:1], scale=lng[:, 0:1]).then_inc(vt_ev, 1)

                    def body(i, r):
                        p = r % 2
                        if runs(i):
                            exps(i, p, 0)
                        if runs(i - 3):
                            vt_copy(i - 3)
                        if runs(i - 2):
                            x2t_copy(i - 2)
                        if runs(i + 1):
                            x_out(i + 1)
                        if runs(i):
                            exps(i, p, 1)
                        if runs(i + 1):
                            taps(i + 1)
                        if runs(i):
                            exps(i, p, 2)
                            exps(i, p, 3)
                        if runs(i + 1):
                            z_gate(i + 1)
                        if runs(i - 2):
                            ffn_tanh(i - 2)
                        if runs(i + 1):
                            x_gate(i + 1)
                        act.preload_act_table_set("natural_log_exp_and_others")
                        if runs(i):
                            exps(i, p, 4)
                        if runs(i + 2):
                            square(i + 2)
                        if runs(i):
                            exps(i, p, 5)
                        if runs(i + 1):
                            dbl_copy(i + 1)
                        if runs(i - 1):
                            h2_copy(i - 1)
                        if runs(i):
                            exps(i, p, 6)
                        if runs(i + 2):
                            rstd_out(i + 2)
                        if runs(i + 1):
                            softplus(i + 1)
                        if runs(i):
                            exps(i, p, 7)

                    act.wait_ge(const_in, CONST_IN)
                    nc.scalar.activation(a_neg[:], a_neg[:], ACT.Exp).then_inc(const_act, 1)
                    act.wait_ge(const_pool, CONST_POOL)
                    act.wait_ge(const_dve, CONST_DVE)
                    over_steps(act, body)

                @block.vector
                def _(dve):
                    def scan(i, p, k):
                        v = UNITS * i + k
                        dve.wait_ge(exp_done, v + 1)
                        dve.wait_ge(dbu_done, v + 1)
                        x = xr[:, k % XRING].rearrange("p n t -> p (n t)")
                        nc.vector.tensor_tensor_scan(x, da[:, k % ARING].rearrange("p n s t -> p (n s t)"), x, 0.0,
                                                     ALU.mult, ALU.add).then_inc(scan_done, 1)

                    def times_c(i, p, k):
                        v = UNITS * i + k
                        if k == 0:
                            dve.wait_ge(c_in, 16 * (i + 1))
                        dve.wait_ge(scan_done, v + 1)
                        nc.vector.tensor_tensor(xr[:, k % XRING], xr[:, k % XRING], cbc[:, p, (k % 2) * HN:(k % 2 + 1) * HN],
                                                ALU.mult).then_inc(hc_done, 1)

                    def y_out(g, p, c):
                        dve.wait_ge(red_mm, UNITS * g + 2 * c + 2)
                        nc.vector.scalar_tensor_tensor(out=ytmp[:], in0=xs[:, p, c], scalar=dsk[:, c:c + 1], in1=y_bank(c),
                                                       op0=ALU.mult, op1=ALU.add).then_inc(skip_done, 1)
                        dve.wait_ge(skip_done, CH * g + c + 1)
                        need(dve, h2_mm, g)
                        nc.vector.tensor_tensor(y[:, c], ytmp[:], sz[:, p, c], ALU.mult).then_inc(y_done, 1)

                    def image_tokens(g, r):
                        dve.wait_ge(tok_mm, g + 1)
                        nc.vector.tensor_tensor(
                            h0[:, r].rearrange("p c (s t) -> p c s t", s=SEQ)[:, :, :, 1:1 + IMG],
                            tok_ps.rearrange("p c (s t) -> p c s t", s=SEQ),
                            pos[:, :, 1:].unsqueeze(2).to_broadcast([P, DC, SEQ, IMG]), ALU.add).then_inc(img_done, 1)

                    def center(g, r):
                        dve.wait_ge(mean_mm, g + 1)
                        nc.vector.tensor_tensor(xh[:], h0[:, r], mean_ps.unsqueeze(1).to_broadcast([P, DC, TOK]),
                                                ALU.subtract).then_inc(cent_done, 1)

                    def normalize(g):
                        dve.wait_ge(rstd_done, g + 1)
                        dve.wait_ge(cent_done, g + 1)
                        nc.vector.tensor_tensor(xh[:], xh[:], rstd[:].unsqueeze(1).to_broadcast([P, DC, TOK]),
                                                ALU.mult).then_inc(xh_done, 1)

                    def z_silu(g, p):
                        for half, bank in ((0, F0), (1, F1)):
                            dve.wait_ge(zt_done, 2 * g + 1 + half)
                            nc.vector.scalar_tensor_tensor(out=sz[:, p, 2 * half:2 * half + 2], in0=z_tanh[:, 2 * half:2 * half + 2],
                                                           scalar=1.0, in1=pair(bank), op0=ALU.add,
                                                           op1=ALU.mult).then_inc(sz_done, 1)

                    def x_silu(g, p):
                        dve.wait_ge(xct_done, g + 1)
                        nc.vector.scalar_tensor_tensor(out=xs[:, p], in0=xc_tanh[:], scalar=1.0, in1=xc[:],
                                                       op0=ALU.add, op1=ALU.mult).then_inc(xs_done, 1)

                    def ffn_gate(g):
                        dve.wait_ge(th1_done, g + 1)
                        nc.vector.scalar_tensor_tensor(out=vv[0:T], in0=th1[0:T], scalar=1.0, in1=x12[0:T, :, 0],
                                                       op0=ALU.add, op1=ALU.mult).then_inc(gate_done, 1)
                        dve.wait_ge(gate_done, g + 1)
                        nc.vector.scalar_tensor_tensor(out=vv[0:T], in0=vv[0:T], scalar=0.5, in1=x12[0:T, :, 1],
                                                       op0=ALU.mult, op1=ALU.mult).then_inc(v_done, 1)

                    def delta_out(g, p):
                        dve.wait_ge(spl_done, g + 1)
                        for half, bank in ((0, F0), (1, F1)):
                            nc.vector.scalar_tensor_tensor(out=delta[:, p, 2 * half:2 * half + 2], in0=pair(bank), scalar=0.0,
                                                           in1=soft[:, 2 * half:2 * half + 2], op0=ALU.max,
                                                           op1=ALU.add).then_inc(delta_done, 1)

                    def ln2_stats(g):
                        dve.wait_ge(h2_ev, g + 1)
                        for s in range(SEQ):
                            ins = nc.vector.bn_stats(st2[0:T, s], h2[0:T, s])
                        ins.then_inc(st2_done, 1)
                        dve.wait_ge(st2_done, g + 1)

                    def ln2_moments(g):
                        for s in range(SEQ):
                            ins = nc.vector.bn_aggr(mv2[0:T, s], st2[0:T, s])
                        ins.then_inc(mv2_done, 1)
                        dve.wait_ge(mv2_done, g + 1)
                        nc.vector.tensor_scalar(ve2[0:T], mv2[0:T, :, 1], EPS, None, ALU.add).then_inc(ve2_done, 1)

                    def ln2_apply(g):
                        dve.wait_ge(rs2_done, g + 1)
                        for s in range(SEQ):
                            ins = nc.vector.tensor_scalar(x2[0:T, s], h2[0:T, s], mv2[0:T, s, 0:1], rs2[0:T, s:s + 1],
                                                          ALU.subtract, ALU.mult)
                        ins.then_inc(x2_done, 1)

                    def ffn_bias(g):
                        dve.wait_ge(f12_mm, g + 1)
                        nc.vector.tensor_tensor(x12[0:T].rearrange("p s a h -> p s (a h)"), f12_ps,
                                                b12[0:T].unsqueeze(1).to_broadcast([T, SEQ, 2 * H]),
                                                ALU.add).then_inc(x12_done, 1)

                    def ln3_stats(g):
                        dve.wait_ge(v_done, g + 1)
                        for s in range(SEQ):
                            ins = nc.vector.bn_stats(st3[0:T, s], vv[0:T, s])
                        ins.then_inc(st3_done, 1)
                        dve.wait_ge(st3_done, g + 1)

                    def ln3_moments(g):
                        for s in range(SEQ):
                            ins = nc.vector.bn_aggr(mv3[0:T, s], st3[0:T, s])
                        ins.then_inc(mv3_done, 1)
                        dve.wait_ge(mv3_done, g + 1)
                        nc.vector.tensor_scalar(ve3[0:T], mv3[0:T, :, 1], EPS, None, ALU.add).then_inc(ve3_done, 1)

                    def ln3_apply(g):
                        dve.wait_ge(rs3_done, g + 1)
                        for s in range(SEQ):
                            ins = nc.vector.tensor_scalar(vv[0:T, s], vv[0:T, s], mv3[0:T, s, 0:1], rs3[0:T, s:s + 1],
                                                          ALU.subtract, ALU.mult)
                        ins.then_inc(vn_done, 1)

                    def ffn_residual(g, p):
                        dve.wait_ge(f3_mm, g + 1)
                        dve.wait_ge(h2b_done, g + 1)
                        nc.vector.tensor_tensor(ob[0:T, p], f3_ps, ob[0:T, p], ALU.add).then_inc(o_done, 1)

                    def body(i, r):
                        p = r % 2
                        q = 1 - p
                        if runs(i - 3):
                            ffn_residual(i - 3, q)
                        if runs(i):
                            scan(i, p, 0)
                        if runs(i + 2):
                            image_tokens(i + 2, (r + 2) % HRING)
                        if runs(i):
                            times_c(i, p, 0)
                        if runs(i - 1):
                            y_out(i - 1, q, CH - 1)
                        if runs(i - 2):
                            ffn_bias(i - 2)
                        if runs(i):
                            scan(i, p, 1)
                            times_c(i, p, 1)
                            scan(i, p, 2)
                        if runs(i + 2):
                            center(i + 2, (r + 2) % HRING)
                        if runs(i):
                            times_c(i, p, 2)
                        if runs(i + 1):
                            z_silu(i + 1, q)
                            x_silu(i + 1, q)
                        if runs(i):
                            scan(i, p, 3)
                            y_out(i, p, 0)
                            times_c(i, p, 3)
                        if runs(i - 2):
                            ffn_gate(i - 2)
                            ln3_stats(i - 2)
                        if runs(i):
                            scan(i, p, 4)
                        elif runs(i - 1):
                            ln2_stats(i - 1)
                        if runs(i - 2):
                            ln3_moments(i - 2)
                        if runs(i):
                            if runs(i - 1):
                                ln2_stats(i - 1)
                            times_c(i, p, 4)
                        if runs(i - 1):
                            ln2_moments(i - 1)
                        if runs(i):
                            scan(i, p, 5)
                            y_out(i, p, 1)
                            times_c(i, p, 5)
                        if runs(i + 1):
                            delta_out(i + 1, q)
                        if runs(i + 2):
                            normalize(i + 2)
                        if runs(i - 1):
                            ln2_apply(i - 1)
                        if runs(i - 2):
                            ln3_apply(i - 2)
                        if runs(i):
                            scan(i, p, 6)
                            times_c(i, p, 6)
                            scan(i, p, 7)
                            y_out(i, p, 2)
                            times_c(i, p, 7)

                    nc.vector.memset(da[:], 0.0).then_inc(const_dve, 1)
                    nc.vector.memset(dbl[32:64, :], 1.0).then_inc(const_dve, 1)
                    dve.wait_ge(const_in, CONST_IN)
                    nc.vector.tensor_scalar(win[:, :, DI:], win[:, :, DI:], 0.5, None, ALU.mult).then_inc(const_dve, 1)
                    nc.vector.tensor_scalar(cw[:], cw[:], 0.5, None, ALU.mult).then_inc(const_dve, 1)
                    for k in range(DC):
                        nc.vector.tensor_scalar(pos[:, k, 1:], pos[:, k, 1:], tokb[:, k:k + 1], None,
                                                ALU.add).then_inc(const_dve, 1)
                    for k in range(DC):
                        nc.vector.tensor_tensor(
                            h0[:, :, k].rearrange("p a (s t) -> p a s t", s=SEQ)[:, :, :, 0],
                            cls[:, k:k + 1].unsqueeze(2).to_broadcast([P, HRING, SEQ]),
                            pos[:, k, 0:1].unsqueeze(2).to_broadcast([P, HRING, SEQ]), ALU.add).then_inc(const_dve, 1)
                    dve.wait_ge(const_dve, CONST_DVE)
                    dve.wait_ge(const_pool, CONST_POOL)
                    over_steps(dve, body)

                @block.gpsimd
                def _(pool):
                    def dbu(i, p, k):
                        c, v = k // 2, UNITS * i + k
                        if k == 0:
                            pool.wait_ge(b_in, 16 * (i + 1))
                            pool.wait_ge(u_done, i + 1)
                        need(pool, red_mm, v - XRING + 1)
                        nc.gpsimd.tensor_tensor(xr[:, k % XRING], bbc[:, p, (k % 2) * HN:(k % 2 + 1) * HN],
                                                u[:, c].unsqueeze(1).to_broadcast([P, HN, TOK]), ALU.mult).then_inc(dbu_done, 1)

                    def convolve(g):
                        pool.wait_ge(tap0_done, g + 1)
                        for t in range(PAD):
                            pool.wait_ge(tap_act, PAD * g + t + 1)
                            if t:
                                pool.wait_ge(taps_done, PAD * g + t)
                            nc.gpsimd.tensor_tensor(xc[:], xc[:], (tap, xc_tanh)[t % 2][:], ALU.add).then_inc(taps_done, 1)

                    def u_out(g, p):
                        pool.wait_ge(delta_done, 2 * g + 2)
                        pool.wait_ge(xs_done, g + 1)
                        need(pool, dbu_done, UNITS * g)
                        nc.gpsimd.tensor_tensor(u[:], delta[:, p], xs[:, p], ALU.mult).then_inc(u_done, 1)

                    def ln2_pow(g):
                        pool.wait_ge(ve2_done, g + 1)
                        nc.gpsimd.tensor_tensor(rs2[0:T], ve2[0:T], neg_half[0:T, 0:SEQ], ALU.pow).then_inc(rs2_done, 1)

                    def residual_bias(g, p):
                        pool.wait_ge(h2_ev, g + 1)
                        need(pool, out_out, 16 * (g - 1))
                        nc.gpsimd.tensor_tensor(ob[0:T, p], h2[0:T], b3[0:T].unsqueeze(1).to_broadcast([T, SEQ, DM]),
                                                ALU.add).then_inc(h2b_done, 1)

                    def ln3_pow(g):
                        pool.wait_ge(ve3_done, g + 1)
                        nc.gpsimd.tensor_tensor(rs3[0:T], ve3[0:T], neg_half[0:T, 0:SEQ], ALU.pow).then_inc(rs3_done, 1)

                    def body(i, r):
                        p = r % 2
                        if runs(i):
                            dbu(i, p, 0)
                            dbu(i, p, 1)
                            dbu(i, p, 2)
                        if runs(i + 1):
                            convolve(i + 1)
                        if runs(i):
                            dbu(i, p, 3)
                            dbu(i, p, 4)
                            dbu(i, p, 5)
                            dbu(i, p, 6)
                        if runs(i - 2):
                            ln3_pow(i - 2)
                        if runs(i - 1):
                            ln2_pow(i - 1)
                            residual_bias(i - 1, 1 - p)
                        if runs(i):
                            dbu(i, p, 7)
                        if runs(i + 1):
                            u_out(i + 1, 1 - p)

                    nc.gpsimd.memset(ident[:], 0.0).then_inc(const_pool, 1)
                    nc.gpsimd.memset(mean_w[:], 1.0 / DM).then_inc(const_pool, 1)
                    nc.gpsimd.memset(neg_half[:], -0.5).then_inc(const_pool, 1)
                    nc.gpsimd.memset(xi[:], 0.0).then_inc(const_pool, 1)
                    nc.gpsimd.memset(eps[:], EPS).then_inc(const_pool, 1)
                    pool.wait_ge(const_pool, 4)
                    nc.gpsimd.affine_select(out=ident[:], in_=ident[:], compare_op=ALU.not_equal, fill=1.0, base=0,
                                            pattern=[[-1, P]], channel_multiplier=1).then_inc(const_pool, 1)
                    pool.wait_ge(const_act, 1)
                    pool.wait_ge(const_in, CONST_IN)
                    nc.gpsimd.tensor_scalar(a_neg[:], a_neg[:], -1.0, None, ALU.mult).then_inc(const_pool, 1)
                    nc.gpsimd.tensor_scalar(cb[:], cb[:], 0.5, None, ALU.mult).then_inc(const_pool, 1)
                    pool.wait_ge(const_dve, CONST_DVE)
                    over_steps(pool, body)

        with ExitStack() as ctx:
            def sb(name, shape, dt=F32):
                return sb_in(ctx, name, shape, dt)

            e1 = sb("e1", [P, DC, E * H])
            e2 = sb("e2", [P, DC, E * H])
            e3 = sb("e3", [P, E, DM])
            eb1b = sb("eb1b", [P, E * H])
            eb2b = sb("eb2b", [P, E * H])
            eb3r = sb("eb3r", [E, DM])
            gw = sb("gw", [P, DC, 1 + E])
            gb = sb("gb", [P, 1 + E])
            xb = sb("xb", [P, E])
            selg = sb("selg", [P, H])
            selb = sb("selb", [P, H])
            prio = sb("prio", [P, E])
            prio_i = sb("prio_i", [P, E], I32)
            ident2 = sb("ident2", [P, P])
            half_neg = sb("half_neg", [P, MT, E])
            raw = sb("raw", [P, 2, MT], I32)
            pos_f = sb("pos_f", [P, 2, MT])
            tmp_f = sb("tmp_f", [P, 2, MT])
            ok_f = sb("ok_f", [P, 2, MT])
            row_f = sb("row_f", [P, MT])
            to_f = sb("to_f", [P, MT])
            row_i = sb("row_i", [P, MT], I32)
            to_i = sb("to_i", [P, MT], I32)
            hg = sb("hg", [P, MT, DM])
            og = sb("og", [P, MT, DM])
            mst = sb("mst", [P, MT, 6])
            mmv = sb("mmv", [P, MT, 2])
            mve = sb("mve", [P, MT])
            mrs = sb("mrs", [P, MT])
            xm = sb("xm", [P, MT, DM])
            xmt = sb("xmt", [P, DC, MT, P])
            sc = sb("sc", [P, MT, 1 + E])
            biased = sb("biased", [P, MT, E])
            best = sb("best", [P, MT])
            hot = sb("hot", [P, MT, E])
            hot_t = sb("hot_t", [E, MT, P])
            two = sb("two", [P, MT, 2])
            wts = sb("wts", [P, MT, 2])
            a1 = sb("a1", [P, 2, E, H])
            a2 = sb("a2", [P, 2, E, H])
            at = sb("at", [P, 2, E, H])
            est = sb("est", [P, 2, E, 6])
            emv = sb("emv", [P, 2, E, 2])
            eve = sb("eve", [P, 2, E])
            ers = sb("ers", [P, 2, E])
            zt = sb("zt", [P, 2, E, P])
            res = sb("res", [P, MT, DM])

            ew_in = sem("ew_in")
            idx_in = sem("idx_in")
            pool_c = sem("pool_c")
            idx_step = sem("idx_step")
            gathered = sem("gathered")
            lnm = sem("lnm")
            lnm_pow = sem("lnm_pow")
            xmt_mm = sem("xmt_mm")
            xmt_ev = sem("xmt_ev")
            gate_mm = sem("gate_mm")
            gate_act = sem("gate_act")
            gate_step = sem("gate_step")
            hot_mm = sem("hot_mm")
            hot_ev = sem("hot_ev")
            h12_mm = sem("h12_mm")
            a_done = sem("a_done")
            at_done = sem("at_done")
            shared_done = sem("shared_done")
            gated_1 = sem("gated_1")
            ev_done = sem("ev_done")
            est_step = sem("est_step")
            ers_done = sem("ers_done")
            zn_step = sem("zn_step")
            zt_mm = sem("zt_mm")
            zt_ev = sem("zt_ev")
            e3_mm = sem("e3_mm")
            part_done = sem("part_done")
            res_done = sem("res_done")
            scattered = sem("scattered")

            EW = [(e1[:], ew1), (e2[:], ew2), (e3[:], ew3), (eb1b[:], eb1.partition_broadcast(P)),
                  (eb2b[:], eb2.partition_broadcast(P)), (eb3r[:], eb3), (gw[:], gate_w),
                  (gb[:, 0:1], sg_b.partition_broadcast(P)), (gb[:, 1:], eg_b.partition_broadcast(P)),
                  (xb[:], exp_bias.partition_broadcast(P)), (selg[:], sel_ln_g.partition_broadcast(P)),
                  (selb[:], sel_ln_b.partition_broadcast(P))]
            EW_IN = 16 * len(EW)

            IDX_STEPS, GATE_STEPS = 15, 17

            with nc.Block() as block:

                def zt_copy(act, m):
                    act.wait_ge(zt_mm, m + 1)
                    if m >= 2:
                        act.wait_ge(e3_mm, m - 1)
                    nc.scalar.activation(zt[:, m % 2].rearrange("p (a e) t -> p a (e t)", a=2), psum[:, 4:6, :],
                                         ACT.Copy).then_inc(zt_ev, 1)

                @block.sync
                def _(sp):
                    sp.dma_start(raw[:, 0], index_b).then_inc(idx_in, 16)
                    sp.dma_start(raw[:, 1], index_t).then_inc(idx_in, 16)
                    for dst, src in EW:
                        sp.dma_start(dst, src).then_inc(ew_in, 16)

                @block.tensor
                def _(pe):
                    pe.wait_ge(pool_c, 3)
                    for m in range(MT):
                        pe.wait_ge(lnm, MT + 2 + m)
                        for k in range(DC):
                            mm = pe.transpose(psum[:, k, m * P:(m + 1) * P], xm[:, m, k * P:(k + 1) * P], ident2[:])
                        mm.then_inc(xmt_mm, 1)
                    pe.wait_ge(xmt_ev, DC)
                    pe.wait_ge(ew_in, EW_IN)
                    for m in range(MT):
                        for k in range(DC):
                            mm = pe.matmul(psum[:, 7, m * (1 + E):(m + 1) * (1 + E)], xmt[:, k, m], gw[:, k],
                                           start=(k == 0), stop=(k == DC - 1))
                    mm.then_inc(gate_mm, 1)

                    def hidden(m):
                        if m >= 1:
                            pe.wait_ge(a_done, 2 * m)
                        for j, w in ((0, e1), (1, e2)):
                            for half in range(2):
                                for k in range(DC):
                                    mm = pe.matmul(psum[:, 2 * j + half, :], xmt[:, k, m], w[:, k, half * 512:(half + 1) * 512],
                                                   start=(k == 0), stop=(k == DC - 1))
                            mm.then_inc(h12_mm, 1)

                    def out_of(m):
                        pe.wait_ge(zn_step, 5 * (m + 1))
                        if m >= 1:
                            pe.wait_ge(zt_ev, m)
                        for x in range(E):
                            mm = pe.transpose(psum[:, 4 + x // 4, (x % 4) * P:(x % 4 + 1) * P], a1[:, m % 2, x], ident2[:])
                        mm.then_inc(zt_mm, 1)
                        pe.wait_ge(zt_ev, m + 1)
                        if m >= 1:
                            pe.wait_ge(res_done, m)
                        pe.matmul(psum[:, 6, 0:DM], hot_t[:, m], eb3r[:], start=True, stop=False)
                        for x in range(E):
                            mm = pe.matmul(psum[:, 6, 0:DM], zt[:, m % 2, x], e3[:, x], start=False, stop=(x == E - 1))
                        mm.then_inc(e3_mm, 1)

                    hidden(0)
                    pe.wait_ge(gate_step, GATE_STEPS)
                    for m in range(MT):
                        mm = pe.transpose(psum[0:E, 7, m * P:(m + 1) * P], hot[:, m], ident2[:])
                    mm.then_inc(hot_mm, 1)
                    pe.wait_ge(hot_ev, 1)
                    for m in range(MT):
                        if m + 1 < MT:
                            hidden(m + 1)
                        out_of(m)

                @block.scalar
                def _(act):
                    act.wait_ge(xmt_mm, MT)
                    for k in range(DC):
                        nc.scalar.activation(xmt[:, k].rearrange("p m t -> p (m t)"), psum[:, k, :], ACT.Copy).then_inc(xmt_ev, 1)
                    act.wait_ge(gate_step, 1)
                    nc.scalar.activation(sc[:], sc[:], ACT.Exp, scale=-1.0).then_inc(gate_act, 1)
                    act.wait_ge(gate_step, GATE_STEPS - 3)
                    nc.scalar.activation(wts[:], two[:], ACT.Exp).then_inc(gate_act, 1)
                    act.wait_ge(hot_mm, 1)
                    nc.scalar.activation(hot_t[:].rearrange("p m t -> p (m t)"), psum[0:E, 7, :], ACT.Copy).then_inc(hot_ev, 1)
                    for m in range(MT):
                        act.wait_ge(a_done, 2 * m + 1)
                        nc.scalar.activation(at[:, m % 2], a1[:, m % 2], ACT.Tanh, scale=0.5).then_inc(at_done, 1)
                        if m >= 1:
                            zt_copy(act, m - 1)
                    zt_copy(act, MT - 1)

                @block.vector
                def _(dve):
                    count = [0]

                    def index(ins):
                        count[0] += 1
                        ins.then_inc(idx_step, 1)
                        dve.wait_ge(idx_step, count[0])

                    dve.wait_ge(idx_in, 32)
                    index(nc.vector.tensor_copy(pos_f[:], raw[:]))
                    for j, size in ((0, BATCH), (1, T)):
                        index(nc.vector.tensor_scalar(tmp_f[:, j], pos_f[:, j], 0.0, float(size), ALU.is_lt, ALU.mult))
                        index(nc.vector.tensor_tensor(pos_f[:, j], pos_f[:, j], tmp_f[:, j], ALU.add))
                        index(nc.vector.tensor_scalar(tmp_f[:, j], pos_f[:, j], 0.0, float(size - 1), ALU.max, ALU.min))
                        index(nc.vector.tensor_tensor(ok_f[:, j], tmp_f[:, j], pos_f[:, j], ALU.is_equal))
                    index(nc.vector.scalar_tensor_tensor(out=row_f[:], in0=tmp_f[:, 0], scalar=float(T), in1=tmp_f[:, 1],
                                                         op0=ALU.mult, op1=ALU.add))
                    index(nc.vector.tensor_tensor(ok_f[:, 0], ok_f[:, 0], ok_f[:, 1], ALU.mult))
                    index(nc.vector.tensor_scalar(ok_f[:, 0], ok_f[:, 0], -float(2 * ROWS), float(2 * ROWS), ALU.mult, ALU.add))
                    index(nc.vector.tensor_tensor(to_f[:], row_f[:], ok_f[:, 0], ALU.add))
                    index(nc.vector.tensor_copy(row_i[:], row_f[:]))
                    index(nc.vector.tensor_copy(to_i[:], to_f[:]))
                    assert count[0] == IDX_STEPS

                    dve.wait_ge(gathered, 16 * 2 * MT)
                    for m in range(MT):
                        ins = nc.vector.bn_stats(mst[:, m], hg[:, m])
                    ins.then_inc(lnm, 1)
                    dve.wait_ge(lnm, 1)
                    for m in range(MT):
                        ins = nc.vector.bn_aggr(mmv[:, m], mst[:, m])
                    ins.then_inc(lnm, 1)
                    dve.wait_ge(lnm, 2)
                    nc.vector.tensor_scalar(mve[:], mmv[:, :, 1], EPS, None, ALU.add).then_inc(lnm, MT - 1)
                    dve.wait_ge(lnm_pow, 1)
                    for m in range(MT):
                        nc.vector.tensor_scalar(xm[:, m], hg[:, m], mmv[:, m, 0:1], mrs[:, m:m + 1],
                                                ALU.subtract, ALU.mult).then_inc(lnm, 1)

                    gates = [0]

                    def gate(ins):
                        gates[0] += 1
                        ins.then_inc(gate_step, 1)
                        dve.wait_ge(gate_step, gates[0])

                    dve.wait_ge(gate_mm, 1)
                    dve.wait_ge(ew_in, EW_IN)
                    gate(nc.vector.tensor_tensor(sc[:], psum[:, 7, 0:MT * (1 + E)].rearrange("p (m e) -> p m e", m=MT),
                                                 gb[:].unsqueeze(1).to_broadcast([P, MT, 1 + E]), ALU.add))
                    dve.wait_ge(gate_act, 1)
                    gate(nc.vector.tensor_scalar(sc[:], sc[:], 1.0, None, ALU.add))
                    gate(nc.vector.reciprocal(sc[:], sc[:]))
                    gate(nc.vector.tensor_tensor(biased[:], sc[:, :, 1:], xb[:].unsqueeze(1).to_broadcast([P, MT, E]), ALU.add))
                    gate(nc.vector.tensor_reduce(best[:], biased[:], AX.X, ALU.max))
                    gate(nc.vector.tensor_tensor(hot[:], biased[:], best[:].unsqueeze(2).to_broadcast([P, MT, E]), ALU.is_equal))
                    dve.wait_ge(pool_c, 3)
                    gate(nc.vector.tensor_tensor(hot[:], hot[:], prio[:].unsqueeze(1).to_broadcast([P, MT, E]), ALU.mult))
                    gate(nc.vector.tensor_reduce(best[:], hot[:], AX.X, ALU.max))
                    gate(nc.vector.tensor_tensor(hot[:], hot[:], best[:].unsqueeze(2).to_broadcast([P, MT, E]), ALU.is_equal))
                    gate(nc.vector.tensor_tensor(biased[:], hot[:], sc[:, :, 1:], ALU.mult))
                    gate(nc.vector.tensor_reduce(two[:, :, 1:2], biased[:], AX.X, ALU.add))
                    gate(nc.vector.tensor_copy(two[:, :, 0:1], sc[:, :, 0:1]))
                    gate(nc.vector.tensor_reduce(best[:], two[:], AX.X, ALU.max))
                    gate(nc.vector.tensor_tensor(two[:], two[:], best[:].unsqueeze(2).to_broadcast([P, MT, 2]), ALU.subtract))
                    dve.wait_ge(gate_act, 2)
                    gate(nc.vector.tensor_reduce(best[:], wts[:], AX.X, ALU.add))
                    gate(nc.vector.reciprocal(best[:], best[:]))
                    gate(nc.vector.tensor_tensor(wts[:], wts[:], best[:].unsqueeze(2).to_broadcast([P, MT, 2]), ALU.mult))
                    assert gates[0] == GATE_STEPS

                    def bias_in(m):
                        for j, (a, b) in enumerate(((a1, eb1b), (a2, eb2b))):
                            dve.wait_ge(h12_mm, 2 * m + j + 1)
                            if m >= 2:
                                dve.wait_ge(zt_mm, m - 1)
                            nc.vector.tensor_tensor(a[:, m % 2].rearrange("p (c e) h -> p c (e h)", c=2),
                                                    psum[:, 2 * j:2 * j + 2, :],
                                                    b[:].rearrange("p (c n) -> p c n", c=2), ALU.add).then_inc(a_done, 1)

                    def gated(m):
                        dve.wait_ge(at_done, m + 1)
                        dve.wait_ge(a_done, 2 * m + 2)
                        nc.vector.scalar_tensor_tensor(out=a1[:, m % 2], in0=at[:, m % 2], scalar=1.0, in1=a1[:, m % 2],
                                                       op0=ALU.add, op1=ALU.mult).then_inc(gated_1, 1)
                        dve.wait_ge(gated_1, m + 1)
                        nc.vector.scalar_tensor_tensor(out=a1[:, m % 2], in0=a1[:, m % 2], scalar=0.5, in1=a2[:, m % 2],
                                                       op0=ALU.mult, op1=ALU.mult).then_inc(ev_done, 1)

                    def stats(m):
                        dve.wait_ge(ev_done, m + 1)
                        for x in range(E):
                            ins = nc.vector.bn_stats(est[:, m % 2, x], a1[:, m % 2, x])
                        ins.then_inc(est_step, 1)
                        dve.wait_ge(est_step, 3 * m + 1)
                        for x in range(E):
                            ins = nc.vector.bn_aggr(emv[:, m % 2, x], est[:, m % 2, x])
                        ins.then_inc(est_step, 1)
                        dve.wait_ge(est_step, 3 * m + 2)
                        nc.vector.tensor_scalar(eve[:, m % 2], emv[:, m % 2, :, 1], EPS, None, ALU.add).then_inc(est_step, 1)

                    def affine(m):
                        z = a1[:, m % 2]
                        over_h = [P, E, H]
                        dve.wait_ge(ers_done, m + 1)
                        steps = ((emv[:, m % 2, :, 0:1].to_broadcast(over_h), ALU.subtract),
                                 (ers[:, m % 2].unsqueeze(2).to_broadcast(over_h), ALU.mult),
                                 (selg[:].unsqueeze(1).to_broadcast(over_h), ALU.mult),
                                 (selb[:].unsqueeze(1).to_broadcast(over_h), ALU.add),
                                 (hot[:, m].unsqueeze(2).to_broadcast(over_h), ALU.mult))
                        for n, (other, op) in enumerate(steps):
                            nc.vector.tensor_tensor(z, z, other, op).then_inc(zn_step, 1)
                            if n < 4:
                                dve.wait_ge(zn_step, 5 * m + n + 1)

                    def combine(m):
                        nc.vector.scalar_tensor_tensor(out=og[:, m], in0=og[:, m], scalar=wts[:, m, 0:1], in1=hg[:, m],
                                                       op0=ALU.mult, op1=ALU.add).then_inc(part_done, 1)
                        dve.wait_ge(part_done, m + 1)
                        dve.wait_ge(e3_mm, m + 1)
                        nc.vector.scalar_tensor_tensor(out=res[:, m], in0=psum[:, 6, 0:DM], scalar=wts[:, m, 1:2], in1=og[:, m],
                                                       op0=ALU.mult, op1=ALU.add).then_inc(res_done, 1)

                    dve.wait_ge(shared_done, 1)
                    bias_in(0)
                    for m in range(MT):
                        if m + 1 < MT:
                            bias_in(m + 1)
                        gated(m)
                        stats(m)
                        affine(m)
                        if m >= 1:
                            combine(m - 1)
                    combine(MT - 1)

                @block.gpsimd
                def _(pool):
                    nc.gpsimd.memset(ident2[:], 0.0).then_inc(pool_c, 1)
                    pool.wait_ge(pool_c, 1)
                    nc.gpsimd.affine_select(out=ident2[:], in_=ident2[:], compare_op=ALU.not_equal, fill=1.0, base=0,
                                            pattern=[[-1, P]], channel_multiplier=1)
                    nc.gpsimd.memset(half_neg[:], -0.5)
                    nc.gpsimd.iota(prio_i[:], [[-1, E]], base=E, channel_multiplier=0).then_inc(pool_c, 1)
                    pool.wait_ge(pool_c, 2)
                    nc.gpsimd.tensor_copy(prio[:], prio_i[:]).then_inc(pool_c, 1)

                    pool.wait_ge(idx_step, IDX_STEPS)
                    for m in range(MT):
                        for dst, table in ((hg, h2_scratch), (og, out_rows)):
                            nc.gpsimd.indirect_dma_start(out=dst[:, m], out_offset=None, in_=table,
                                                         in_offset=bass.IndirectOffsetOnAxis(ap=row_i[:, m:m + 1], axis=0)
                                                         ).then_inc(gathered, 16)
                    pool.wait_ge(lnm, 1 + MT)
                    nc.gpsimd.tensor_tensor(mrs[:], mve[:], half_neg[:, :, 0], ALU.pow).then_inc(lnm_pow, 1)
                    nc.gpsimd.tensor_tensor(og[:], og[:], hg[:], ALU.subtract).then_inc(shared_done, 1)

                    def rstd_of(m):
                        pool.wait_ge(est_step, 3 * m + 3)
                        nc.gpsimd.tensor_tensor(ers[:, m % 2], eve[:, m % 2], half_neg[:, 0], ALU.pow).then_inc(ers_done, 1)

                    def scatter(m):
                        pool.wait_ge(res_done, m + 1)
                        nc.gpsimd.indirect_dma_start(out=out_rows, out_offset=bass.IndirectOffsetOnAxis(ap=to_i[:, m:m + 1], axis=0),
                                                     in_=res[:, m], in_offset=None, bounds_check=ROWS - 1,
                                                     oob_is_err=False).then_inc(scattered, 16)

                    for m in range(MT):
                        rstd_of(m)
                        if m >= 1:
                            scatter(m - 1)
                    scatter(MT - 1)
                    pool.wait_ge(scattered, 16 * MT)


def kernel(**inputs):
    import numpy as np
    import concourse.bacc as bacc
    from concourse.bass_utils import run_bass_kernel_spmd

    a = {k.replace("L0_", ""): np.asarray(v) for k, v in inputs.items()}

    def chunks(w):
        w = w.reshape(w.shape[0], -1)
        return w.reshape(-1, P, w.shape[1]).transpose(1, 0, 2)

    B, C, HW, _ = a["x"].shape
    PATCH, SEQ = 16, 2
    S = HW // PATCH
    G = B // SEQ
    DM = a["tok_W"].shape[0]
    R = a["attn_W_dt"].shape[0]
    E, H, _ = a["ffn_ew1"].shape
    M = a["ffn_index_b"].shape[0]
    x = a["x"].reshape(G, SEQ, C, S, PATCH, S, PATCH).transpose(2, 4, 6, 0, 1, 3, 5)
    x = x.reshape(-1, P, G, SEQ * S * S).transpose(2, 1, 0, 3)
    txt = a["txt"].reshape(G, SEQ, -1, DM // P, P).transpose(0, 4, 3, 1, 2)
    w_x = a["attn_W_x"]
    feed = {
        "x_patches": x, "txt_t": txt, "tok_w": chunks(a["tok_W"].T), "tok_b": a["tok_b"].reshape(-1, P).T,
        "cls_t": a["tok_cls_token"].reshape(-1, P).T, "pos_t": chunks(a["tok_pos_enc"][0].T),
        "w_in": chunks(a["attn_W_in"]), "conv_w": chunks(a["attn_conv_w"]), "conv_b": a["attn_conv_b"].reshape(-1, P).T,
        "w_x": chunks(np.concatenate([w_x[:, R:], w_x[:, :R]], axis=1)), "w_dt": a["attn_W_dt"],
        "b_dt": a["attn_b_dt"][None], "a_log": chunks(a["attn_A_log"]), "d_skip": a["attn_D"].reshape(-1, P).T,
        "w_out": chunks(a["attn_W_out"]), "index_b": a["ffn_index_b"].reshape(M // P, P).T,
        "index_t": a["ffn_index_t"].reshape(M // P, P).T, "sw1": chunks(a["ffn_sw1"].T), "sb1": a["ffn_sb1"],
        "sw2": chunks(a["ffn_sw2"].T), "sb2": a["ffn_sb2"], "sw3": a["ffn_sw3"].T, "sb3": a["ffn_sb3"],
        "s_ln_g": a["ffn_s_ln_g"][:, None], "s_ln_b": a["ffn_s_ln_b"][:, None], "gate_w": chunks(np.concatenate([a["ffn_sg_w"], a["ffn_eg_w"]]).T),
        "sg_b": a["ffn_sg_b"], "eg_b": a["ffn_eg_b"], "exp_bias": a["ffn_exp_bias"],
        "ew1": chunks(a["ffn_ew1"].reshape(E * H, DM).T), "eb1": a["ffn_eb1"].reshape(-1),
        "ew2": chunks(a["ffn_ew2"].reshape(E * H, DM).T), "eb2": a["ffn_eb2"].reshape(-1),
        "ew3": a["ffn_ew3"].transpose(2, 0, 1), "eb3": a["ffn_eb3"],
        "sel_ln_g": a["ffn_sel_ln_g"], "sel_ln_b": a["ffn_sel_ln_b"],
    }
    feed = {k: np.ascontiguousarray(v) for k, v in feed.items()}
    nc = bacc.Bacc("TRN2", target_bir_lowering=False, num_devices=1)
    args = {k: nc.dram_tensor(k, v.shape, mybir.dt.from_np(v.dtype), kind="ExternalInput").ap() for k, v in feed.items()}
    T = 1 + S * S + a["txt"].shape[1]
    out = nc.dram_tensor("out", (B, T, DM), F32, kind="ExternalOutput").ap()
    fusion_kernel(nc, out=out, **args)
    r = run_bass_kernel_spmd(nc, [feed], core_ids=[0])
    return r.results[0]["out"]
```

```python
from contextlib import ExitStack

import concourse.bass as bass
from concourse import mybir

ALU = mybir.AluOpType
ACT = mybir.ActivationFunctionType
AX = mybir.AxisListType
F32 = mybir.dt.float32
I32 = mybir.dt.int32

P = 128
EPS = 1e-5


def fusion_kernel(nc, x_patches, txt_t, tok_w, tok_b, cls_t, pos_t, w_in, conv_w, conv_b, w_x, w_dt, b_dt,
                  a_log, d_skip, w_out, index_b, index_t, sw1, sb1, sw2, sb2, sw3, sb3, s_ln_g, s_ln_b,
                  gate_w, sg_b, eg_b, exp_bias, ew1, eb1, ew2, eb2, ew3, eb3, sel_ln_g, sel_ln_b, out):
    GROUPS, _, FK, IMG2 = x_patches.shape
    SEQ = 2
    IMG = IMG2 // SEQ
    TXT = txt_t.shape[-1]
    T = 1 + IMG + TXT
    TOK = SEQ * T
    DM = out.shape[2]
    DC = DM // P
    DI = d_skip.shape[0] * d_skip.shape[1]
    CH = DI // P
    NS = 2 * a_log.shape[3]
    HS = NS // 2
    QS = HS // 2
    DH = P // 2
    UNITS = 2 * CH
    TAPS = conv_w.shape[2]
    PAD = TAPS - 1
    R = w_dt.shape[0]
    H = sw3.shape[0]
    BATCH = GROUPS * SEQ
    ROWS = BATCH * T
    XRING, ARING, HRING = 4, 2, 4
    M = index_b.shape[0] * index_b.shape[1]
    MT = M // P
    E = gate_w.shape[2] - 1

    bc_scratch = nc.dram_tensor("bc_scratch", (2, 2 * NS, TOK), F32, kind="Internal").ap()
    h2_scratch = nc.dram_tensor("h2_scratch", (ROWS, DM), F32, kind="Internal").ap()
    h2_groups = h2_scratch.rearrange("(g s t) d -> g t s d", s=SEQ, t=T)
    out_groups = out.rearrange("(g s) t d -> g t s d", s=SEQ)
    out_rows = out.rearrange("b t d -> (b t) d")

    with ExitStack() as whole:
        def sem(name):
            return whole.enter_context(nc.semaphore(name))

        def sb_in(stack, name, shape, dt=F32):
            return stack.enter_context(nc.sbuf_tensor(name, shape, dt))

        psum = whole.enter_context(nc.psum_tensor("psum", [P, 8, 512], F32))
        raw = sb_in(whole, "raw", [P, 2, MT], I32)
        pos_f = sb_in(whole, "pos_f", [P, 2, MT])
        tmp_f = sb_in(whole, "tmp_f", [P, 2, MT])
        ok_f = sb_in(whole, "ok_f", [P, 2, MT])
        row_f = sb_in(whole, "row_f", [P, MT])
        to_f = sb_in(whole, "to_f", [P, MT])
        row_i = sb_in(whole, "row_i", [P, MT], I32)
        to_i = sb_in(whole, "to_i", [P, MT], I32)
        idx_in = sem("idx_in")
        idx_step = sem("idx_step")
        IDX_STEPS = 15

        with ExitStack() as ctx:
            def sb(name, shape, dt=F32):
                return sb_in(ctx, name, shape, dt)

            tokw = sb("tokw", [P, FK, DM])
            tokb = sb("tokb", [P, DC])
            cls = sb("cls", [P, DC])
            pos = sb("pos", [P, DC, 1 + IMG])
            win = sb("win", [P, DC, 2 * DI])
            cw = sb("cw", [P, CH, TAPS])
            cb = sb("cb", [P, CH])
            wx = sb("wx", [P, CH, 2 * NS + R])
            wdt = sb("wdt", [64, DI])
            a_neg = sb("a_neg", [P, CH, 2, HS])
            dsk = sb("dsk", [P, CH])
            skip_w = sb("skip_w", [P, CH, P])
            wout = sb("wout", [P, CH, DM])
            w12 = sb("w12", [P, DC, 2 * H])
            b12 = sb("b12", [P, 2 * H])
            w3 = sb("w3", [P, DM])
            b3 = sb("b3", [P, DM])
            lng = sb("lng", [P, 1])
            lnb = sb("lnb", [P, 1])
            ident = sb("ident", [P, P])
            fold = sb("fold", [P, DH])
            mean_w = sb("mean_w", [P, P])
            neg_half = sb("neg_half", [P, SEQ])

            xp = sb("xp", [P, FK, IMG2])
            h0 = sb("h0", [P, HRING, DC, TOK])
            xh = sb("xh", [P, DC, TOK])
            sq = sb("sq", [P, DC, TOK])
            lnv = sb("lnv", [P, TOK])
            eps = sb("eps", [P, 1])
            rstd = sb("rstd", [P, TOK])
            xi = sb("xi", [P, CH, SEQ, PAD + T])
            xc = sb("xc", [P, CH, TOK])
            tap = sb("tap", [P, CH, TOK])
            xc_tanh = sb("xc_tanh", [P, CH, TOK])
            z_tanh = sb("z_tanh", [P, CH, TOK])
            soft = z_tanh
            xs = sb("xs", [P, 2, CH, TOK])
            sz = sb("sz", [P, 2, CH, TOK])
            dbl = sb("dbl", [64, TOK])
            delta = sb("delta", [P, CH, TOK])
            u = sb("u", [P, CH, TOK])
            bbc = sb("bbc", [P, 2, HS, TOK])
            cbc = sb("cbc", [P, 2, HS, TOK])
            delta2 = sb("delta2", [P, 2, CH, 2, TOK])
            u2 = sb("u2", [P, 2, CH, 2, TOK])
            da = sb("da", [P, ARING, 2, QS, SEQ, T])
            xr = sb("xr", [P, XRING, 2, QS, TOK])
            y = sb("y", [P, CH, TOK])
            h2 = sb("h2", [P, SEQ, DM])
            st2 = sb("st2", [P, SEQ, 6])
            mv2 = sb("mv2", [P, SEQ, 2])
            rs2 = sb("rs2", [P, SEQ])
            ve2 = sb("ve2", [P, SEQ])
            x2 = sb("x2", [P, SEQ, DM])
            x2t = sb("x2t", [P, DC, SEQ, T])
            x12 = sb("x12", [P, SEQ, 2, H])
            th1 = sb("th1", [P, SEQ, H])
            vv = x12[:, :, 0]
            st3 = sb("st3", [P, SEQ, 6])
            mv3 = sb("mv3", [P, SEQ, 2])
            ve3 = sb("ve3", [P, SEQ])
            rs3 = sb("rs3", [P, SEQ])
            vt = sb("vt", [P, SEQ, T])
            ob = sb("ob", [P, 2, SEQ, DM])

            def y_bank(c):
                return psum[:, c % 2, 0:TOK]
            F0, F1 = 2, 3

            def pair(bank):
                return psum[:, bank, 0:2 * TOK].rearrange("p (c t) -> p c t", c=2)
            tok_ps = psum[:, 4, 0:DC * IMG2].rearrange("p (c t) -> p c t", c=DC)
            var_ps = psum[:, 4, 0:TOK]
            mean_ps = psum[:, 5, 0:TOK]
            dbl_ps = psum[0:2 * NS + R, 5, 0:TOK]
            h2_ps = psum[0:T, 6, 0:SEQ * DM].rearrange("p (s d) -> p s d", s=SEQ)
            f12_ps = psum[0:T, 6, 0:SEQ * 2 * H].rearrange("p (s d) -> p s d", s=SEQ)
            x2t_ps = psum[:, 7, 0:DC * TOK].rearrange("p (c s t) -> p c s t", c=DC, s=SEQ)
            vt_ps = psum[:, 5, 0:TOK].rearrange("p (s t) -> p s t", s=SEQ)
            f3_ps = psum[0:T, 6, 0:SEQ * DM].rearrange("p (s d) -> p s d", s=SEQ)

            const_in = sem("const_in")
            const_pool = sem("const_pool")
            const_dve = sem("const_dve")
            const_act = sem("const_act")
            xp_in = sem("xp_in")
            txt_in = sem("txt_in")
            tok_mm = sem("tok_mm")
            img_done = sem("img_done")
            mean_mm = sem("mean_mm")
            cent_done = sem("cent_done")
            sq_done = sem("sq_done")
            var_mm = sem("var_mm")
            lnv_done = sem("lnv_done")
            rstd_done = sem("rstd_done")
            xh_done = sem("xh_done")
            xi_mm = sem("xi_mm")
            xi_ev = sem("xi_ev")
            tap0_done = sem("tap0_done")
            tap_act = sem("tap_act")
            taps_done = sem("taps_done")
            xct_done = sem("xct_done")
            xs_done = sem("xs_done")
            z_mm = sem("z_mm")
            zt_done = sem("zt_done")
            sz_done = sem("sz_done")
            dbl_mm = sem("dbl_mm")
            dbl_ev = sem("dbl_ev")
            bc_out = sem("bc_out")
            b_in = sem("b_in")
            c_in = sem("c_in")
            delta_in = sem("delta_in")
            u_in = sem("u_in")
            dt_mm = sem("dt_mm")
            abs_done = sem("abs_done")
            spe_done = sem("spe_done")
            spl_done = sem("spl_done")
            delta_done = sem("delta_done")
            u_done = sem("u_done")
            exp_done = sem("exp_done")
            dbu_done = sem("dbu_done")
            scan_done = sem("scan_done")
            hc_done = sem("hc_done")
            red_mm = sem("red_mm")
            y_done = sem("y_done")
            h2_mm = sem("h2_mm")
            h2_ev = sem("h2_ev")
            h2_out = sem("h2_out")
            h2b_done = sem("h2b_done")
            st2_done = sem("st2_done")
            mv2_done = sem("mv2_done")
            ve2_done = sem("ve2_done")
            rs2_done = sem("rs2_done")
            x2_done = sem("x2_done")
            x2t_mm = sem("x2t_mm")
            x2t_ev = sem("x2t_ev")
            f12_mm = sem("f12_mm")
            x12_done = sem("x12_done")
            th1_done = sem("th1_done")
            gate_done = sem("gate_done")
            v_done = sem("v_done")
            st3_done = sem("st3_done")
            mv3_done = sem("mv3_done")
            ve3_done = sem("ve3_done")
            rs3_done = sem("rs3_done")
            vn_done = sem("vn_done")
            vt_mm = sem("vt_mm")
            vt_ev = sem("vt_ev")
            f3_mm = sem("f3_mm")
            o_done = sem("o_done")
            out_out = sem("out_out")

            const_loads = [
                (tokw[:], tok_w), (tokb[:], tok_b), (cls[:], cls_t), (pos[:], pos_t), (win[:], w_in),
                (cw[:], conv_w), (cb[:], conv_b), (wx[:], w_x), (wdt[32:32 + R, :], w_dt),
                (wdt[32 + R:33 + R, :], b_dt), (a_neg[:], a_log), (dsk[:], d_skip), (wout[:], w_out),
                (w12[:, :, 0:H], sw1), (w12[:, :, H:2 * H], sw2), (w3[:], sw3),
                (b12[:, 0:H], sb1.partition_broadcast(P)), (b12[:, H:2 * H], sb2.partition_broadcast(P)),
                (b3[:], sb3.partition_broadcast(P)), (lng[:], s_ln_g), (lnb[:], s_ln_b),
            ]
            CONST_IN = 16 * len(const_loads)
            CONST_POOL = 8
            CONST_DVE = 5 + 2 * DC + CH

            def need(e, semaphore, value):
                if not isinstance(value, int) or value > 0:
                    e.wait_ge(semaphore, value)

            def runs(g):
                return not isinstance(g, int) or 0 <= g < GROUPS

            def upto(count):
                return min(count, GROUPS) if isinstance(count, int) else count

            def over_steps(e, body):
                turns = (GROUPS - 6) // HRING
                for i in range(-3, 3):
                    body(i, i % HRING)
                with e.Fori(0, turns) as turn:
                    for j in range(HRING):
                        body(HRING * turn + 3 + j, (3 + j) % HRING)
                for i in range(3 + HRING * turns, GROUPS + 3):
                    body(i, i % HRING)

            with nc.Block() as block:

                @block.sync
                def _(sp):
                    def load_patches(g):
                        sp.dma_start(xp[:], x_patches[g]).then_inc(xp_in, 16)

                    def spread(src, dst, done):
                        for j in range(2):
                            for q in range(2):
                                sp.dma_start(dst[q * DH:(q + 1) * DH, :, j], src[j * DH:(j + 1) * DH]).then_inc(done, 16)

                    def load_text(g, r):
                        for s in range(SEQ):
                            sp.dma_start(h0[:, r, :, s * T + 1 + IMG:(s + 1) * T], txt_t[g, :, :, s]).then_inc(txt_in, 16)

                    def body(i, r):
                        if runs(i - 3):
                            sp.wait_ge(o_done, i - 2)
                            sp.dma_start(out_groups[i - 3], ob[0:T, (r - 3) % 2]).then_inc(out_out, 16)
                        if runs(i):
                            need(sp, dbu_done, UNITS * i)
                            need(sp, hc_done, UNITS * i)
                        if runs(i + 3):
                            if isinstance(i, int):
                                need(sp, mean_mm, i + 3)
                            need(sp, h2_mm, i)
                            load_text(i + 3, (r + 3) % HRING)
                        if runs(i + 1):
                            p = (r + 1) % 2
                            sp.wait_ge(dbl_ev, i + 2)
                            sp.dma_start(bc_scratch[p], dbl[0:2 * NS, :]).then_inc(bc_out, 16)
                            sp.wait_ge(bc_out, 16 * (i + 2))
                            for buf, lo, s in ((bbc, 0, b_in), (cbc, NS, c_in)):
                                for q in range(2):
                                    rows = bc_scratch[p, lo + q * HS:lo + (q + 1) * HS].rearrange("n t -> (n t)")
                                    sp.dma_start(buf[q * DH:(q + 1) * DH, p].rearrange("p n t -> p (n t)"),
                                                 rows.partition_broadcast(DH)).then_inc(s, 16)
                        if runs(i - 1):
                            sp.wait_ge(h2_ev, i)
                            sp.wait_ge(h2b_done, i)
                            sp.dma_start(h2_groups[i - 1], h2[0:T]).then_inc(h2_out, 16)
                        if runs(i + 1):
                            sp.wait_ge(delta_done, 2 * i + 4)
                            spread(delta, delta2[:, (r + 1) % 2], delta_in)
                            sp.wait_ge(u_done, i + 2)
                            spread(u, u2[:, (r + 1) % 2], u_in)
                        if runs(i + 4):
                            sp.wait_ge(tok_mm, i + 4)
                            load_patches(i + 4)

                    sp.dma_start(raw[:, 0], index_b).then_inc(idx_in, 16)
                    sp.dma_start(raw[:, 1], index_t).then_inc(idx_in, 16)
                    for dst, src in const_loads:
                        sp.dma_start(dst, src).then_inc(const_in, 16)
                    load_patches(0)
                    over_steps(sp, body)
                    sp.wait_ge(h2_out, 16 * GROUPS)
                    sp.wait_ge(out_out, 16 * GROUPS)

                @block.tensor
                def _(pe):
                    def project(bank, half, lhs, first):
                        for c in range(2):
                            for k in range(DC):
                                mm = pe.matmul(pair(bank)[:, c], lhs[:, k, (first + 2 * half + c) * P:(first + 2 * half + c + 1) * P],
                                               xh[:, k], start=(k == 0), stop=(k == DC - 1))
                        return mm

                    def tokens(g):
                        pe.wait_ge(xp_in, 16 * (g + 1))
                        need(pe, lnv_done, g)
                        for c in range(DC):
                            for k in range(FK):
                                mm = pe.matmul(tok_ps[:, c], tokw[:, k, c * P:(c + 1) * P], xp[:, k],
                                               start=(k == 0), stop=(k == FK - 1))
                        mm.then_inc(tok_mm, 1)

                    def mean(g, r):
                        pe.wait_ge(img_done, g + 1)
                        pe.wait_ge(txt_in, 16 * SEQ * (g + 1))
                        need(pe, dbl_ev, g - 1)
                        need(pe, vt_ev, g - 4)
                        for k in range(DC):
                            mm = pe.matmul(mean_ps, mean_w[:], h0[:, r, k], start=(k == 0), stop=(k == DC - 1))
                        mm.then_inc(mean_mm, 1)

                    def var(g):
                        pe.wait_ge(sq_done, g + 1)
                        for k in range(DC):
                            mm = pe.matmul(var_ps, mean_w[:], sq[:, k], start=(k == 0), stop=(k == DC - 1))
                        mm.then_inc(var_mm, 1)

                    def proj_x(g):
                        pe.wait_ge(xh_done, g + 1)
                        for half, bank in ((0, F0), (1, F1)):
                            if not (isinstance(g, int) and g == 0):
                                pe.wait_ge(delta_done, 2 * g - 1 + half)
                            project(bank, half, win, 0).then_inc(xi_mm, 1)

                    def proj_z(g):
                        for half, bank in ((0, F0), (1, F1)):
                            pe.wait_ge(xi_ev, 2 * g + 1 + half)
                            project(bank, half, win, CH).then_inc(z_mm, 1)

                    def proj_bcdt(g, p):
                        pe.wait_ge(xs_done, g + 1)
                        pe.wait_ge(cent_done, upto(g + 2))
                        for c in range(CH):
                            mm = pe.matmul(dbl_ps, wx[:, c], xs[:, p, c], start=(c == 0), stop=(c == CH - 1))
                        mm.then_inc(dbl_mm, 1)

                    def proj_delta(g):
                        pe.wait_ge(dbl_ev, g + 1)
                        for half, bank in ((0, F0), (1, F1)):
                            pe.wait_ge(sz_done, 2 * g + 1 + half)
                            for c in range(2):
                                mm = pe.matmul(pair(bank)[:, c], wdt[32:33 + R, (2 * half + c) * P:(2 * half + c + 1) * P],
                                               dbl[32:33 + R, :], start=True, stop=True)
                            mm.then_inc(dt_mm, 1)

                    def reduce_states(i, r, k):
                        c, v = k // 2, UNITS * i + k
                        pe.wait_ge(hc_done, v + 1)
                        if k % 2 == 0:
                            need(pe, y_done, CH * i + c - 1)
                            pe.matmul(y_bank(c), skip_w[:, c], xs[:, r % 2, c], start=True, stop=False)
                        for n in range(QS):
                            for j in range(2):
                                mm = pe.matmul(y_bank(c)[j * DH:(j + 1) * DH], fold[:], xr[:, k % XRING, j, n],
                                               start=False, stop=(k % 2 == 1 and n == QS - 1))
                        mm.then_inc(red_mm, 1)

                    def out_proj(g, r):
                        pe.wait_ge(y_done, CH * (g + 1))
                        need(pe, x12_done, g)
                        for s in range(SEQ):
                            for k in range(DC):
                                pe.matmul(h2_ps[:, s, k * P:(k + 1) * P], h0[:, r, k, s * T:(s + 1) * T], ident[:],
                                          start=(k == 0), stop=False)
                            for c in range(CH):
                                mm = pe.matmul(h2_ps[:, s], y[:, c, s * T:(s + 1) * T], wout[:, c],
                                               start=False, stop=(c == CH - 1))
                        mm.then_inc(h2_mm, 1)

                    def x2_turn(g):
                        pe.wait_ge(x2_done, g + 1)
                        need(pe, x2t_ev, g)
                        for k in range(DC):
                            for s in range(SEQ):
                                mm = pe.transpose(x2t_ps[:, k, s], x2[0:T, s, k * P:(k + 1) * P], ident[0:T, 0:T])
                        mm.then_inc(x2t_mm, 1)

                    def ffn_in(g):
                        pe.wait_ge(x2t_ev, g + 1)
                        need(pe, o_done, g)
                        for s in range(SEQ):
                            for k in range(DC):
                                mm = pe.matmul(f12_ps[:, s], x2t[:, k, s], w12[:, k], start=(k == 0), stop=(k == DC - 1))
                        mm.then_inc(f12_mm, 1)

                    def v_turn(g):
                        pe.wait_ge(vn_done, g + 1)
                        pe.wait_ge(dbl_ev, upto(g + 4))
                        for s in range(SEQ):
                            mm = pe.transpose(vt_ps[:, s], vv[0:T, s], ident[0:T, 0:T])
                        mm.then_inc(vt_mm, 1)

                    def ffn_out(g):
                        pe.wait_ge(vt_ev, g + 1)
                        pe.wait_ge(h2_ev, upto(g + 2))
                        for s in range(SEQ):
                            mm = pe.matmul(f3_ps[:, s], vt[:, s], w3[:], start=True, stop=True)
                        mm.then_inc(f3_mm, 1)

                    def body(i, r):
                        if runs(i + 1):
                            proj_z(i + 1)
                        if runs(i - 2):
                            ffn_in(i - 2)
                        if runs(i):
                            reduce_states(i, r, 0)
                        if runs(i + 2):
                            mean(i + 2, (r + 2) % HRING)
                        if runs(i):
                            reduce_states(i, r, 1)
                        if runs(i - 1):
                            out_proj(i - 1, (r - 1) % HRING)
                        if runs(i):
                            reduce_states(i, r, 2)
                        if runs(i + 1):
                            proj_bcdt(i + 1, (r + 1) % 2)
                        if runs(i + 1):
                            proj_delta(i + 1)
                        if runs(i):
                            reduce_states(i, r, 3)
                        if runs(i + 2):
                            var(i + 2)
                        if runs(i):
                            reduce_states(i, r, 4)
                            reduce_states(i, r, 5)
                        if runs(i - 1):
                            x2_turn(i - 1)
                        if runs(i - 2):
                            v_turn(i - 2)
                        if runs(i + 2):
                            proj_x(i + 2)
                        if runs(i):
                            reduce_states(i, r, 6)
                        if runs(i - 2):
                            ffn_out(i - 2)
                        if runs(i + 3):
                            tokens(i + 3)
                        if runs(i):
                            reduce_states(i, r, 7)

                    pe.wait_ge(const_in, CONST_IN)
                    pe.wait_ge(const_pool, CONST_POOL)
                    pe.wait_ge(const_dve, CONST_DVE)
                    over_steps(pe, body)

                @block.scalar
                def _(act):
                    def exps(i, p, k):
                        c, v, slot = k // 2, UNITS * i + k, k % ARING
                        act.wait_ge(delta_in, 64 * (i + 1))
                        need(act, scan_done, v - ARING + 1)
                        for j in range(2):
                            for n in range(QS):
                                st = (k % 2) * QS + n
                                ins = nc.scalar.activation(
                                    da[:, slot, j, n, :, 1:T], delta2[:, p, c, j].rearrange("p (s t) -> p s t", s=SEQ)[:, :, 1:T],
                                    ACT.Exp, scale=a_neg[:, c, j, st:st + 1])
                        ins.then_inc(exp_done, 1)

                    def square(g):
                        act.wait_ge(cent_done, g + 1)
                        nc.scalar.activation(sq[:], xh[:], ACT.Square).then_inc(sq_done, 1)

                    def rstd_out(g):
                        act.wait_ge(var_mm, g + 1)
                        nc.scalar.activation(lnv[:], var_ps, ACT.Ln, bias=eps[:, 0:1]).then_inc(lnv_done, 1)
                        act.wait_ge(lnv_done, g + 1)
                        nc.scalar.activation(rstd[:], lnv[:], ACT.Exp, scale=-0.5).then_inc(rstd_done, 1)

                    def x_out(g):
                        for half, bank in ((0, F0), (1, F1)):
                            act.wait_ge(xi_mm, 2 * g + 1 + half)
                            nc.scalar.activation(xi[:, 2 * half:2 * half + 2, :, PAD:],
                                                 pair(bank).rearrange("p c (s t) -> p c s t", s=SEQ),
                                                 ACT.Copy).then_inc(xi_ev, 1)
                        act.wait_ge(xi_ev, 2 * g + 2)
                        need(act, xs_done, g)
                        for c in range(CH):
                            ins = nc.scalar.activation(xc[:, c].rearrange("p (s t) -> p s t", s=SEQ), xi[:, c, :, PAD:],
                                                       ACT.Identity, bias=cb[:, c:c + 1], scale=cw[:, c, PAD:TAPS])
                        ins.then_inc(tap0_done, 1)

                    def taps(g, first, end):
                        for t in range(first, end):
                            if t >= 2:
                                act.wait_ge(taps_done, PAD * g + t - 1)
                            to = (tap, xc_tanh)[t % 2]
                            for c in range(CH):
                                ins = nc.scalar.activation(to[:, c].rearrange("p (s t) -> p s t", s=SEQ), xi[:, c, :, t:t + T],
                                                           ACT.Copy, scale=cw[:, c, t:t + 1])
                            ins.then_inc(tap_act, 1)

                    def z_gate(g):
                        for half, bank in ((0, F0), (1, F1)):
                            act.wait_ge(z_mm, 2 * g + 1 + half)
                            nc.scalar.activation(z_tanh[:, 2 * half:2 * half + 2], pair(bank), ACT.Tanh).then_inc(zt_done, 1)

                    def x_gate(g):
                        act.wait_ge(taps_done, PAD * (g + 1))
                        nc.scalar.activation(xc_tanh[:], xc[:], ACT.Tanh).then_inc(xct_done, 1)

                    def dbl_copy(g):
                        act.wait_ge(dbl_mm, g + 1)
                        need(act, bc_out, 16 * g)
                        nc.scalar.activation(dbl[0:2 * NS + R, :], dbl_ps, ACT.Copy).then_inc(dbl_ev, 1)

                    def softplus(g):
                        for half, bank in ((0, F0), (1, F1)):
                            act.wait_ge(dt_mm, 2 * g + 1 + half)
                            nc.scalar.activation(soft[:, 2 * half:2 * half + 2], pair(bank), ACT.Abs).then_inc(abs_done, 1)
                        act.wait_ge(abs_done, 2 * g + 2)
                        nc.scalar.activation(soft[:], soft[:], ACT.Exp, scale=-1.0).then_inc(spe_done, 1)
                        act.wait_ge(spe_done, g + 1)
                        nc.scalar.activation(soft[:], soft[:], ACT.Ln, bias=1.0).then_inc(spl_done, 1)

                    def h2_copy(g):
                        act.wait_ge(h2_mm, g + 1)
                        need(act, h2_out, 16 * g)
                        need(act, h2b_done, g)
                        nc.scalar.activation(h2[0:T], h2_ps, ACT.Copy).then_inc(h2_ev, 1)

                    def x2t_copy(g):
                        act.wait_ge(x2t_mm, g + 1)
                        nc.scalar.activation(x2t[:], x2t_ps, ACT.Copy).then_inc(x2t_ev, 1)

                    def ffn_tanh(g):
                        act.wait_ge(x12_done, g + 1)
                        nc.scalar.activation(th1[0:T], x12[0:T, :, 0], ACT.Tanh, scale=0.5).then_inc(th1_done, 1)

                    def vt_copy(g):
                        act.wait_ge(vt_mm, g + 1)
                        nc.scalar.activation(vt[:], vt_ps, ACT.Identity, bias=lnb[:, 0:1], scale=lng[:, 0:1]).then_inc(vt_ev, 1)

                    def body(i, r):
                        p = r % 2
                        if runs(i):
                            exps(i, p, 0)
                        if runs(i - 3):
                            vt_copy(i - 3)
                        if runs(i - 2):
                            x2t_copy(i - 2)
                        if runs(i + 1):
                            x_out(i + 1)
                        if runs(i + 1):
                            taps(i + 1, 0, 2)
                        if runs(i):
                            exps(i, p, 1)
                        if runs(i):
                            exps(i, p, 2)
                        if runs(i + 1):
                            taps(i + 1, 2, PAD)
                        if runs(i):
                            exps(i, p, 3)
                        if runs(i + 1):
                            z_gate(i + 1)
                        if runs(i - 2):
                            ffn_tanh(i - 2)
                        if runs(i + 1):
                            x_gate(i + 1)
                        act.preload_act_table_set("natural_log_exp_and_others")
                        if runs(i):
                            exps(i, p, 4)
                        if runs(i + 1):
                            dbl_copy(i + 1)
                        if runs(i - 1):
                            h2_copy(i - 1)
                        if runs(i + 2):
                            square(i + 2)
                        if runs(i):
                            exps(i, p, 5)
                        if runs(i + 1):
                            softplus(i + 1)
                        if runs(i):
                            exps(i, p, 6)
                        if runs(i + 2):
                            rstd_out(i + 2)
                        if runs(i):
                            exps(i, p, 7)

                    act.wait_ge(const_in, CONST_IN)
                    nc.scalar.activation(a_neg[:], a_neg[:], ACT.Exp).then_inc(const_act, 1)
                    act.wait_ge(const_pool, CONST_POOL)
                    act.wait_ge(const_dve, CONST_DVE)
                    over_steps(act, body)

                @block.vector
                def _(dve):
                    def scan(i, p, k):
                        v = UNITS * i + k
                        dve.wait_ge(exp_done, v + 1)
                        dve.wait_ge(dbu_done, v + 1)
                        x = xr[:, k % XRING].rearrange("p j n t -> p (j n t)")
                        nc.vector.tensor_tensor_scan(x, da[:, k % ARING].rearrange("p j n s t -> p (j n s t)"), x, 0.0,
                                                     ALU.mult, ALU.add).then_inc(scan_done, 1)

                    def times_c(i, p, k):
                        v = UNITS * i + k
                        if k == 0:
                            dve.wait_ge(c_in, 32 * (i + 1))
                        dve.wait_ge(scan_done, v + 1)
                        nc.vector.tensor_tensor(xr[:, k % XRING], xr[:, k % XRING],
                                                cbc[:, p, (k % 2) * QS:(k % 2 + 1) * QS].unsqueeze(1).to_broadcast([P, 2, QS, TOK]),
                                                ALU.mult).then_inc(hc_done, 1)

                    def y_out(g, p, c):
                        dve.wait_ge(red_mm, UNITS * g + 2 * c + 2)
                        need(dve, h2_mm, g)
                        nc.vector.tensor_tensor(y[:, c], y_bank(c), sz[:, p, c], ALU.mult).then_inc(y_done, 1)

                    def image_tokens(g, r):
                        dve.wait_ge(tok_mm, g + 1)
                        nc.vector.tensor_tensor(
                            h0[:, r].rearrange("p c (s t) -> p c s t", s=SEQ)[:, :, :, 1:1 + IMG],
                            tok_ps.rearrange("p c (s t) -> p c s t", s=SEQ),
                            pos[:, :, 1:].unsqueeze(2).to_broadcast([P, DC, SEQ, IMG]), ALU.add).then_inc(img_done, 1)

                    def center(g, r):
                        dve.wait_ge(mean_mm, g + 1)
                        nc.vector.tensor_tensor(xh[:], h0[:, r], mean_ps.unsqueeze(1).to_broadcast([P, DC, TOK]),
                                                ALU.subtract).then_inc(cent_done, 1)

                    def normalize(g):
                        dve.wait_ge(rstd_done, g + 1)
                        dve.wait_ge(cent_done, g + 1)
                        nc.vector.tensor_tensor(xh[:], xh[:], rstd[:].unsqueeze(1).to_broadcast([P, DC, TOK]),
                                                ALU.mult).then_inc(xh_done, 1)

                    def z_silu(g, p):
                        for half, bank in ((0, F0), (1, F1)):
                            dve.wait_ge(zt_done, 2 * g + 1 + half)
                            nc.vector.scalar_tensor_tensor(out=sz[:, p, 2 * half:2 * half + 2], in0=z_tanh[:, 2 * half:2 * half + 2],
                                                           scalar=1.0, in1=pair(bank), op0=ALU.add,
                                                           op1=ALU.mult).then_inc(sz_done, 1)

                    def x_silu(g, p):
                        dve.wait_ge(xct_done, g + 1)
                        nc.vector.scalar_tensor_tensor(out=xs[:, p], in0=xc_tanh[:], scalar=1.0, in1=xc[:],
                                                       op0=ALU.add, op1=ALU.mult).then_inc(xs_done, 1)

                    def ffn_gate(g):
                        dve.wait_ge(th1_done, g + 1)
                        nc.vector.scalar_tensor_tensor(out=vv[0:T], in0=th1[0:T], scalar=1.0, in1=x12[0:T, :, 0],
                                                       op0=ALU.add, op1=ALU.mult).then_inc(gate_done, 1)
                        dve.wait_ge(gate_done, g + 1)
                        nc.vector.scalar_tensor_tensor(out=vv[0:T], in0=vv[0:T], scalar=0.5, in1=x12[0:T, :, 1],
                                                       op0=ALU.mult, op1=ALU.mult).then_inc(v_done, 1)

                    def delta_out(g):
                        dve.wait_ge(spl_done, g + 1)
                        need(dve, u_done, g)
                        need(dve, delta_in, 64 * g)
                        for half, bank in ((0, F0), (1, F1)):
                            nc.vector.scalar_tensor_tensor(out=delta[:, 2 * half:2 * half + 2], in0=pair(bank), scalar=0.0,
                                                           in1=soft[:, 2 * half:2 * half + 2], op0=ALU.max,
                                                           op1=ALU.add).then_inc(delta_done, 1)

                    def ln2_stats(g):
                        dve.wait_ge(h2_ev, g + 1)
                        for s in range(SEQ):
                            ins = nc.vector.bn_stats(st2[0:T, s], h2[0:T, s])
                        ins.then_inc(st2_done, 1)
                        dve.wait_ge(st2_done, g + 1)

                    def ln2_moments(g):
                        for s in range(SEQ):
                            ins = nc.vector.bn_aggr(mv2[0:T, s], st2[0:T, s])
                        ins.then_inc(mv2_done, 1)
                        dve.wait_ge(mv2_done, g + 1)
                        nc.vector.tensor_scalar(ve2[0:T], mv2[0:T, :, 1], EPS, None, ALU.add).then_inc(ve2_done, 1)

                    def ln2_apply(g):
                        dve.wait_ge(rs2_done, g + 1)
                        for s in range(SEQ):
                            ins = nc.vector.tensor_scalar(x2[0:T, s], h2[0:T, s], mv2[0:T, s, 0:1], rs2[0:T, s:s + 1],
                                                          ALU.subtract, ALU.mult)
                        ins.then_inc(x2_done, 1)

                    def ffn_bias(g):
                        dve.wait_ge(f12_mm, g + 1)
                        nc.vector.tensor_tensor(x12[0:T].rearrange("p s a h -> p s (a h)"), f12_ps,
                                                b12[0:T].unsqueeze(1).to_broadcast([T, SEQ, 2 * H]),
                                                ALU.add).then_inc(x12_done, 1)

                    def ln3_stats(g):
                        dve.wait_ge(v_done, g + 1)
                        for s in range(SEQ):
                            ins = nc.vector.bn_stats(st3[0:T, s], vv[0:T, s])
                        ins.then_inc(st3_done, 1)
                        dve.wait_ge(st3_done, g + 1)

                    def ln3_moments(g):
                        for s in range(SEQ):
                            ins = nc.vector.bn_aggr(mv3[0:T, s], st3[0:T, s])
                        ins.then_inc(mv3_done, 1)
                        dve.wait_ge(mv3_done, g + 1)
                        nc.vector.tensor_scalar(ve3[0:T], mv3[0:T, :, 1], EPS, None, ALU.add).then_inc(ve3_done, 1)

                    def ln3_apply(g):
                        dve.wait_ge(rs3_done, g + 1)
                        for s in range(SEQ):
                            ins = nc.vector.tensor_scalar(vv[0:T, s], vv[0:T, s], mv3[0:T, s, 0:1], rs3[0:T, s:s + 1],
                                                          ALU.subtract, ALU.mult)
                        ins.then_inc(vn_done, 1)

                    def ffn_residual(g, p):
                        dve.wait_ge(f3_mm, g + 1)
                        dve.wait_ge(h2b_done, g + 1)
                        nc.vector.tensor_tensor(ob[0:T, p], f3_ps, ob[0:T, p], ALU.add).then_inc(o_done, 1)

                    def body(i, r):
                        p = r % 2
                        q = 1 - p
                        if runs(i - 3):
                            ffn_residual(i - 3, q)
                        if runs(i):
                            scan(i, p, 0)
                        if runs(i + 2):
                            image_tokens(i + 2, (r + 2) % HRING)
                        if runs(i):
                            times_c(i, p, 0)
                        if runs(i - 1):
                            y_out(i - 1, q, CH - 1)
                        if runs(i):
                            scan(i, p, 1)
                            times_c(i, p, 1)
                        if runs(i - 2):
                            ffn_bias(i - 2)
                        if runs(i):
                            scan(i, p, 2)
                        if runs(i + 2):
                            center(i + 2, (r + 2) % HRING)
                        if runs(i):
                            times_c(i, p, 2)
                        if runs(i + 1):
                            z_silu(i + 1, q)
                            x_silu(i + 1, q)
                        if runs(i):
                            scan(i, p, 3)
                            y_out(i, p, 0)
                            times_c(i, p, 3)
                        if runs(i - 2):
                            ffn_gate(i - 2)
                            ln3_stats(i - 2)
                        if runs(i):
                            scan(i, p, 4)
                        elif runs(i - 1):
                            ln2_stats(i - 1)
                        if runs(i - 2):
                            ln3_moments(i - 2)
                        if runs(i):
                            if runs(i - 1):
                                ln2_stats(i - 1)
                            times_c(i, p, 4)
                        if runs(i - 1):
                            ln2_moments(i - 1)
                        if runs(i + 1):
                            delta_out(i + 1)
                        if runs(i):
                            scan(i, p, 5)
                            y_out(i, p, 1)
                            times_c(i, p, 5)
                        if runs(i + 2):
                            normalize(i + 2)
                        if runs(i - 1):
                            ln2_apply(i - 1)
                        if runs(i - 2):
                            ln3_apply(i - 2)
                        if runs(i):
                            scan(i, p, 6)
                            times_c(i, p, 6)
                            scan(i, p, 7)
                            y_out(i, p, 2)
                            times_c(i, p, 7)

                    nc.vector.memset(da[:], 0.0).then_inc(const_dve, 1)
                    count = [0]

                    def index(ins):
                        count[0] += 1
                        ins.then_inc(idx_step, 1)
                        dve.wait_ge(idx_step, count[0])

                    dve.wait_ge(idx_in, 32)
                    index(nc.vector.tensor_copy(pos_f[:], raw[:]))
                    for j, size in ((0, BATCH), (1, T)):
                        index(nc.vector.tensor_scalar(tmp_f[:, j], pos_f[:, j], 0.0, float(size), ALU.is_lt, ALU.mult))
                        index(nc.vector.tensor_tensor(pos_f[:, j], pos_f[:, j], tmp_f[:, j], ALU.add))
                        index(nc.vector.tensor_scalar(tmp_f[:, j], pos_f[:, j], 0.0, float(size - 1), ALU.max, ALU.min))
                        index(nc.vector.tensor_tensor(ok_f[:, j], tmp_f[:, j], pos_f[:, j], ALU.is_equal))
                    index(nc.vector.scalar_tensor_tensor(out=row_f[:], in0=tmp_f[:, 0], scalar=float(T), in1=tmp_f[:, 1],
                                                         op0=ALU.mult, op1=ALU.add))
                    index(nc.vector.tensor_tensor(ok_f[:, 0], ok_f[:, 0], ok_f[:, 1], ALU.mult))
                    index(nc.vector.tensor_scalar(ok_f[:, 0], ok_f[:, 0], -float(2 * ROWS), float(2 * ROWS), ALU.mult, ALU.add))
                    index(nc.vector.tensor_tensor(to_f[:], row_f[:], ok_f[:, 0], ALU.add))
                    index(nc.vector.tensor_copy(row_i[:], row_f[:]))
                    index(nc.vector.tensor_copy(to_i[:], to_f[:]))
                    assert count[0] == IDX_STEPS
                    nc.vector.memset(dbl[32:64, :], 1.0).then_inc(const_dve, 1)
                    dve.wait_ge(const_in, CONST_IN)
                    nc.vector.tensor_scalar(win[:, :, DI:], win[:, :, DI:], 0.5, None, ALU.mult).then_inc(const_dve, 1)
                    nc.vector.tensor_scalar(cw[:], cw[:], 0.5, None, ALU.mult).then_inc(const_dve, 1)
                    for k in range(DC):
                        nc.vector.tensor_scalar(pos[:, k, 1:], pos[:, k, 1:], tokb[:, k:k + 1], None,
                                                ALU.add).then_inc(const_dve, 1)
                    for k in range(DC):
                        nc.vector.tensor_tensor(
                            h0[:, :, k].rearrange("p a (s t) -> p a s t", s=SEQ)[:, :, :, 0],
                            cls[:, k:k + 1].unsqueeze(2).to_broadcast([P, HRING, SEQ]),
                            pos[:, k, 0:1].unsqueeze(2).to_broadcast([P, HRING, SEQ]), ALU.add).then_inc(const_dve, 1)
                    dve.wait_ge(const_pool, CONST_POOL)
                    nc.vector.tensor_tensor(fold[:], ident[:, 0:DH], ident[:, DH:P], ALU.add).then_inc(const_dve, 1)
                    for c in range(CH):
                        nc.vector.tensor_scalar(skip_w[:, c], ident[:], dsk[:, c:c + 1], None, ALU.mult).then_inc(const_dve, 1)
                    dve.wait_ge(const_dve, CONST_DVE)
                    dve.wait_ge(const_pool, CONST_POOL)
                    over_steps(dve, body)

                @block.gpsimd
                def _(pool):
                    def dbu(i, p, k):
                        c, v = k // 2, UNITS * i + k
                        if k == 0:
                            pool.wait_ge(b_in, 32 * (i + 1))
                            pool.wait_ge(u_in, 64 * (i + 1))
                        need(pool, red_mm, v - XRING + 1)
                        nc.gpsimd.tensor_tensor(xr[:, k % XRING],
                                                bbc[:, p, (k % 2) * QS:(k % 2 + 1) * QS].unsqueeze(1).to_broadcast([P, 2, QS, TOK]),
                                                u2[:, p, c].unsqueeze(2).to_broadcast([P, 2, QS, TOK]), ALU.mult).then_inc(dbu_done, 1)

                    def convolve(g, first, end):
                        if first == 0:
                            pool.wait_ge(tap0_done, g + 1)
                        for t in range(first, end):
                            pool.wait_ge(tap_act, PAD * g + t + 1)
                            if t:
                                pool.wait_ge(taps_done, PAD * g + t)
                            nc.gpsimd.tensor_tensor(xc[:], xc[:], (tap, xc_tanh)[t % 2][:], ALU.add).then_inc(taps_done, 1)

                    def u_out(g, p):
                        pool.wait_ge(delta_done, 2 * g + 2)
                        pool.wait_ge(xs_done, g + 1)
                        need(pool, u_in, 64 * g)
                        nc.gpsimd.tensor_tensor(u[:], delta[:], xs[:, p], ALU.mult).then_inc(u_done, 1)

                    def ln2_pow(g):
                        pool.wait_ge(ve2_done, g + 1)
                        nc.gpsimd.tensor_tensor(rs2[0:T], ve2[0:T], neg_half[0:T, 0:SEQ], ALU.pow).then_inc(rs2_done, 1)

                    def residual_bias(g, p):
                        pool.wait_ge(h2_ev, g + 1)
                        need(pool, out_out, 16 * (g - 1))
                        nc.gpsimd.tensor_tensor(ob[0:T, p], h2[0:T], b3[0:T].unsqueeze(1).to_broadcast([T, SEQ, DM]),
                                                ALU.add).then_inc(h2b_done, 1)

                    def ln3_pow(g):
                        pool.wait_ge(ve3_done, g + 1)
                        nc.gpsimd.tensor_tensor(rs3[0:T], ve3[0:T], neg_half[0:T, 0:SEQ], ALU.pow).then_inc(rs3_done, 1)

                    def body(i, r):
                        p = r % 2
                        if runs(i):
                            dbu(i, p, 0)
                            dbu(i, p, 1)
                        if runs(i + 1):
                            convolve(i + 1, 0, 2)
                        if runs(i):
                            dbu(i, p, 2)
                        if runs(i + 1):
                            convolve(i + 1, 2, PAD)
                        if runs(i):
                            dbu(i, p, 3)
                            dbu(i, p, 4)
                            dbu(i, p, 5)
                            dbu(i, p, 6)
                        if runs(i - 2):
                            ln3_pow(i - 2)
                        if runs(i - 1):
                            ln2_pow(i - 1)
                            residual_bias(i - 1, 1 - p)
                        if runs(i + 1):
                            u_out(i + 1, 1 - p)
                        if runs(i):
                            dbu(i, p, 7)

                    nc.gpsimd.memset(ident[:], 0.0).then_inc(const_pool, 1)
                    nc.gpsimd.memset(mean_w[:], 1.0 / DM).then_inc(const_pool, 1)
                    nc.gpsimd.memset(neg_half[:], -0.5).then_inc(const_pool, 1)
                    nc.gpsimd.memset(xi[:], 0.0).then_inc(const_pool, 1)
                    nc.gpsimd.memset(eps[:], EPS).then_inc(const_pool, 1)
                    pool.wait_ge(const_pool, 4)
                    nc.gpsimd.affine_select(out=ident[:], in_=ident[:], compare_op=ALU.not_equal, fill=1.0, base=0,
                                            pattern=[[-1, P]], channel_multiplier=1).then_inc(const_pool, 1)
                    pool.wait_ge(const_act, 1)
                    pool.wait_ge(const_in, CONST_IN)
                    nc.gpsimd.tensor_scalar(a_neg[:], a_neg[:], -1.0, None, ALU.mult).then_inc(const_pool, 1)
                    nc.gpsimd.tensor_scalar(cb[:], cb[:], 0.5, None, ALU.mult).then_inc(const_pool, 1)
                    pool.wait_ge(const_dve, CONST_DVE)
                    over_steps(pool, body)

        with ExitStack() as ctx:
            def sb(name, shape, dt=F32):
                return sb_in(ctx, name, shape, dt)

            e1 = sb("e1", [P, DC, E * H])
            e2 = sb("e2", [P, DC, E * H])
            e3 = sb("e3", [P, E, DM])
            eb1b = sb("eb1b", [P, E * H])
            eb2b = sb("eb2b", [P, E * H])
            eb3r = sb("eb3r", [E, DM])
            gw = sb("gw", [P, DC, 1 + E])
            gb = sb("gb", [P, 1 + E])
            xb = sb("xb", [P, E])
            selg = sb("selg", [P, 1])
            selb = sb("selb", [P, 1])
            selb_e = sb("selb_e", [P, E, E])
            prio = sb("prio", [P, E])
            prio_i = sb("prio_i", [P, E], I32)
            ident2 = sb("ident2", [P, P])
            half_neg = sb("half_neg", [P, MT, E])
            hg = sb("hg", [P, MT, DM])
            og = sb("og", [P, MT, DM])
            mst = sb("mst", [P, MT, 6])
            mmv = sb("mmv", [P, MT, 2])
            mve = sb("mve", [P, MT])
            mrs = sb("mrs", [P, MT])
            xm = sb("xm", [P, MT, DM])
            xmt = sb("xmt", [P, DC, MT, P])
            sc = sb("sc", [P, MT, 1 + E])
            biased = sb("biased", [P, MT, E])
            best = sb("best", [P, MT])
            hot = sb("hot", [P, MT, E])
            hot_t = sb("hot_t", [E, MT, P])
            two = sb("two", [P, MT, 2])
            wts = sb("wts", [P, MT, 2])
            a1 = sb("a1", [P, MT, E, H])
            a2 = sb("a2", [P, MT, E, H])
            at = sb("at", [P, MT, E, H])
            est = sb("est", [P, MT, E, 6])
            emv = sb("emv", [P, MT, E, 2])
            eve = sb("eve", [P, MT, E])
            ers = sb("ers", [P, MT, E])
            ebs = sb("ebs", [P, MT, E])
            eb3x = sb("eb3x", [E, DM])
            zt = sb("zt", [P, 2, E, P])
            res = sb("res", [P, MT, DM])

            gw_in = sem("gw_in")
            ew_in = sem("ew_in")
            pool_c = sem("pool_c")
            gathered = sem("gathered")
            lnm = sem("lnm")
            lnm_pow = sem("lnm_pow")
            xmt_mm = sem("xmt_mm")
            xmt_ev = sem("xmt_ev")
            gate_mm = sem("gate_mm")
            gate_act = sem("gate_act")
            gate_step = sem("gate_step")
            hot_mm = sem("hot_mm")
            hot_ev = sem("hot_ev")
            h12_mm = sem("h12_mm")
            a_done = sem("a_done")
            at_done = sem("at_done")
            shared_done = sem("shared_done")
            gated_1 = sem("gated_1")
            ev_done = sem("ev_done")
            est_step = sem("est_step")
            zn_done = sem("zn_done")
            eb3_mm = sem("eb3_mm")
            eb3_done = sem("eb3_done")
            hot_rs = sem("hot_rs")
            zt_mm = sem("zt_mm")
            zt_ev = sem("zt_ev")
            e3_mm = sem("e3_mm")
            part_done = sem("part_done")
            res_done = sem("res_done")
            scattered = sem("scattered")

            GW = [(gw[:], gate_w), (gb[:, 0:1], sg_b.partition_broadcast(P)), (gb[:, 1:], eg_b.partition_broadcast(P)),
                  (xb[:], exp_bias.partition_broadcast(P)), (selg[:], sel_ln_g), (selb[:], sel_ln_b)]
            GW_IN = 16 * len(GW)
            EW = [(e1[:], ew1), (e2[:], ew2), (eb1b[:], eb1.partition_broadcast(P)),
                  (eb2b[:], eb2.partition_broadcast(P)), (e3[:], ew3), (eb3r[:], eb3)]
            EW_IN = 16 * len(EW)

            GATE_STEPS = 17

            with nc.Block() as block:

                def zt_copy(act, m):
                    act.wait_ge(zt_mm, m + 1)
                    if m >= 2:
                        act.wait_ge(e3_mm, m - 1)
                    nc.scalar.activation(zt[:, m % 2].rearrange("p (a e) t -> p a (e t)", a=2), psum[:, 4:6, :],
                                         ACT.Copy, scale=selg[:, 0:1]).then_inc(zt_ev, 1)

                @block.sync
                def _(sp):
                    for dst, src in GW:
                        sp.dma_start(dst, src).then_inc(gw_in, 16)
                    for dst, src in EW:
                        sp.dma_start(dst, src).then_inc(ew_in, 16)

                @block.tensor
                def _(pe):
                    pe.wait_ge(pool_c, 3)
                    for m in range(MT):
                        pe.wait_ge(lnm, 4 + m)
                        for k in range(DC):
                            mm = pe.transpose(psum[:, k, m * P:(m + 1) * P], xm[:, m, k * P:(k + 1) * P], ident2[:])
                        mm.then_inc(xmt_mm, 1)
                    pe.wait_ge(xmt_ev, DC)
                    pe.wait_ge(gw_in, GW_IN)
                    for m in range(MT):
                        for k in range(DC):
                            mm = pe.matmul(psum[:, 7, m * (1 + E):(m + 1) * (1 + E)], xmt[:, k, m], gw[:, k],
                                           start=(k == 0), stop=(k == DC - 1))
                    mm.then_inc(gate_mm, 1)

                    def hidden(m):
                        if m >= 1:
                            pe.wait_ge(a_done, 2 * m)
                        for j, w in ((0, e1), (1, e2)):
                            for half in range(2):
                                for k in range(DC):
                                    mm = pe.matmul(psum[:, 2 * j + half, :], xmt[:, k, m], w[:, k, half * 512:(half + 1) * 512],
                                                   start=(k == 0), stop=(k == DC - 1))
                            mm.then_inc(h12_mm, 1)

                    def out_of(m):
                        pe.wait_ge(zn_done, m + 1)
                        if m >= 1:
                            pe.wait_ge(zt_ev, m)
                        for x in range(E):
                            mm = pe.transpose(psum[:, 4 + x // 4, (x % 4) * P:(x % 4 + 1) * P], a1[:, m, x], ident2[:])
                        mm.then_inc(zt_mm, 1)
                        pe.wait_ge(zt_ev, m + 1)
                        if m >= 1:
                            pe.wait_ge(res_done, m)
                        else:
                            pe.wait_ge(eb3_done, 1)
                        pe.matmul(psum[:, 6, 0:DM], hot_t[:, m], eb3x[:], start=True, stop=False)
                        for x in range(E):
                            mm = pe.matmul(psum[:, 6, 0:DM], zt[:, m % 2, x], e3[:, x], start=False, stop=(x == E - 1))
                        mm.then_inc(e3_mm, 1)

                    pe.wait_ge(ew_in, EW_IN)
                    hidden(0)
                    pe.wait_ge(pool_c, 5)
                    for x in range(E):
                        mm = pe.matmul(psum[0:E, 6, 0:DM], selb_e[:, x], e3[:, x], start=(x == 0), stop=(x == E - 1))
                    mm.then_inc(eb3_mm, 1)
                    pe.wait_ge(gate_step, GATE_STEPS)
                    for m in range(MT):
                        mm = pe.transpose(psum[0:E, 7, m * P:(m + 1) * P], hot[:, m], ident2[:])
                    mm.then_inc(hot_mm, 1)
                    hidden(1)
                    pe.wait_ge(hot_ev, 1)
                    for m in range(MT):
                        if m + 2 < MT:
                            hidden(m + 2)
                        out_of(m)

                @block.scalar
                def _(act):
                    def affine(m):
                        act.wait_ge(hot_rs, 4 * m + 4)
                        for x in range(E):
                            ins = nc.scalar.activation(a1[:, m, x], a1[:, m, x], ACT.Identity,
                                                       bias=ebs[:, m, x:x + 1], scale=ers[:, m, x:x + 1])
                        ins.then_inc(zn_done, 1)

                    act.wait_ge(xmt_mm, MT)
                    for k in range(DC):
                        nc.scalar.activation(xmt[:, k].rearrange("p m t -> p (m t)"), psum[:, k, :], ACT.Copy).then_inc(xmt_ev, 1)
                    act.wait_ge(gate_step, 1)
                    nc.scalar.activation(sc[:], sc[:], ACT.Exp, scale=-1.0).then_inc(gate_act, 1)
                    act.wait_ge(gate_step, GATE_STEPS - 3)
                    nc.scalar.activation(wts[:], two[:], ACT.Exp).then_inc(gate_act, 1)
                    act.wait_ge(hot_mm, 1)
                    nc.scalar.activation(hot_t[:].rearrange("p m t -> p (m t)"), psum[0:E, 7, :], ACT.Copy).then_inc(hot_ev, 1)
                    for m in range(MT):
                        act.wait_ge(a_done, 2 * m + 1)
                        nc.scalar.activation(at[:, m], a1[:, m], ACT.Tanh, scale=0.5).then_inc(at_done, 1)
                        if m >= 1:
                            affine(m - 1)
                            zt_copy(act, m - 1)
                    affine(MT - 1)
                    zt_copy(act, MT - 1)

                @block.vector
                def _(dve):
                    dve.wait_ge(gathered, 16 * 2 * MT)
                    for m in range(MT):
                        ins = nc.vector.bn_stats(mst[:, m], hg[:, m])
                    ins.then_inc(lnm, 1)
                    dve.wait_ge(lnm, 1)
                    for m in range(MT):
                        ins = nc.vector.bn_aggr(mmv[:, m], mst[:, m])
                    ins.then_inc(lnm, 1)
                    dve.wait_ge(lnm, 2)
                    nc.vector.tensor_scalar(mve[:], mmv[:, :, 1], EPS, None, ALU.add).then_inc(lnm, 1)
                    dve.wait_ge(lnm_pow, 1)
                    for m in range(MT):
                        nc.vector.tensor_scalar(xm[:, m], hg[:, m], mmv[:, m, 0:1], mrs[:, m:m + 1],
                                                ALU.subtract, ALU.mult).then_inc(lnm, 1)

                    gates = [0]

                    def gate(ins):
                        gates[0] += 1
                        ins.then_inc(gate_step, 1)
                        dve.wait_ge(gate_step, gates[0])

                    dve.wait_ge(gate_mm, 1)
                    dve.wait_ge(gw_in, GW_IN)
                    gate(nc.vector.tensor_tensor(sc[:], psum[:, 7, 0:MT * (1 + E)].rearrange("p (m e) -> p m e", m=MT),
                                                 gb[:].unsqueeze(1).to_broadcast([P, MT, 1 + E]), ALU.add))
                    dve.wait_ge(gate_act, 1)
                    gate(nc.vector.tensor_scalar(sc[:], sc[:], 1.0, None, ALU.add))
                    gate(nc.vector.reciprocal(sc[:], sc[:]))
                    gate(nc.vector.tensor_tensor(biased[:], sc[:, :, 1:], xb[:].unsqueeze(1).to_broadcast([P, MT, E]), ALU.add))
                    gate(nc.vector.tensor_reduce(best[:], biased[:], AX.X, ALU.max))
                    gate(nc.vector.tensor_tensor(hot[:], biased[:], best[:].unsqueeze(2).to_broadcast([P, MT, E]), ALU.is_equal))
                    dve.wait_ge(pool_c, 3)
                    gate(nc.vector.tensor_tensor(hot[:], hot[:], prio[:].unsqueeze(1).to_broadcast([P, MT, E]), ALU.mult))
                    gate(nc.vector.tensor_reduce(best[:], hot[:], AX.X, ALU.max))
                    gate(nc.vector.tensor_tensor(hot[:], hot[:], best[:].unsqueeze(2).to_broadcast([P, MT, E]), ALU.is_equal))
                    gate(nc.vector.tensor_tensor(biased[:], hot[:], sc[:, :, 1:], ALU.mult))
                    gate(nc.vector.tensor_reduce(two[:, :, 1:2], biased[:], AX.X, ALU.add))
                    gate(nc.vector.tensor_copy(two[:, :, 0:1], sc[:, :, 0:1]))
                    gate(nc.vector.tensor_reduce(best[:], two[:], AX.X, ALU.max))
                    gate(nc.vector.tensor_tensor(two[:], two[:], best[:].unsqueeze(2).to_broadcast([P, MT, 2]), ALU.subtract))
                    dve.wait_ge(gate_act, 2)
                    gate(nc.vector.tensor_reduce(best[:], wts[:], AX.X, ALU.add))
                    gate(nc.vector.reciprocal(best[:], best[:]))
                    gate(nc.vector.tensor_tensor(wts[:], wts[:], best[:].unsqueeze(2).to_broadcast([P, MT, 2]), ALU.mult))
                    assert gates[0] == GATE_STEPS

                    dve.wait_ge(ew_in, EW_IN)

                    def bias_in(m):
                        for j, (a, b) in enumerate(((a1, eb1b), (a2, eb2b))):
                            dve.wait_ge(h12_mm, 2 * m + j + 1)
                            nc.vector.tensor_tensor(a[:, m].rearrange("p (c e) h -> p c (e h)", c=2),
                                                    psum[:, 2 * j:2 * j + 2, :],
                                                    b[:].rearrange("p (c n) -> p c n", c=2), ALU.add).then_inc(a_done, 1)

                    def gated(m):
                        dve.wait_ge(at_done, m + 1)
                        dve.wait_ge(a_done, 2 * m + 2)
                        nc.vector.scalar_tensor_tensor(out=a1[:, m], in0=at[:, m], scalar=1.0, in1=a1[:, m],
                                                       op0=ALU.add, op1=ALU.mult).then_inc(gated_1, 1)
                        dve.wait_ge(gated_1, m + 1)
                        nc.vector.scalar_tensor_tensor(out=a1[:, m], in0=a1[:, m], scalar=0.5, in1=a2[:, m],
                                                       op0=ALU.mult, op1=ALU.mult).then_inc(ev_done, 1)

                    def stats(m):
                        dve.wait_ge(ev_done, m + 1)
                        for x in range(E):
                            ins = nc.vector.bn_stats(est[:, m, x], a1[:, m, x])
                        ins.then_inc(est_step, 1)
                        dve.wait_ge(est_step, 3 * m + 1)
                        for x in range(E):
                            ins = nc.vector.bn_aggr(emv[:, m, x], est[:, m, x])
                        ins.then_inc(est_step, 1)
                        dve.wait_ge(est_step, 3 * m + 2)
                        nc.vector.tensor_scalar(eve[:, m], emv[:, m, :, 1], EPS, None, ALU.add).then_inc(est_step, 1)

                    def combine(m):
                        nc.vector.scalar_tensor_tensor(out=og[:, m], in0=og[:, m], scalar=wts[:, m, 0:1], in1=hg[:, m],
                                                       op0=ALU.mult, op1=ALU.add).then_inc(part_done, 1)
                        dve.wait_ge(part_done, m + 1)
                        dve.wait_ge(e3_mm, m + 1)
                        nc.vector.scalar_tensor_tensor(out=res[:, m], in0=psum[:, 6, 0:DM], scalar=wts[:, m, 1:2], in1=og[:, m],
                                                       op0=ALU.mult, op1=ALU.add).then_inc(res_done, 1)

                    bias_in(0)
                    dve.wait_ge(eb3_mm, 1)
                    nc.vector.tensor_tensor(eb3x[:], psum[0:E, 6, 0:DM], eb3r[:], ALU.add).then_inc(eb3_done, 1)
                    gated(0)
                    stats(0)
                    dve.wait_ge(shared_done, 1)
                    for m in range(1, MT):
                        bias_in(m)
                        gated(m)
                        stats(m)
                        if m >= 2:
                            combine(m - 2)
                    combine(MT - 2)
                    combine(MT - 1)

                @block.gpsimd
                def _(pool):
                    for m in range(MT):
                        for dst, table in ((hg, h2_scratch), (og, out_rows)):
                            nc.gpsimd.indirect_dma_start(out=dst[:, m], out_offset=None, in_=table,
                                                         in_offset=bass.IndirectOffsetOnAxis(ap=row_i[:, m:m + 1], axis=0)
                                                         ).then_inc(gathered, 16)
                    nc.gpsimd.memset(ident2[:], 0.0).then_inc(pool_c, 1)
                    pool.wait_ge(pool_c, 1)
                    nc.gpsimd.affine_select(out=ident2[:], in_=ident2[:], compare_op=ALU.not_equal, fill=1.0, base=0,
                                            pattern=[[-1, P]], channel_multiplier=1)
                    nc.gpsimd.memset(half_neg[:], -0.5)
                    nc.gpsimd.iota(prio_i[:], [[-1, E]], base=E, channel_multiplier=0).then_inc(pool_c, 1)
                    pool.wait_ge(pool_c, 2)
                    nc.gpsimd.tensor_copy(prio[:], prio_i[:]).then_inc(pool_c, 1)
                    pool.wait_ge(gw_in, GW_IN)
                    nc.gpsimd.memset(selb_e[:], 0.0).then_inc(pool_c, 1)
                    pool.wait_ge(pool_c, 4)
                    nc.gpsimd.tensor_copy(selb_e[:].rearrange("p a b -> p (a b)")[:, 0:E * E:E + 1],
                                          selb[:].to_broadcast([P, E])).then_inc(pool_c, 1)
                    pool.wait_ge(lnm, 3)
                    nc.gpsimd.tensor_tensor(mrs[:], mve[:], half_neg[:, :, 0], ALU.pow).then_inc(lnm_pow, 1)
                    nc.gpsimd.tensor_tensor(og[:], og[:], hg[:], ALU.subtract).then_inc(shared_done, 1)

                    def rstd_of(m):
                        pool.wait_ge(est_step, 3 * m + 3)
                        nc.gpsimd.tensor_tensor(ers[:, m], eve[:, m], half_neg[:, 0], ALU.pow).then_inc(hot_rs, 1)
                        pool.wait_ge(hot_rs, 4 * m + 1)
                        pool.wait_ge(gate_step, GATE_STEPS)
                        nc.gpsimd.tensor_tensor(ers[:, m], ers[:, m], hot[:, m], ALU.mult).then_inc(hot_rs, 1)
                        pool.wait_ge(hot_rs, 4 * m + 2)
                        nc.gpsimd.tensor_tensor(ebs[:, m], ers[:, m], emv[:, m, :, 0], ALU.mult).then_inc(hot_rs, 1)
                        pool.wait_ge(hot_rs, 4 * m + 3)
                        nc.gpsimd.tensor_scalar(ebs[:, m], ebs[:, m], -1.0, None, ALU.mult).then_inc(hot_rs, 1)

                    def scatter(m):
                        pool.wait_ge(res_done, m + 1)
                        nc.gpsimd.indirect_dma_start(out=out_rows, out_offset=bass.IndirectOffsetOnAxis(ap=to_i[:, m:m + 1], axis=0),
                                                     in_=res[:, m], in_offset=None, bounds_check=ROWS - 1,
                                                     oob_is_err=False).then_inc(scattered, 16)

                    for m in range(MT):
                        rstd_of(m)
                        if m >= 2:
                            scatter(m - 2)
                    scatter(MT - 2)
                    scatter(MT - 1)
                    pool.wait_ge(scattered, 16 * MT)


def kernel(**inputs):
    import numpy as np
    import concourse.bacc as bacc
    from concourse.bass_utils import run_bass_kernel_spmd

    a = {k.replace("L0_", ""): np.asarray(v) for k, v in inputs.items()}

    def chunks(w):
        w = w.reshape(w.shape[0], -1)
        return w.reshape(-1, P, w.shape[1]).transpose(1, 0, 2)

    B, C, HW, _ = a["x"].shape
    PATCH, SEQ = 16, 2
    S = HW // PATCH
    G = B // SEQ
    DM = a["tok_W"].shape[0]
    R = a["attn_W_dt"].shape[0]
    E, H, _ = a["ffn_ew1"].shape
    M = a["ffn_index_b"].shape[0]
    x = a["x"].reshape(G, SEQ, C, S, PATCH, S, PATCH).transpose(2, 4, 6, 0, 1, 3, 5)
    x = x.reshape(-1, P, G, SEQ * S * S).transpose(2, 1, 0, 3)
    txt = a["txt"].reshape(G, SEQ, -1, DM // P, P).transpose(0, 4, 3, 1, 2)
    w_x = a["attn_W_x"]
    NS = a["attn_A_log"].shape[1]
    a_log = a["attn_A_log"].reshape(-1, 2, P // 2, 2, NS // 2).transpose(3, 2, 0, 1, 4).reshape(P, -1, 2, NS // 2)
    feed = {
        "x_patches": x, "txt_t": txt, "tok_w": chunks(a["tok_W"].T), "tok_b": a["tok_b"].reshape(-1, P).T,
        "cls_t": a["tok_cls_token"].reshape(-1, P).T, "pos_t": chunks(a["tok_pos_enc"][0].T),
        "w_in": chunks(a["attn_W_in"]), "conv_w": chunks(a["attn_conv_w"]), "conv_b": a["attn_conv_b"].reshape(-1, P).T,
        "w_x": chunks(np.concatenate([w_x[:, R:], w_x[:, :R]], axis=1)), "w_dt": a["attn_W_dt"],
        "b_dt": a["attn_b_dt"][None], "a_log": a_log, "d_skip": a["attn_D"].reshape(-1, P).T,
        "w_out": chunks(a["attn_W_out"]), "index_b": a["ffn_index_b"].reshape(M // P, P).T,
        "index_t": a["ffn_index_t"].reshape(M // P, P).T, "sw1": chunks(a["ffn_sw1"].T), "sb1": a["ffn_sb1"],
        "sw2": chunks(a["ffn_sw2"].T), "sb2": a["ffn_sb2"], "sw3": a["ffn_sw3"].T, "sb3": a["ffn_sb3"],
        "s_ln_g": a["ffn_s_ln_g"][:, None], "s_ln_b": a["ffn_s_ln_b"][:, None], "gate_w": chunks(np.concatenate([a["ffn_sg_w"], a["ffn_eg_w"]]).T),
        "sg_b": a["ffn_sg_b"], "eg_b": a["ffn_eg_b"], "exp_bias": a["ffn_exp_bias"],
        "ew1": chunks(a["ffn_ew1"].reshape(E * H, DM).T), "eb1": a["ffn_eb1"].reshape(-1),
        "ew2": chunks(a["ffn_ew2"].reshape(E * H, DM).T), "eb2": a["ffn_eb2"].reshape(-1),
        "ew3": a["ffn_ew3"].transpose(2, 0, 1), "eb3": a["ffn_eb3"],
        "sel_ln_g": a["ffn_sel_ln_g"][:, None], "sel_ln_b": a["ffn_sel_ln_b"][:, None],
    }
    feed = {k: np.ascontiguousarray(v) for k, v in feed.items()}
    nc = bacc.Bacc("TRN2", target_bir_lowering=False, num_devices=1)
    args = {k: nc.dram_tensor(k, v.shape, mybir.dt.from_np(v.dtype), kind="ExternalInput").ap() for k, v in feed.items()}
    T = 1 + S * S + a["txt"].shape[1]
    out = nc.dram_tensor("out", (B, T, DM), F32, kind="ExternalOutput").ap()
    fusion_kernel(nc, out=out, **args)
    r = run_bass_kernel_spmd(nc, [feed], core_ids=[0])
    return r.results[0]["out"]
```
